# Optimizing a Trainium2 kernel written in Bass

```python
import numpy as np
import jax
import jax.numpy as jnp

def _softmax(x, axis=-1):
    return jax.nn.softmax(x, axis=axis)

def _gelu(x):
    return jax.nn.gelu(x, approximate=True)

def _silu(x):
    return jax.nn.silu(x)

def _sigmoid(x):
    return jax.nn.sigmoid(x)

def _layernorm(x, axis=-1, eps=1e-05):
    m = jnp.mean(x, axis=axis, keepdims=True)
    v = jnp.var(x, axis=axis, keepdims=True)
    return (x - m) / jnp.sqrt(v + eps)

def _scatter_add(tgt, idx, src, axis=0):
    return tgt.at[idx].add(src)

def _segment_sum(src, seg, n):
    return jax.ops.segment_sum(src, seg, n)
kernel_name = 'mk_gnn_resnorm_d2_gnn_r8_a5f576'

def setup_inputs(seed: int=0):
    np.random.seed(seed)
    _w = jnp.asarray

    def _rec_inputs():
        import jax
        import jax.numpy as jnp
        _gk = jax.random.key(seed)
        x = -0.0003713 + 1 * jax.random.normal(jax.random.fold_in(_gk, 1), (12500, 256), jnp.float32)
        src = jax.random.randint(jax.random.fold_in(_gk, 2), (200000,), 0, 12500, jnp.int32)
        dst = jnp.minimum((12500 * jax.random.uniform(jax.random.fold_in(_gk, 3), (200000,)) ** 2.0).astype(jnp.int32), 99999)
        _o = jnp.argsort(dst, stable=True)
        src = src[_o]
        dst = dst[_o]
        return (x, src, dst)
    x, src, dst = _rec_inputs()

    def _L0_gnn_setup():
        import jax, jax.numpy as jnp
        import numpy as np
        N_NODES = 6250
        IN_DIM = 256
        OUT_DIM = 128
        NUM_HEADS = 2
        N_EDGES = 100000

        def _gat_forward(x, edge_index, W_w, W_b, a):
            N = x.shape[0]
            H, D = (NUM_HEADS, OUT_DIM)
            Wh = (x @ W_w + W_b).reshape(N, H, D)
            src, dst = (edge_index[0], edge_index[1])
            a_src, a_dst = (a[:D], a[D:])
            s = jnp.einsum('nhd,d->nh', Wh, a_src)
            t = jnp.einsum('nhd,d->nh', Wh, a_dst)
            e = jax.nn.leaky_relu(s[src] + t[dst], negative_slope=0.2)
            m = jax.ops.segment_max(e, src, num_segments=N)
            ex = jnp.exp(e - m[src])
            denom = jax.ops.segment_sum(ex, src, num_segments=N)
            alpha = ex / denom[src]
            agg = jax.ops.segment_sum(alpha[:, :, None] * Wh[dst], src, num_segments=N)
            deg = jax.ops.segment_sum(jnp.ones_like(src, dtype=Wh.dtype), src, num_segments=N)
            h_prime = jnp.where(deg[:, None, None] > 0, agg, Wh)
            return h_prime.reshape(N, H * D)
        key = jax.random.key(seed)
        k1, k2, k3, k4, k5 = jax.random.split(key, 5)
        x = jax.random.normal(k1, (N_NODES, IN_DIM), dtype=jnp.float32)
        edge_index = jax.random.randint(k2, (2, N_EDGES), 0, N_NODES, dtype=jnp.int64)
        fan = IN_DIM + OUT_DIM * NUM_HEADS
        W_w = jax.random.uniform(k3, (IN_DIM, OUT_DIM * NUM_HEADS), dtype=jnp.float32, minval=-np.sqrt(6.0 / fan), maxval=np.sqrt(6.0 / fan))
        W_b = jnp.zeros((OUT_DIM * NUM_HEADS,), dtype=jnp.float32)
        fa = 1 + 2 * OUT_DIM
        a = jax.random.uniform(k4, (2 * OUT_DIM,), dtype=jnp.float32, minval=-np.sqrt(6.0 / fa), maxval=np.sqrt(6.0 / fa))
        return {'x': x, 'edge_index': edge_index, 'W_w': W_w, 'W_b': W_b, 'a': a}
    _L0_gnn_all = _L0_gnn_setup()
    _L0_gnn_in = {k: v for k, v in _L0_gnn_all.items() if k in ('W_w', 'W_b', 'a')}
    del _L0_gnn_all

    def _L1_gnn_setup():
        import jax, jax.numpy as jnp
        import numpy as np
        N_NODES = 12500
        N_EDGES = 400000
        D_IN = 256
        D_HID = 256
        D_OUT = 256

        def _sage_conv(x, src, tgt, W_l, b_l, W_r):
            n = x.shape[0]
            msgs = x[src]
            agg = jax.ops.segment_sum(msgs, tgt, num_segments=n)
            deg = jax.ops.segment_sum(jnp.ones((src.shape[0],), x.dtype), tgt, num_segments=n)
            agg = agg / jnp.maximum(deg, 1.0)[:, None]
            return agg @ W_l + b_l + x @ W_r
        key = jax.random.key(seed)
        ks = jax.random.split(key, 8)
        x = jax.random.normal(ks[0], (N_NODES, D_IN), dtype=jnp.float32)
        edge_index = jax.random.randint(ks[1], (2, N_EDGES), 0, N_NODES, dtype=jnp.int64)
        s1 = 1.0 / np.sqrt(D_IN)
        s2 = 1.0 / np.sqrt(D_HID)
        return {'x': x, 'edge_index': edge_index, 'W_l1': jax.random.uniform(ks[2], (D_IN, D_HID), jnp.float32, -s1, s1), 'b1': jnp.zeros((D_HID,), jnp.float32), 'W_r1': jax.random.uniform(ks[3], (D_IN, D_HID), jnp.float32, -s1, s1), 'W_l2': jax.random.uniform(ks[4], (D_HID, D_OUT), jnp.float32, -s2, s2), 'b2': jnp.zeros((D_OUT,), jnp.float32), 'W_r2': jax.random.uniform(ks[5], (D_HID, D_OUT), jnp.float32, -s2, s2)}
    _L1_gnn_all = _L1_gnn_setup()
    _L1_gnn_in = {k: v for k, v in _L1_gnn_all.items() if k in ('W_l1', 'b1', 'W_r1', 'W_l2', 'b2', 'W_r2')}
    del _L1_gnn_all
    return {'x': x, 'src': src, 'dst': dst, 'L0_gnn_W_w': _L0_gnn_in['W_w'], 'L0_gnn_W_b': _L0_gnn_in['W_b'], 'L0_gnn_a': _L0_gnn_in['a'], 'L1_gnn_W_l1': _L1_gnn_in['W_l1'], 'L1_gnn_b1': _L1_gnn_in['b1'], 'L1_gnn_W_r1': _L1_gnn_in['W_r1'], 'L1_gnn_W_l2': _L1_gnn_in['W_l2'], 'L1_gnn_b2': _L1_gnn_in['b2'], 'L1_gnn_W_r2': _L1_gnn_in['W_r2']}

def reference(x, src, dst, L0_gnn_W_w, L0_gnn_W_b, L0_gnn_a, L1_gnn_W_l1, L1_gnn_b1, L1_gnn_W_r1, L1_gnn_W_l2, L1_gnn_b2, L1_gnn_W_r2):
    import jax
    import jax.numpy as jnp

    def _L0_gnn_ref(x, edge_index, W_w, W_b, a):
        import jax, jax.numpy as jnp
        import numpy as np
        N_NODES = 6250
        IN_DIM = 256
        OUT_DIM = 128
        NUM_HEADS = 2
        N_EDGES = 100000

        def _gat_forward(x, edge_index, W_w, W_b, a):
            N = x.shape[0]
            H, D = (NUM_HEADS, OUT_DIM)
            Wh = (x @ W_w + W_b).reshape(N, H, D)
            src, dst = (edge_index[0], edge_index[1])
            a_src, a_dst = (a[:D], a[D:])
            s = jnp.einsum('nhd,d->nh', Wh, a_src)
            t = jnp.einsum('nhd,d->nh', Wh, a_dst)
            e = jax.nn.leaky_relu(s[src] + t[dst], negative_slope=0.2)
            m = jax.ops.segment_max(e, src, num_segments=N)
            ex = jnp.exp(e - m[src])
            denom = jax.ops.segment_sum(ex, src, num_segments=N)
            alpha = ex / denom[src]
            agg = jax.ops.segment_sum(alpha[:, :, None] * Wh[dst], src, num_segments=N)
            deg = jax.ops.segment_sum(jnp.ones_like(src, dtype=Wh.dtype), src, num_segments=N)
            h_prime = jnp.where(deg[:, None, None] > 0, agg, Wh)
            return h_prime.reshape(N, H * D)
        return _gat_forward(x, edge_index, W_w, W_b, a)

    def _L1_gnn_ref(x, edge_index, W_l1, b1, W_r1, W_l2, b2, W_r2):
        import jax, jax.numpy as jnp
        import numpy as np
        N_NODES = 12500
        N_EDGES = 400000
        D_IN = 256
        D_HID = 256
        D_OUT = 256

        def _sage_conv(x, src, tgt, W_l, b_l, W_r):
            n = x.shape[0]
            msgs = x[src]
            agg = jax.ops.segment_sum(msgs, tgt, num_segments=n)
            deg = jax.ops.segment_sum(jnp.ones((src.shape[0],), x.dtype), tgt, num_segments=n)
            agg = agg / jnp.maximum(deg, 1.0)[:, None]
            return agg @ W_l + b_l + x @ W_r
        src, tgt = (edge_index[0], edge_index[1])
        h = jax.nn.relu(_sage_conv(x, src, tgt, W_l1, b1, W_r1))
        logits = _sage_conv(h, src, tgt, W_l2, b2, W_r2)
        return logits
    edge_index = jnp.stack([src, dst])
    x = _layernorm(x + _L0_gnn_ref(x, edge_index, L0_gnn_W_w, L0_gnn_W_b, L0_gnn_a), axis=-1)
    x = _layernorm(x + _L1_gnn_ref(x, edge_index, L1_gnn_W_l1, L1_gnn_b1, L1_gnn_W_r1, L1_gnn_W_l2, L1_gnn_b2, L1_gnn_W_r2), axis=-1)
    return x

_drawn_inputs = setup_inputs


def setup_inputs(seed=0):
    import zlib

    import numpy as np

    out = dict(_drawn_inputs(seed))
    spreads = {'L0_gnn_W_b': (0.0, 0.1), 'L1_gnn_b1': (0.0, 0.1), 'L1_gnn_b2': (0.0, 0.1)}
    factors = {}
    for name, (base, spread) in spreads.items():
        noise = np.random.default_rng([zlib.crc32(name.encode()), seed]).standard_normal(out[name].shape)
        drawn = base * np.exp(spread * noise) if base else spread * noise
        out[name] = jnp.asarray(drawn.astype(out[name].dtype))
    for name, factor in factors.items():
        out[name] = (out[name] * factor).astype(out[name].dtype)
    return out
```

```python
from contextlib import ExitStack

import concourse.bass as bass
from concourse import mybir

F32 = mybir.dt.float32
BF16 = mybir.dt.bfloat16
I32 = mybir.dt.int32
ALU = mybir.AluOpType
ACT = mybir.ActivationFunctionType
X = mybir.AxisListType.X
ds = bass.ds

P = 128
N = 12500
D = 256
HEADS = 2
HD = D // HEADS
E = 200000
NB = -(-N // P)
LAST = N - (NB - 1) * P
EP = 125
EC = E // EP
LISTS = 2
GROUP = 4
RING = 8
BODY = GROUP * RING
CHUNKS = -(-((E + NB * (P - 1)) // P) // BODY) * BODY
GROUPS = CHUNKS // GROUP
TURNS = GROUPS // RING
SHIFT = 7
LOC = 256
PAD = N * LOC + 200
FAR = -1.0e30
ROWT = D + HEADS
ACC = HEADS * (HD + 1)
EPS = 1e-5
SLOPE = 0.2


def wait(eng, sem, value):
    if isinstance(value, int) and value <= 0:
        return
    eng.wait_ge(sem, value)


def per_head(ap):
    return ap.rearrange("p (h d) -> p h d", h=HEADS)


class Kernel:
    pass


def constants(nc, k, ctx):
    sb = k.sb
    k.ramp = sb("ramp", [P, P], F32)
    k.place = sb("place", [P, 1], F32)
    k.ident = sb("ident", [P, P], F32)
    k.ones = sb("ones", [P, P], F32)
    with ExitStack() as c:
        ramp_i = c.enter_context(nc.sbuf_tensor("ramp_i", [P, P], I32))
        place_i = c.enter_context(nc.sbuf_tensor("place_i", [P, 1], I32))
        iotas = c.enter_context(nc.semaphore("iotas"))
        ramps = c.enter_context(nc.semaphore("ramps"))
        block = c.enter_context(nc.Block())

        @block.gpsimd
        def _(pool):
            pool.iota(ramp_i[:, :], pattern=[[1, P]], base=0, channel_multiplier=0).then_inc(iotas, 1)
            pool.iota(place_i[:, :], pattern=[[1, 1]], base=0, channel_multiplier=1).then_inc(iotas, 1)

        @block.vector
        def _(dve):
            dve.memset(k.ones[:, :], 1.0)
            dve.wait_ge(iotas, 2)
            dve.tensor_copy(k.ramp[:, :], ramp_i[:, :]).then_inc(ramps, 1)
            dve.tensor_copy(k.place[:, :], place_i[:, :]).then_inc(ramps, 1)
            dve.wait_ge(ramps, 2)
            dve.tensor_scalar(k.ident[:, :], k.ramp[:, :], k.place[:, 0:1], None, ALU.is_equal)


def sort_edges(nc, k, src, dst):
    HALF = 8
    AHEAD = HALF - 1
    TURN = 2 * HALF
    assert EC % TURN == 0
    COLS = EC + HALF
    PIECES = 4
    PIECE = CHUNKS // PIECES
    sb = k.sb
    k.block_row = [sb(f"block_row{q}", [1, CHUNKS], I32) for q in range(LISTS)]
    with ExitStack() as c:
        def tmp(name, shape, dt):
            return c.enter_context(nc.sbuf_tensor(name, shape, dt))

        def sem(name):
            return c.enter_context(nc.semaphore(name))

        ends = tmp("ends", [EP, LISTS, EC], I32)
        key_block = tmp("key_block", [EP, LISTS, COLS], F32)
        entry = tmp("entry", [EP, LISTS, EC], I32)
        work_i = tmp("work_i", [EP, EC], I32)
        work_f = tmp("work_f", [EP, EC], F32)
        hits = tmp("hits", [EP, 2, EC], BF16)
        count = tmp("count", [EP, LISTS, NB], F32)
        pads = tmp("pads", [P, CHUNKS], I32)
        before = tmp("before", [EP, EP], BF16)
        after = tmp("after", [EP, EP], BF16)
        before_f = tmp("before_f", [P, P], F32)
        chunks_i = tmp("chunks_i", [NB, LISTS], I32)
        chunks_j = tmp("chunks_j", [NB, LISTS], I32)
        chunks_f = tmp("chunks_f", [NB, LISTS], F32)
        start = tmp("start", [NB, LISTS], F32)
        base = tmp("base", [NB, LISTS, EP], F32)
        chunk_no = tmp("chunk_no", [NB, CHUNKS], I32)
        begun = tmp("begun", [NB, LISTS, CHUNKS], BF16)
        ones_b = tmp("ones_b", [NB, P], BF16)
        block_f = tmp("block_f", [P, LISTS, CHUNKS], F32)
        same = tmp("same", [P, CHUNKS], F32)
        onehot = tmp("onehot", [EP, LISTS, HALF, NB], BF16)
        ranked = tmp("ranked", [EP, LISTS, NB], F32)
        spot_f = tmp("spot_f", [EP, 2, LISTS * HALF], F32)
        spot_i = tmp("spot_i", [EP, 2, LISTS * HALF], I32)
        spot_p = tmp("spot_p", [EP, 2, LISTS * HALF], I32)
        spot_c = tmp("spot_c", [EP, 2, LISTS * HALF], I32)
        address = tmp("address", [EP, 2, LISTS * HALF], I32)
        moved = tmp("moved", [EP, 2, LISTS * HALF], I32)

        loaded = sem("loaded")
        pads_set = sem("pads_set")
        pads_in = sem("pads_in")
        numbers = sem("numbers")
        step = sem("step")
        counted = sem("counted")
        counts_sum = sem("counts_sum")
        chunks_known = sem("chunks_known")
        starts_sum = sem("starts_sum")
        base_set = sem("base_set")
        blocks_sum = sem("blocks_sum")
        hot = [sem(f"hot{q}") for q in range(LISTS)]
        place_known = [sem(f"place_known{q}") for q in range(LISTS)]
        rank_sum = [sem(f"rank_sum{q}") for q in range(LISTS)]
        spots = sem("spots")
        placed = sem("placed")
        scattered = [sem(f"scattered{h}") for h in range(2)]

        def ps(name, shape):
            return c.enter_context(nc.psum_tensor(name, shape, F32))

        sums = ps("sums", [NB, 2 * LISTS])
        running = [ps(f"running{q}", [EP, NB]) for q in range(LISTS)]
        block_sum = ps("block_sum", [P, PIECES, 512])
        block = c.enter_context(nc.Block())

        @block.sync
        def _(sp):
            for q, e in enumerate((src, dst)):
                sp.dma_start(ends[:, q, :], e.rearrange("(p c) -> p c", p=EP)).then_inc(loaded, 16)
            sp.wait_ge(pads_set, 1)
            for q in range(LISTS):
                sp.dma_start(k.edges[q], pads[:, :]).then_inc(pads_in, 16)

        @block.gpsimd
        def _(pool):
            pool.iota(chunk_no[:, :], pattern=[[1, CHUNKS]], base=0, channel_multiplier=0).then_inc(numbers, 1)
            bound = pool.to_reg(P * CHUNKS - 1)
            due = pool.alloc_register("due")
            pool.reg_mov(due, 1)
            pool.wait_ge(pads_in, 16 * LISTS)
            with pool.Fori(0, EC // TURN):
                for h in range(2):
                    pool.wait_ge(spots, due)
                    pool.reg_add(due, due, 1)
                    for q in range(LISTS):
                        flat = k.edges[q].rearrange("p (c o) -> (p c) o", o=1)
                        for j in range(HALF):
                            at = q * HALF + j
                            pool.indirect_dma_start(
                                out=flat, out_offset=bass.IndirectOffsetOnAxis(ap=address[:, h, at:at + 1], axis=0),
                                in_=moved[:, h, at:at + 1], in_offset=None,
                                bounds_check=bound, oob_is_err=False).then_inc(scattered[h], 16)
            for h in range(2):
                pool.wait_ge(scattered[h], 16 * LISTS * HALF * (EC // TURN))

        @block.tensor
        def _(pe):
            pe.wait_ge(counted, LISTS)
            for q in range(LISTS):
                last = pe.matmul(sums[:, q:q + 1], count[:, q, :], k.ones[0:EP, 0:1], start=True, stop=True)
            last.then_inc(counts_sum, 1)
            pe.wait_ge(chunks_known, 1)
            pe.matmul(sums[:, LISTS:2 * LISTS], before_f[0:NB, 0:NB], chunks_f[:, :],
                      start=True, stop=True).then_inc(starts_sum, 1)
            pe.wait_ge(base_set, 1)
            for q in range(LISTS):
                for j in range(PIECES):
                    pe.matmul(block_sum[:, j, 0:PIECE], ones_b[:, :], begun[:, q, j * PIECE:(j + 1) * PIECE],
                              start=True, stop=True).then_inc(blocks_sum, 1)
                if q + 1 < LISTS:
                    pe.wait_ge(chunks_known, 2)
            for q in range(LISTS):
                pe.matmul(running[q][:, :], base[:, q, :], k.ident[0:NB, 0:NB], start=True, stop=True)

            def column(g, j):
                for q in range(LISTS):
                    if j != 0 or not isinstance(g, int):
                        wait(pe, place_known[q], g + j)
                        pe.matmul(running[q][:, :], after[:, :], onehot[:, q, (j - 1) % HALF, :],
                                  start=False, stop=True, skip_group_check=True)
                    pe.wait_ge(hot[q], g + j + 1)
                    pe.matmul(running[q][:, :], before[:, :], onehot[:, q, j % HALF, :],
                              start=False, stop=True, skip_group_check=True).then_inc(rank_sum[q], 1)

            for j in range(TURN):
                column(0, j)
            with pe.Fori(1, EC // TURN) as i:
                for j in range(TURN):
                    column(i * TURN, j)

        @block.vector
        def _(dve):
            done = [0]

            def after_all(ins):
                ins.then_inc(step, 1)
                done[0] += 1
                dve.wait_ge(step, done[0])

            dve.memset(pads[:, :], PAD).then_inc(pads_set, 1)
            dve.memset(ones_b[:, :], 1.0)
            dve.memset(key_block[:, :, EC:COLS], 0.0)
            dve.tensor_scalar(before[:, :], k.ramp[0:EP, 0:EP], k.place[0:EP, 0:1], None, ALU.is_gt)
            dve.tensor_scalar(after[:, :], k.ramp[0:EP, 0:EP], k.place[0:EP, 0:1], None, ALU.is_le)
            dve.tensor_scalar(before_f[:, :], k.ramp[:, :], k.place[:, 0:1], None, ALU.is_gt)
            dve.wait_ge(loaded, 16 * LISTS)
            for q in range(LISTS):
                after_all(dve.tensor_single_scalar(work_i[:, :], ends[:, q, :], SHIFT, ALU.logical_shift_right))
                after_all(dve.tensor_copy(key_block[:, q, 0:EC], work_i[:, :]))
                after_all(dve.tensor_single_scalar(work_i[:, :], ends[:, q, :], P - 1, ALU.bitwise_and))
                after_all(dve.tensor_copy(work_f[:, :], work_i[:, :]))
                after_all(dve.scalar_tensor_tensor(entry[:, q, :], ends[:, 1 - q, :], float(LOC), work_f[:, :],
                                                   ALU.mult, ALU.add))
            for q in range(LISTS):
                for b in range(NB):
                    ins = dve.tensor_scalar(hits[:, b % 2, :], key_block[:, q, 0:EC], float(b), None,
                                            ALU.is_equal, ALU.add, accum_out=count[:, q, b:b + 1])
                    ins.then_inc(step, 1)
                    done[0] += 1
                    if b:
                        dve.wait_ge(step, done[0] - 1)
                dve.nop()
                dve.wait_ge(step, done[0])
                dve.nop().then_inc(counted, 1)
            dve.wait_ge(counts_sum, 1)
            after_all(dve.tensor_scalar(chunks_i[:, :], sums[:, 0:LISTS], float(P - 1), None, ALU.add))
            after_all(dve.tensor_single_scalar(chunks_j[:, :], chunks_i[:, :], SHIFT, ALU.logical_shift_right))
            dve.tensor_copy(chunks_f[:, :], chunks_j[:, :]).then_inc(chunks_known, 1)
            dve.wait_ge(starts_sum, 1)
            after_all(dve.tensor_copy(start[:, :], sums[:, LISTS:2 * LISTS]))
            dve.wait_ge(numbers, 1)
            for q in range(LISTS):
                dve.tensor_scalar(base[:, q, :], k.ones[0:NB, 0:EP], start[:, q:q + 1], float(P), ALU.mult, ALU.mult)
                last = dve.tensor_scalar(begun[:, q, :], chunk_no[:, :], start[:, q:q + 1], None, ALU.is_ge)
            last.then_inc(base_set, 1)
            for q in range(LISTS):
                dve.wait_ge(blocks_sum, PIECES * (q + 1))
                after_all(dve.tensor_scalar(block_f[:, q, :].rearrange("p (a b) -> p a b", a=PIECES),
                                            block_sum[:, :, 0:PIECE], -1.0, None, ALU.add))
                if q == 0:
                    dve.nop().then_inc(chunks_known, 1)
                dve.tensor_copy(k.block_row[q][:, :], block_f[0:1, q, :])
            dve.memset(same[:, 0:1], 0.0)
            after_all(dve.tensor_tensor(same[:, 1:CHUNKS], block_f[:, 0, 1:CHUNKS], block_f[:, 0, 0:CHUNKS - 1],
                                        ALU.is_equal))
            after_all(dve.memset(k.carry[:, :, :, :], 0.0))
            for h in range(HEADS):
                dve.tensor_copy(k.carry[:, :, h, 1:GROUP + 1], same[:, :].rearrange("p (g c) -> p g c", c=GROUP))
            dve.tensor_scalar(k.fresh[:, :], same[:, :], 1.0, -FAR, ALU.subtract, ALU.mult)

            def hot_rows(col, j, q):
                dve.tensor_scalar(onehot[:, q, j % HALF, :], k.ramp[0:EP, 0:NB], key_block[:, q, ds(col, 1)], None,
                                  ALU.is_equal).then_inc(hot[q], 1)

            def half(i, h):
                first = isinstance(i, int)
                for j in range(h * HALF, (h + 1) * HALF):
                    col = i * TURN + j
                    for q in range(LISTS):
                        at = q * HALF + j % HALF
                        dve.wait_ge(rank_sum[q], col + 1)
                        wait(dve, place_known[q], col)
                        dve.scalar_tensor_tensor(ranked[:, q, :], k.ramp[0:EP, 0:NB], key_block[:, q, ds(col, 1)],
                                                 running[q][:, :], ALU.is_equal, ALU.mult,
                                                 accum_out=spot_f[:, h, at:at + 1]).then_inc(place_known[q], 1)
                        hot_rows(col + AHEAD, j + AHEAD, q)
                for q in range(LISTS):
                    dve.wait_ge(place_known[q], i * TURN + (h + 1) * HALF)
                n = 2 * i + h
                dve.tensor_copy(spot_i[:, h, :], spot_f[:, h, :]).then_inc(placed, 1)
                dve.wait_ge(placed, 3 * n + 1)
                dve.tensor_single_scalar(spot_p[:, h, :], spot_i[:, h, :], P - 1, ALU.bitwise_and)
                dve.tensor_single_scalar(spot_c[:, h, :], spot_i[:, h, :], SHIFT,
                                         ALU.logical_shift_right).then_inc(placed, 1)
                if not first:
                    dve.wait_ge(scattered[h], i * (16 * LISTS * HALF))
                dve.tensor_copy(moved[:, h, :].rearrange("p (q j) -> p q j", q=LISTS),
                                entry[:, :, ds(i * TURN + h * HALF, HALF)])
                dve.wait_ge(placed, 3 * n + 2)
                dve.scalar_tensor_tensor(address[:, h, :], spot_p[:, h, :], float(CHUNKS), spot_c[:, h, :],
                                         ALU.mult, ALU.add).then_inc(placed, 1)
                dve.wait_ge(placed, 3 * n + 3)
                dve.nop().then_inc(spots, 1)

            for q in range(LISTS):
                for j in range(AHEAD):
                    hot_rows(j, j, q)
            half(0, 0)
            half(0, 1)
            with dve.Fori(1, EC // TURN) as i:
                half(i, 0)
                half(i, 1)


def load_list(nc, k, q):
    with ExitStack() as c:
        raw = c.enter_context(nc.sbuf_tensor(f"raw{q}", [P, CHUNKS], I32))
        part = c.enter_context(nc.sbuf_tensor(f"low_bits{q}", [P, CHUNKS], I32))
        read = c.enter_context(nc.semaphore(f"read{q}"))
        cut = c.enter_context(nc.semaphore(f"cut{q}"))
        block = c.enter_context(nc.Block())

        @block.sync
        def _(sp):
            sp.dma_start(raw[:, :], k.edges[q]).then_inc(read, 16)

        @block.vector
        def _(dve):
            dve.wait_ge(read, 16)
            dve.tensor_single_scalar(k.row[:, :], raw[:, :], 8, ALU.logical_shift_right)
            dve.tensor_single_scalar(part[:, :], raw[:, :], LOC - 1, ALU.bitwise_and).then_inc(cut, 1)
            dve.wait_ge(cut, 1)
            dve.tensor_copy(k.spot[:, :], part[:, :])


def project(nc, k, x, Ww, Wb, a):
    W_EXT = D + 2 * HEADS
    RX = 4
    with ExitStack() as c:
        def tmp(name, shape, dt=F32):
            return c.enter_context(nc.sbuf_tensor(name, shape, dt))

        def sem(name):
            return c.enter_context(nc.semaphore(name))

        w = tmp("w", [P, 2, W_EXT])
        bias = tmp("bias", [P, W_EXT])
        a_all = tmp("a_all", [P, 2 * HD])
        junk = tmp("junk", [P, 12, HD])
        xin = tmp("xin", [P, RX, D])
        xT = tmp("xT", [P, 2, 2, P])
        wh = tmp("wh", [P, RX, W_EXT])
        t_all = tmp("t_all", [P, HEADS, NB])
        empty = tmp("empty", [P, ROWT])
        low = tmp("low", [P, HEADS])
        low_n = tmp("low_n", [P, HEADS])
        low_r = tmp("low_r", [P, HEADS])
        w_in = sem("w_in")
        cleared = sem("cleared")
        w_done = sem("w_done")
        x_in = [sem(f"x_in{r}") for r in range(RX)]
        turned = sem("turned")
        copied = sem("copied")
        product = sem("product")
        rows = sem("rows")
        stored = [sem(f"stored{r}") for r in range(RX)]
        empties = sem("empties")
        lows = sem("lows")
        all_low = sem("all_low")
        pT = c.enter_context(nc.psum_tensor("pT", [P, 2, 512], F32))
        pW = c.enter_context(nc.psum_tensor("pW", [P, 2, 512], F32))
        MAIN = NB - 1 - (NB - 1) % RX
        TAIL = range(MAIN, NB)

        def size(b):
            return LAST if isinstance(b, int) and b == NB - 1 else P

        def rows_of(t, b, n):
            return t[ds(b * P, n), :] if not isinstance(b, int) else t[b * P:b * P + n, :]

        def each(eng, f):
            for r in range(RX):
                f(r, r, 0)
            with eng.Fori(1, MAIN // RX) as i:
                for r in range(RX):
                    f(i * RX + r, r, i)
            for b in TAIL:
                f(b, b % RX, b // RX)

        block = c.enter_context(nc.Block())

        @block.sync
        def _(sp):
            sp.dma_start(w[:, :, 0:D], Ww.rearrange("(k p) n -> p k n", p=P)).then_inc(w_in, 16)
            sp.dma_start(bias[:, 0:D], Wb.rearrange("(o n) -> o n", o=1).to_broadcast([P, D])).then_inc(w_in, 16)
            sp.dma_start(a_all[:, :], a.rearrange("(o n) -> o n", o=1).to_broadcast([P, 2 * HD])).then_inc(w_in, 16)

            def load(b, r, i):
                wait(sp, copied, b - RX + 1)
                sp.dma_start(xin[0:size(b), r, :], rows_of(x, b, size(b))).then_inc(x_in[r], 16)

            each(sp, load)

        @block.scalar
        def _(act):
            def copy(b, r, i):
                act.wait_ge(turned, b + 1)
                wait(act, product, b - 1)
                n = size(b)
                act.activation(xT[:, r % 2, :, 0:n], pT[:, r % 2, 0:2 * P].rearrange("p (a n) -> p a n", a=2)[:, :, 0:n],
                               ACT.Copy).then_inc(copied, 1)

            each(act, copy)
            act.wait_ge(cleared, 1)
            act.dma_start(k.table[N:NB * P, :], empty[0:NB * P - N, :]).then_inc(empties, 16)
            act.wait_ge(empties, 16)

        @block.tensor
        def _(pe):
            def turn(b, r, i):
                pe.wait_ge(x_in[r], i * 16 + 16)
                wait(pe, copied, b - 1)
                n = size(b)
                for j in range(2):
                    last = pe.transpose(pT[:, r % 2, j * P:j * P + n], xin[0:n, r, j * P:(j + 1) * P],
                                        k.ident[0:n, 0:n])
                last.then_inc(turned, 1)

            def multiply(b, r, i):
                pe.wait_ge(copied, b + 1)
                wait(pe, rows, b - 1)
                n = size(b)
                for j in range(2):
                    last = pe.matmul(pW[0:n, r % 2, 0:W_EXT], xT[:, r % 2, j, 0:n], w[:, j, :],
                                     start=(j == 0), stop=(j == 1))
                last.then_inc(product, 1)

            def both(b, r, i):
                turn(b, r, i)
                if not (isinstance(b, int) and b == 0):
                    multiply(b - 1, (r - 1) % RX, i)

            pe.wait_ge(w_done, 1)
            each(pe, both)
            multiply(NB - 1, (NB - 1) % RX, 0)

        @block.gpsimd
        def _(pool):
            def store(b, r, i):
                pool.wait_ge(rows, b + 1)
                pool.dma_start(rows_of(k.table, b, size(b)), wh[0:size(b), r, 0:ROWT]).then_inc(stored[r], 16)

            def store_loop(i):
                for r in range(RX):
                    store(i * RX + r, r, i)

            due = pool.alloc_register("due_rows")
            for r in range(RX):
                store(r, r, 0)
            pool.reg_mov(due, RX + 1)
            with pool.Fori(1, MAIN // RX) as i:
                for r in range(RX):
                    pool.wait_ge(rows, due)
                    pool.reg_add(due, due, 1)
                    pool.dma_start(k.table[ds(i * (RX * P) + r * P, P), :], wh[:, r, 0:ROWT]).then_inc(stored[r], 16)
            for b in TAIL:
                store(b, b % RX, 0)
            pool.wait_ge(lows, 1)
            pool.partition_all_reduce(low_r[:, :], low_n[:, :], P, bass.bass_isa.ReduceOp.max).then_inc(all_low, 1)
            for r in range(RX):
                pool.wait_ge(stored[r], 16 * (len(range(r, NB, RX))))

        @block.vector
        def _(dve):
            dve.memset(empty[:, 0:D], 0.0)
            dve.memset(empty[:, D:ROWT], FAR).then_inc(cleared, 1)
            dve.memset(t_all[:, :, :], -FAR)
            dve.memset(k.s_all[:, :, :], 0.0)
            dve.wait_ge(w_in, 48)
            n = 0
            for part in range(2):
                for h in range(HEADS):
                    col = D + part * HEADS + h
                    av = a_all[:, (1 - part) * HD:(2 - part) * HD]
                    for j in range(3):
                        wv, to = (w[:, j, h * HD:(h + 1) * HD], w[:, j, col:col + 1]) if j < 2 else (
                            bias[:, h * HD:(h + 1) * HD], bias[:, col:col + 1])
                        last = dve.tensor_tensor_reduce(junk[:, n, :], wv, av, 1.0, 0.0, ALU.mult, ALU.add, to)
                        n += 1
            last.then_inc(w_done, 1)
            dve.wait_ge(w_done, 1)

            def finish(b, r, i):
                dve.wait_ge(product, b + 1)
                if not (isinstance(i, int) and i == 0):
                    dve.wait_ge(stored[r], i * 16)
                n = size(b)
                dve.tensor_tensor(wh[0:n, r, :], pW[0:n, r % 2, 0:W_EXT], bias[0:n, :], ALU.add).then_inc(rows, 1)
                dve.wait_ge(rows, b + 1)
                bs = slice(b, b + 1) if isinstance(b, int) else ds(b, 1)
                dve.tensor_copy(t_all[0:n, :, bs], wh[0:n, r, D:ROWT].unsqueeze(2))
                dve.tensor_copy(k.s_all[0:n, bs, :], wh[0:n, r, ROWT:W_EXT].unsqueeze(1))

            each(dve, finish)
            link = [0]

            def after_all(ins):
                link[0] += 1
                ins.then_inc(lows_step, 1)
                dve.wait_ge(lows_step, link[0])

            lows_step = k.link
            after_all(dve.nop())
            after_all(dve.drain())
            after_all(dve.tensor_reduce(low[:, :], t_all[:, :, :], X, ALU.min))
            dve.tensor_scalar(low_n[:, :], low[:, :], -1.0, None, ALU.mult).then_inc(lows, 1)
            dve.wait_ge(all_low, 1)
            after_all(dve.tensor_scalar(k.t_low[:, :], low_r[:, :], -1.0, None, ALU.mult))
            dve.tensor_tensor(k.s_all[:, :, :], k.s_all[:, :, :],
                              k.t_low[:, :].unsqueeze(1).to_broadcast([P, NB, HEADS]), ALU.add)


def slots(i, j):
    return i * RING + j, i + j // RING, j % RING


def gather_rows(pool, k, table, width, table_rows, ready, lead):
    bound = pool.to_reg(table_rows - 1)
    due = pool.alloc_register("due_group" + table.name)

    def gather(r):
        for c in range(GROUP):
            at = r * GROUP + c
            pool.indirect_dma_start(out=k.rows[:, at, 0:width], out_offset=None, in_=table[:, :],
                                    in_offset=bass.IndirectOffsetOnAxis(ap=k.wanted[:, at:at + 1], axis=0),
                                    bounds_check=bound, oob_is_err=False).then_inc(k.gathered[r], 16)

    for r in range(RING):
        pool.wait_ge(ready, max(1, r - lead + 2))
        gather(r)
    pool.reg_mov(due, RING - lead + 2)
    with pool.Fori(1, TURNS):
        for r in range(RING):
            pool.wait_ge(ready, due)
            pool.reg_add(due, due, 1)
            gather(r)


def block_values(eng, regs, k, q, g):
    eng.load(regs, k.block_row[q][0:1, ds(g * GROUP, GROUP)])
    return [eng.snap(r, min_val=0, max_val=NB - 1) for r in regs]


def turns(eng, step):
    for j in range(RING):
        step(0, j, True, False)
    with eng.Fori(1, TURNS - 1) as i:
        for j in range(RING):
            step(i, j, False, False)
    for j in range(RING):
        step(TURNS - 1, j, False, True)


def gat_pass(nc, k):
    LEAD = RING - 1
    with ExitStack() as c_:
        def tmp(name, shape, dt=F32):
            return c_.enter_context(nc.sbuf_tensor(name, shape, dt))

        def sem(name):
            return c_.enter_context(nc.semaphore(name))

        def ps(name, shape):
            return c_.enter_context(nc.psum_tensor(name, shape, F32))

        onehot = tmp("onehot_g", [P, 4, GROUP, P])
        scores = tmp("scores", [P, HEADS, GROUP, P])
        t_edge = tmp("t_edge", [P, 4, GROUP, HEADS])
        hot_node = tmp("hot_node", [P, GROUP, P])
        weighted = tmp("weighted", [P, 2, GROUP, ACC])
        top = tmp("top", [P, 2, HEADS, GROUP + 1])
        running = tmp("running_max", [P, 2, HEADS, GROUP + 1])
        z_node = tmp("z_node", [P, 2, HEADS, GROUP])
        m_before = tmp("m_before", [P, HEADS, GROUP])
        fall = tmp("fall", [P, HEADS, GROUP])
        fall_m = tmp("fall_m", [P, 2, HEADS, GROUP])
        factor = tmp("factor", [P, 2, HEADS, GROUP])
        node = tmp("node", [P, 2, GROUP, 2 * HEADS])
        z_edge = tmp("z_edge", [P, GROUP, HEADS])
        e_edge = tmp("e_edge", [P, GROUP, HEADS])
        power = tmp("power", [P, 2, GROUP, HEADS])

        known = sem("known")
        started = sem("started")
        k.gathered = [sem(f"gathered{r}") for r in range(RING)]
        t_ready = sem("t_ready")
        scored = sem("scored")
        turned = sem("turned_g")
        s_ready = sem("s_ready")
        maxed = sem("maxed")
        scanned = sem("scanned")
        z_ready = sem("z_ready")
        m_ready = sem("m_ready")
        fell = sem("fell")
        fall_ready = sem("fall_ready")
        factor_ready = sem("factor_ready")
        hot_copied = sem("hot_copied")
        q_ready = sem("q_ready")
        z_known = sem("z_known")
        e_known = sem("e_known")
        power_ready = sem("power_ready")
        weights = sem("weights")
        scaled = sem("scaled")
        summed = sem("summed")
        added = sem("added")

        scores_t = ps("scores_t", [P, HEADS * GROUP, P])
        hot_t = ps("hot_t", [P, GROUP, P])
        part = ps("part", [P, GROUP, 512])
        q_edge = ps("q_edge", [P, GROUP, 2 * HEADS])

        def weights_at(s):
            return weighted[:, s, :, :].rearrange("p c (h d) -> p c h d", h=HEADS)[:, :, :, HD:HD + 1]

        block = c_.enter_context(nc.Block())

        @block.gpsimd
        def _(pool):
            gather_rows(pool, k, k.table, ROWT, NB * P, known, LEAD)

        @block.scalar
        def _(act):
            regs = [act.alloc_register(f"act_block{c}") for c in range(GROUP)]

            def node_s(i, j):
                g, _, _ = slots(i, j)
                for c, b in enumerate(block_values(act, regs, k, 0, g)):
                    last = act.activation(node[:, j % 2, c, 0:HEADS],
                                          k.s_all[:, ds(b, 1), :].rearrange("p o h -> p (o h)"), ACT.Copy)
                last.then_inc(s_ready, 1)

            def weigh(i, j):
                g, _, r = slots(i, j)
                act.wait_ge(power_ready, g + 1)
                act.activation(weights_at(j % 2), power[:, j % 2, :, :].unsqueeze(3), ACT.Exp).then_inc(weights, 1)
                act.wait_ge(weights, g + 1)
                for c in range(GROUP):
                    for h in range(HEADS):
                        o = h * (HD + 1)
                        last = act.activation(weighted[:, j % 2, c, o:o + HD],
                                              k.rows[:, r * GROUP + c, h * HD:(h + 1) * HD], ACT.Copy,
                                              scale=weighted[:, j % 2, c, o + HD:o + HD + 1])
                    last.then_inc(scaled, 1)

            def step(i, j, first, last):
                g, _, _ = slots(i, j)
                if not (first and j == 0):
                    weigh(i, j - 1)
                act.wait_ge(turned, g + 1)
                act.activation(hot_node[:, :, :], hot_t[:, :, :], ACT.Copy).then_inc(hot_copied, 1)
                act.wait_ge(fall_ready, g + 1)
                act.activation(factor[:, j % 2, :, :], fall_m[:, j % 2, :, :], ACT.Exp).then_inc(factor_ready, 1)
                if not (last and j == RING - 1):
                    node_s(i, j + 1)

            node_s(0, 0)
            turns(act, step)
            weigh(TURNS - 1, RING - 1)

        @block.tensor
        def _(pe):
            def turn_scores(i, j):
                g, _, _ = slots(i, j)
                for c in range(GROUP):
                    pe.wait_ge(scored, g * GROUP + c + 1)
                    for h in range(HEADS):
                        pe.transpose(scores_t[:, h * GROUP + c, :], scores[:, h, c, :], k.ident[:, :])
                    last = pe.transpose(hot_t[:, c, :], onehot[:, j % 4, c, :], k.ident[:, :])
                last.then_inc(turned, 1)

            def add_up(i, j):
                g, _, _ = slots(i, j)
                for c in range(GROUP):
                    pe.wait_ge(scaled, g * GROUP + c + 1)
                    pe.matmul(part[:, c, 0:ACC], onehot[:, j % 4, c, :], weighted[:, j % 2, c, :],
                              start=True, stop=True).then_inc(summed, 1)

            def step(i, j, first, last):
                g, _, _ = slots(i, j)
                if not (first and j == 0):
                    add_up(i, j - 1)
                pe.wait_ge(hot_copied, g + 1)
                pe.wait_ge(m_ready, g + 1)
                for c in range(GROUP):
                    mm = pe.matmul(q_edge[:, c, :], hot_node[:, c, :], node[:, j % 2, c, :], start=True, stop=True)
                mm.then_inc(q_ready, 1)
                if not (last and j == RING - 1):
                    turn_scores(i, j + 1)

            turn_scores(0, 0)
            turns(pe, step)
            add_up(TURNS - 1, RING - 1)

        @block.vector
        def _(dve):
            regs = [dve.alloc_register(f"dve_block{c}") for c in range(GROUP)]

            def edge_t(i, j):
                g, turn, r = slots(i, j)
                dve.wait_ge(k.gathered[r], (turn + 1) * (16 * GROUP))
                dve.tensor_tensor(t_edge[:, j % 4, :, :], k.rows[:, r * GROUP:(r + 1) * GROUP, D:ROWT],
                                  k.t_low[:, :].unsqueeze(1).to_broadcast([P, GROUP, HEADS]),
                                  ALU.subtract).then_inc(t_ready, 1)

            def edge_scores(i, j, c):
                g, _, _ = slots(i, j)
                at = k.spot[:, ds(g * GROUP + c, 1)]
                dve.tensor_scalar(onehot[:, j % 4, c, :], k.ramp[:, :], at, None, ALU.is_equal)
                if c == 0:
                    dve.wait_ge(t_ready, g + 1)
                for h in range(HEADS):
                    last = dve.tensor_scalar(scores[:, h, c, :], k.ramp[:, :], at, t_edge[:, j % 4, c, h:h + 1],
                                             ALU.is_equal, ALU.mult)
                last.then_inc(scored, 1)

            def node_max(i, j):
                g, _, _ = slots(i, j)
                s = j % 2
                dve.wait_ge(turned, g + 1)
                dve.tensor_reduce(top[:, s, :, 1:GROUP + 1],
                                  scores_t[:, :, :].rearrange("p (h c) e -> p h c e", h=HEADS), X, ALU.max)
                dve.tensor_copy(top[:, s, :, 0:1], running[:, 1 - s, :, GROUP:GROUP + 1]).then_inc(maxed, 1)
                dve.wait_ge(maxed, g + 1)
                dve.tensor_tensor_scan(running[:, s, :, :].rearrange("p h c -> p (h c)"),
                                       k.carry[:, ds(g, 1), :, :].rearrange("p o h c -> p (o h c)"),
                                       top[:, s, :, :].rearrange("p h c -> p (h c)"), 0.0,
                                       ALU.mult, ALU.max).then_inc(scanned, 1)
                dve.wait_ge(scanned, g + 1)
                dve.wait_ge(s_ready, g + 1)
                s_here = node[:, s, :, 0:HEADS].rearrange("p c h -> p h c")
                dve.tensor_tensor(z_node[:, 0, :, :], running[:, s, :, 1:GROUP + 1], s_here, ALU.add)
                dve.tensor_tensor(z_node[:, 1, :, :], running[:, s, :, 0:GROUP], s_here, ALU.add).then_inc(z_ready, 1)
                dve.wait_ge(z_ready, g + 1)
                m_here = node[:, s, :, HEADS:2 * HEADS].rearrange("p c h -> p h c")
                dve.scalar_tensor_tensor(m_here, z_node[:, 0, :, :], SLOPE, z_node[:, 0, :, :], ALU.mult, ALU.max)
                dve.scalar_tensor_tensor(m_before[:, :, :], z_node[:, 1, :, :], SLOPE, z_node[:, 1, :, :],
                                         ALU.mult, ALU.max).then_inc(m_ready, 1)
                dve.wait_ge(m_ready, g + 1)
                dve.tensor_tensor(fall[:, :, :], m_before[:, :, :], m_here, ALU.subtract).then_inc(fell, 1)
                dve.wait_ge(fell, g + 1)
                dve.scalar_tensor_tensor(fall_m[:, s, :, :], fall[:, :, :], 0.0,
                                         k.fresh[:, ds(g * GROUP, GROUP)].unsqueeze(1).to_broadcast([P, HEADS, GROUP]),
                                         ALU.min, ALU.add).then_inc(fall_ready, 1)

            def add_chunk(i, j, c, b):
                g, _, _ = slots(i, j)
                dve.wait_ge(summed, g * GROUP + c + 1)
                wait(dve, added, g * GROUP + c)
                for h in range(HEADS):
                    mine = k.acc[:, ds(b * ACC + h * (HD + 1), HD + 1)]
                    last = dve.scalar_tensor_tensor(mine, mine, factor[:, j % 2, h, c:c + 1],
                                                    part[:, c, h * (HD + 1):(h + 1) * (HD + 1)], ALU.mult, ALU.add)
                last.then_inc(added, 1)

            def edge_power(i, j):
                g, _, _ = slots(i, j)
                dve.wait_ge(q_ready, g + 1)
                dve.tensor_tensor(z_edge[:, :, :], q_edge[:, :, 0:HEADS], t_edge[:, j % 4, :, :],
                                  ALU.add).then_inc(z_known, 1)
                dve.wait_ge(z_known, g + 1)
                dve.scalar_tensor_tensor(e_edge[:, :, :], z_edge[:, :, :], SLOPE, z_edge[:, :, :],
                                         ALU.mult, ALU.max).then_inc(e_known, 1)
                dve.wait_ge(e_known, g + 1)
                dve.tensor_tensor(power[:, j % 2, :, :], e_edge[:, :, :], q_edge[:, :, HEADS:2 * HEADS],
                                  ALU.subtract).then_inc(power_ready, 1)

            def step(i, j, first, last):
                g, _, _ = slots(i, j)
                has_next = not (last and j == RING - 1)
                has_prev = not (first and j == 0)
                if has_next:
                    edge_t(i, j + 1)
                node_max(i, j)
                if has_prev:
                    blocks = block_values(dve, regs, k, 0, g - 1)
                    dve.wait_ge(factor_ready, g)
                for c in range(GROUP):
                    if has_prev:
                        add_chunk(i, j - 1, c, blocks[c])
                    if has_next:
                        edge_scores(i, j + 1, c)
                if not last or j == 0:
                    r = (j + LEAD) % RING
                    dve.tensor_copy(k.wanted[:, r * GROUP:(r + 1) * GROUP],
                                    k.row[:, ds((g + LEAD) * GROUP, GROUP)]).then_inc(known, 1)
                edge_power(i, j)

            dve.memset(k.acc[:, :], 0.0)
            dve.memset(running[:, :, :, :], 0.0)
            dve.tensor_copy(k.wanted[:, 0:LEAD * GROUP], k.row[:, 0:LEAD * GROUP]).then_inc(known, 1)
            dve.nop().then_inc(started, 1)
            edge_t(0, 0)
            for c in range(GROUP):
                edge_scores(0, 0, c)
            turns(dve, step)
            end = block_values(dve, regs, k, 0, GROUPS - 1)
            dve.wait_ge(factor_ready, GROUPS)
            for c in range(GROUP):
                add_chunk(TURNS - 1, RING - 1, c, end[c])


def sage_pass(nc, k, table, count):
    LEAD = RING
    WIDE = D + 1 if count else D
    tag = int(not count)
    with ExitStack() as c_:
        def sem(name):
            return c_.enter_context(nc.semaphore(name))

        onehot = c_.enter_context(nc.sbuf_tensor(f"onehot_s{tag}", [P, 4, GROUP, P], F32))
        known = sem(f"known_s{tag}")
        k.gathered = [sem(f"gathered_s{tag}{r}") for r in range(RING)]
        hot = sem(f"hot_s{tag}")
        summed = sem(f"summed_s{tag}")
        added = sem(f"added_s{tag}")
        part = c_.enter_context(nc.psum_tensor(f"part_s{tag}", [P, 2, GROUP, 512], F32))
        block = c_.enter_context(nc.Block())

        @block.gpsimd
        def _(pool):
            gather_rows(pool, k, table, D, NB * P, known, LEAD)

        @block.tensor
        def _(pe):
            def step(i, j, first, last):
                g, turn, r = slots(i, j)
                pe.wait_ge(k.gathered[r], (turn + 1) * (16 * GROUP))
                pe.wait_ge(hot, g + 1)
                wait(pe, added, g * GROUP - GROUP)
                for c in range(GROUP):
                    pe.matmul(part[:, j % 2, c, 0:WIDE], onehot[:, j % 4, c, :],
                              k.rows[:, r * GROUP + c, 0:WIDE], start=True, stop=True).then_inc(summed, 1)

            turns(pe, step)

        @block.vector
        def _(dve):
            regs = [dve.alloc_register(f"dve_block_s{tag}{c}") for c in range(GROUP)]

            def hot_rows(i, j, c):
                g, _, _ = slots(i, j)
                ins = dve.tensor_scalar(onehot[:, j % 4, c, :], k.ramp[:, :], k.spot[:, ds(g * GROUP + c, 1)], None,
                                        ALU.is_equal)
                if c == GROUP - 1:
                    ins.then_inc(hot, 1)

            def step(i, j, first, last):
                g, _, _ = slots(i, j)
                blocks = block_values(dve, regs, k, 1, g)
                for c in range(GROUP):
                    dve.wait_ge(summed, g * GROUP + c + 1)
                    wait(dve, added, g * GROUP + c)
                    mine = k.acc[:, ds(blocks[c] * ACC, WIDE)]
                    dve.tensor_tensor(mine, mine, part[:, j % 2, c, 0:WIDE], ALU.add).then_inc(added, 1)
                    if not (last and j >= RING - 2):
                        hot_rows(i, j + 2, c)
                if not last:
                    r = j % RING
                    dve.tensor_copy(k.wanted[:, r * GROUP:(r + 1) * GROUP],
                                    k.row[:, ds((g + LEAD) * GROUP, GROUP)]).then_inc(known, 1)

            dve.memset(k.acc[:, :], 0.0)
            if count:
                dve.memset(k.rows[:, :, D:D + 1], 1.0)
            dve.nop()
            dve.tensor_copy(k.wanted[:, 0:LEAD * GROUP], k.row[:, 0:LEAD * GROUP]).then_inc(known, 1)
            for j in range(2):
                for c in range(GROUP):
                    hot_rows(0, j, c)
            turns(dve, step)


UNIT = 7
UNITS = NB // UNIT
assert UNITS * UNIT == NB and UNITS % 2 == 0


def unit_rows(table, u):
    rows = table[ds(u * (UNIT * P), UNIT * P), :] if not isinstance(u, int) else table[u * UNIT * P:(u + 1) * UNIT * P, :]
    return rows.rearrange("(b p) d -> p b d", p=P)


def move_unit(eng, on_chip, table, u, sem, load):
    whole = UNIT - 1
    first = u * (UNIT * P)
    last_rows = LAST if isinstance(u, int) and u == UNITS - 1 else P

    def rows(start, n):
        return table[start:start + n, :] if isinstance(start, int) else table[ds(start, n), :]

    for chip, dram in ((on_chip[:, 0:whole, :], rows(first, whole * P).rearrange("(b p) d -> p b d", p=P)),
                       (on_chip[0:last_rows, whole, :], rows(first + whole * P, last_rows))):
        eng.dma_start(*((chip, dram) if load else (dram, chip))).then_inc(sem, 16)


def unit_turns(eng, f):
    for h in range(2):
        f(h, h, 0)
    with eng.Fori(1, UNITS // 2 - 1) as i:
        for h in range(2):
            f(i * 2 + h, h, i)
    for h in range(2):
        f(UNITS - 2 + h, h, UNITS // 2 - 1)


def gat_end(nc, k, x):
    with ExitStack() as c:
        def tmp(name, shape, dt=F32):
            return c.enter_context(nc.sbuf_tensor(name, shape, dt))

        def sem(name):
            return c.enter_context(nc.semaphore(name))

        xin = tmp("xin_e", [P, 2, UNIT, D])
        own = tmp("own", [P, 2, UNIT, D])
        total = tmp("total", [P, 2, UNIT, D])
        weight = tmp("weight", [P, NB, HEADS])
        alone = tmp("alone", [P, NB, HEADS])
        stats = tmp("stats", [P, UNIT, 6])
        mean = tmp("mean", [P, UNIT, 2])
        spread = tmp("spread", [P, UNIT])
        eps = tmp("eps", [P, 1])
        x_in = [sem(f"x_in_e{h}") for h in range(2)]
        own_in = [sem(f"own_in{h}") for h in range(2)]
        tick = sem("tick")
        cleared = sem("cleared_e")
        var_ready = sem("var_ready")
        stats_seen = sem("stats_seen")
        root_ready = sem("root_ready")
        normed = sem("normed")
        stored = [sem(f"stored_e{h}") for h in range(2)]
        block = c.enter_context(nc.Block())

        @block.sync
        def _(sp):
            def load(u, h, i):
                if h == 0 and isinstance(u, int) and u == 0:
                    sp.wait_ge(cleared, 1)
                wait(sp, normed, u - 1)
                move_unit(sp, xin[:, h, :, :], x, u, x_in[h], True)
                sp.dma_start(own[:, h, :, :], unit_rows(k.table, u)[:, :, 0:D]).then_inc(own_in[h], 16)

            unit_turns(sp, load)

        @block.scalar
        def _(act):
            def store(u, h, i):
                act.wait_ge(var_ready, u + 1)
                act.activation(spread[:, :], mean[:, :, 1:2].rearrange("p u o -> p (u o)"), ACT.Sqrt,
                               bias=eps[:, 0:1]).then_inc(root_ready, 1)
                act.wait_ge(normed, u + 1)
                act.dma_start(unit_rows(k.x1, u), total[:, h, :, :]).then_inc(stored[h], 16)

            unit_turns(act, store)
            for h in range(2):
                act.wait_ge(stored[h], 16 * (UNITS // 2))

        @block.vector
        def _(dve):
            dve.memset(eps[:, :], EPS)
            dve.memset(xin[:, :, UNIT - 1, :], 0.0).then_inc(cleared, 1)
            sums = k.acc[:, :].rearrange("p (b h d) -> p b h d", b=NB, h=HEADS)
            total_w = sums[:, :, :, HD:HD + 1].rearrange("p b h o -> p b (h o)")
            dve.tensor_scalar(alone[:, :, :], total_w, 0.0, None, ALU.is_equal)
            dve.tensor_scalar(weight[:, :, :], total_w, 1e-30, None, ALU.max).then_inc(tick, 1)
            dve.wait_ge(tick, 1)
            dve.reciprocal(weight[:, :, :], weight[:, :, :]).then_inc(tick, 1)
            dve.wait_ge(tick, 2)
            PER = 5

            def finish(u, h, i):
                n = u * PER + 2

                def stage(s):
                    dve.wait_ge(tick, n + s)

                dve.wait_ge(x_in[h], (i + 1) * 32)
                if not (isinstance(i, int) and i == 0):
                    dve.wait_ge(stored[h], i * 16)
                for b in range(UNIT):
                    for hd in range(HEADS):
                        at = u * UNIT + b
                        cut = slice(hd * HD, (hd + 1) * HD)
                        last = dve.scalar_tensor_tensor(
                            total[:, h, b, cut], k.acc[:, ds(at * ACC + hd * (HD + 1), HD)],
                            weight[:, ds(at, 1), hd:hd + 1].rearrange("p o h -> p (o h)"), xin[:, h, b, cut],
                            ALU.mult, ALU.add)
                last.then_inc(tick, 1)
                stage(1)
                dve.wait_ge(own_in[h], (i + 1) * 16)
                for b in range(UNIT):
                    for hd in range(HEADS):
                        cut = slice(hd * HD, (hd + 1) * HD)
                        last = dve.scalar_tensor_tensor(
                            total[:, h, b, cut], own[:, h, b, cut],
                            alone[:, ds(u * UNIT + b, 1), hd:hd + 1].rearrange("p o h -> p (o h)"),
                            total[:, h, b, cut], ALU.mult, ALU.add)
                last.then_inc(tick, 1)
                stage(2)
                for b in range(UNIT):
                    last = dve.bn_stats(stats[:, b, :], total[:, h, b, :])
                last.then_inc(tick, 1)
                stage(3)
                dve.nop().then_inc(stats_seen, 1)
                for b in range(UNIT):
                    last = dve.bn_aggr(mean[:, b, :], stats[:, b, :])
                last.then_inc(var_ready, 1)
                dve.wait_ge(root_ready, u + 1)
                dve.wait_ge(var_ready, u + 1)
                dve.reciprocal(spread[:, :], spread[:, :]).then_inc(tick, 1)
                stage(4)
                for b in range(UNIT):
                    last = dve.tensor_scalar(total[:, h, b, :], total[:, h, b, :], mean[:, b, 0:1],
                                             spread[:, b:b + 1], ALU.subtract, ALU.mult)
                last.then_inc(normed, 1)
                dve.wait_ge(normed, u + 1)
                dve.nop().then_inc(tick, 1)

            unit_turns(dve, finish)


def sage_end(nc, k, table, Wl, bl, Wr, out, final):
    with ExitStack() as c:
        def tmp(name, shape, dt=F32):
            return c.enter_context(nc.sbuf_tensor(name, shape, dt))

        def sem(name):
            return c.enter_context(nc.semaphore(name))

        tag = "f" if final else "h"
        wl = tmp("wl" + tag, [P, 2, D])
        wr = tmp("wr" + tag, [P, 2, D])
        bias = tmp("bias" + tag, [P, D])
        rows = tmp("rows_e" + tag, [P, 2, UNIT, D])
        first = tmp("first" + tag, [P, 2, UNIT, D]) if final else None
        result = tmp("result" + tag, [P, 2, UNIT, D])
        average = tmp("average" + tag, [P, 4, D])
        turned_sb = tmp("turned_sb" + tag, [P, 2, 4, P])
        biased = tmp("biased" + tag, [P, 2, D])
        stats = tmp("stats" + tag, [P, UNIT, 6])
        mean = tmp("mean" + tag, [P, UNIT, 2])
        spread = tmp("spread" + tag, [P, UNIT])
        eps = tmp("eps" + tag, [P, 1])
        w_in = sem("w_in" + tag)
        rows_in = [sem(f"rows_in{tag}{h}") for h in range(2)]
        first_in = [sem(f"first_in{tag}{h}") for h in range(2)]
        setup = sem("setup" + tag)
        averaged = sem("averaged" + tag)
        turned = sem("turned" + tag)
        copied = sem("copied" + tag)
        product = sem("product" + tag)
        biased_ready = sem("biased_ready" + tag)
        tick = sem("tick" + tag)
        var_ready = sem("var_ready" + tag)
        stats_seen = sem("stats_seen" + tag)
        root_ready = sem("root_ready" + tag)
        unit_done = sem("unit_done" + tag)
        stored = [sem(f"stored{tag}{h}") for h in range(2)]
        pT = c.enter_context(nc.psum_tensor("pT" + tag, [P, 2, 4, P], F32))
        pO = c.enter_context(nc.psum_tensor("pO" + tag, [P, 2, 512], F32))
        block = c.enter_context(nc.Block())

        @block.sync
        def _(sp):
            for t, w in ((wl, Wl), (wr, Wr)):
                sp.dma_start(t[:, :, :], w.rearrange("(j p) n -> p j n", p=P)).then_inc(w_in, 16)
            sp.dma_start(bias[:, :], bl.rearrange("(o n) -> o n", o=1).to_broadcast([P, D])).then_inc(w_in, 16)

            def load(u, h, i):
                wait(sp, unit_done, u - 1)
                sp.dma_start(rows[:, h, :, :], unit_rows(table, u)).then_inc(rows_in[h], 16)
                if final:
                    sp.dma_start(first[:, h, :, :], unit_rows(k.x1, u)).then_inc(first_in[h], 16)

            unit_turns(sp, load)

        @block.tensor
        def _(pe):
            def turn(u, h, i, b):
                n = u * UNIT + b
                s = (h * UNIT + b)
                if b == 0:
                    pe.wait_ge(rows_in[h], (i + 1) * 16)
                pe.wait_ge(averaged, n + 1)
                wait(pe, copied, n - 1)
                for j in range(2):
                    pe.transpose(pT[:, s % 2, j, :], average[:, s % 2, j * P:(j + 1) * P],
                                 k.ident[:, :])
                for j in range(2):
                    last = pe.transpose(pT[:, s % 2, 2 + j, :], rows[:, h, b, j * P:(j + 1) * P], k.ident[:, :])
                last.then_inc(turned, 1)

            def multiply(u, h, b):
                n = u * UNIT + b
                s = (h * UNIT + b) % 2
                pe.wait_ge(copied, n + 1)
                wait(pe, biased_ready, n - 1)
                for j in range(4):
                    w = (wl, wr)[j // 2]
                    last = pe.matmul(pO[:, s, 0:D], turned_sb[:, s, j, :], w[:, j % 2, :], start=(j == 0),
                                     stop=(j == 3))
                last.then_inc(product, 1)

            def unit(u, h, i):
                for b in range(UNIT):
                    turn(u, h, i, b)
                    if not (isinstance(u, int) and u == 0 and b == 0):
                        if b:
                            multiply(u, h, b - 1)
                        else:
                            multiply(u - 1, 1 - h, UNIT - 1)

            pe.wait_ge(w_in, 48)
            unit_turns(pe, unit)
            multiply(UNITS - 1, 1, UNIT - 1)

        @block.scalar
        def _(act):
            act.wait_ge(setup, 1)

            def unit(u, h, i):
                for b in range(UNIT):
                    n = u * UNIT + b
                    s = (h * UNIT + b) % 2
                    act.wait_ge(turned, n + 1)
                    wait(act, product, n - 1)
                    act.activation(turned_sb[:, s, :, :], pT[:, s, :, :], ACT.Copy).then_inc(copied, 1)
                    if not final and not (isinstance(u, int) and u == 0 and b == 0):
                        rectify(u, h, i, b - 1)
                if final:
                    root(u)

            def rectify(u, h, i, b):
                if b < 0:
                    u, h, i, b = u - 1, 1 - h, (i if h == 1 else i - 1), UNIT - 1
                n = u * UNIT + b
                s = (h * UNIT + b) % 2
                if b == 0 and not (isinstance(i, int) and i == 0):
                    act.wait_ge(stored[h], i * 16)
                act.wait_ge(biased_ready, n + 1)
                ins = act.activation(result[:, h, b, :], biased[:, s, :], ACT.Relu)
                ins.then_inc(tick, 1)
                if b == UNIT - 1:
                    act.wait_ge(tick, n + 1)
                    act.nop().then_inc(unit_done, 1)

            def root(u):
                act.wait_ge(var_ready, u + 1)
                act.activation(spread[:, :], mean[:, :, 1:2].rearrange("p u o -> p (u o)"), ACT.Sqrt,
                               bias=eps[:, 0:1]).then_inc(root_ready, 1)

            unit_turns(act, unit)
            if not final:
                rectify(UNITS - 1, 1, UNITS // 2 - 1, UNIT - 1)

        @block.gpsimd
        def _(pool):
            due = pool.alloc_register("due_unit" + tag)
            pool.reg_mov(due, 3)

            def store(u, h, i):
                if isinstance(u, int):
                    pool.wait_ge(unit_done, u + 1)
                else:
                    pool.wait_ge(unit_done, due)
                    pool.reg_add(due, due, 1)
                if final:
                    move_unit(pool, result[:, h, :, :], out, u, stored[h], False)
                else:
                    pool.dma_start(unit_rows(out, u), result[:, h, :, :]).then_inc(stored[h], 16)

            unit_turns(pool, store)
            for h in range(2):
                pool.wait_ge(stored[h], (32 if final else 16) * (UNITS // 2))

        @block.vector
        def _(dve):
            dve.memset(eps[:, :], EPS).then_inc(setup, 1)
            if not final:
                counts = k.acc[:, :].rearrange("p (b d) -> p b d", b=NB)[:, :, D:D + 1].rearrange("p b o -> p (b o)")
                dve.tensor_scalar(k.share[:, :], counts, 1.0, None, ALU.max).then_inc(setup, 1)
                dve.wait_ge(setup, 2)
                dve.reciprocal(k.share[:, :], k.share[:, :]).then_inc(setup, 1)
                dve.wait_ge(setup, 3)

            def average_of(u, h, b):
                n = u * UNIT + b
                s = (h * UNIT + b) % 2
                wait(dve, turned, n - 1)
                dve.tensor_scalar(average[:, s, :], k.acc[:, ds(n * ACC, D)], k.share[:, ds(n, 1)], None,
                                  ALU.mult).then_inc(averaged, 1)

            dve.wait_ge(w_in, 48)

            def unit(u, h, i):
                if final:
                    dve.wait_ge(first_in[h], (i + 1) * 16)
                    if not (isinstance(i, int) and i == 0):
                        dve.wait_ge(stored[h], i * 32)
                for b in range(UNIT):
                    n = u * UNIT + b
                    s = (h * UNIT + b) % 2
                    if b < UNIT - 1:
                        average_of(u, h, b + 1)
                    elif not (isinstance(u, int) and u == UNITS - 1):
                        average_of(u + 1, 1 - h, 0)
                    dve.wait_ge(product, n + 1)
                    if final:
                        wait(dve, biased_ready, n)
                    dve.tensor_tensor(biased[:, s, :], pO[:, s, 0:D], bias[:, :], ALU.add).then_inc(biased_ready, 1)
                    if final:
                        dve.wait_ge(biased_ready, n + 1)
                        dve.tensor_tensor(result[:, h, b, :], biased[:, s, :], first[:, h, b, :],
                                          ALU.add).then_inc(tick, 1)
                if not final:
                    return
                t = u * (UNIT + 2)
                dve.wait_ge(tick, t + UNIT)
                for b in range(UNIT):
                    last = dve.bn_stats(stats[:, b, :], result[:, h, b, :])
                last.then_inc(tick, 1)
                dve.wait_ge(tick, t + UNIT + 1)
                dve.nop().then_inc(stats_seen, 1)
                for b in range(UNIT):
                    last = dve.bn_aggr(mean[:, b, :], stats[:, b, :])
                last.then_inc(var_ready, 1)
                dve.wait_ge(root_ready, u + 1)
                dve.reciprocal(spread[:, :], spread[:, :]).then_inc(tick, 1)
                dve.wait_ge(tick, t + UNIT + 2)
                for b in range(UNIT):
                    last = dve.tensor_scalar(result[:, h, b, :], result[:, h, b, :], mean[:, b, 0:1],
                                             spread[:, b:b + 1], ALU.subtract, ALU.mult)
                last.then_inc(unit_done, 1)

            average_of(0, 0, 0)
            unit_turns(dve, unit)


def build(nc, x, src, dst, Ww, Wb, a, Wl1, b1, Wr1, Wl2, b2, Wr2, out, debug=()):
    with ExitStack() as ctx:
        k = Kernel()

        def sb(name, shape, dt):
            return ctx.enter_context(nc.sbuf_tensor(name, shape, dt))

        def dram(name, shape, dt):
            kind = "ExternalOutput" if name in debug else "Internal"
            return nc.dram_tensor(name, shape, dt, kind=kind).ap()

        k.sb = sb
        k.dbg = ctx.enter_context(nc.semaphore("dbg"))
        k.link = ctx.enter_context(nc.semaphore("link"))
        k.edges = [dram(f"edges{q}", (P, CHUNKS), I32) for q in range(LISTS)]
        k.table = dram("table", (NB * P, ROWT), F32)
        k.x1 = dram("x1", (NB * P, D), F32)
        k.hidden = dram("hidden", (NB * P, D), F32)
        k.carry = sb("carry", [P, GROUPS, HEADS, GROUP + 1], BF16)
        k.fresh = sb("fresh", [P, CHUNKS], F32)
        k.s_all = sb("s_all", [P, NB, HEADS], F32)
        k.t_low = sb("t_low", [P, HEADS], F32)
        constants(nc, k, ctx)
        sort_edges(nc, k, src, dst)
        project(nc, k, x, Ww, Wb, a)
        k.acc = sb("acc", [P, NB * ACC], F32)
        k.share = sb("share", [P, NB], F32)
        k.row = sb("row", [P, CHUNKS], I32)
        k.spot = sb("spot", [P, CHUNKS], F32)
        load_list(nc, k, 0)
        with ExitStack() as c:
            k.rows = c.enter_context(nc.sbuf_tensor("rows", [P, GROUP * RING, ROWT], F32))
            k.wanted = c.enter_context(nc.sbuf_tensor("wanted", [P, GROUP * RING], I32))
            gat_pass(nc, k)
        gat_end(nc, k, x)
        load_list(nc, k, 1)
        for n, (table, Wl, bl, Wr, to) in enumerate(((k.x1, Wl1, b1, Wr1, k.hidden), (k.hidden, Wl2, b2, Wr2, out))):
            with ExitStack() as c:
                k.rows = c.enter_context(nc.sbuf_tensor(f"rows_s{n}", [P, GROUP * RING, D + 1], F32))
                k.wanted = c.enter_context(nc.sbuf_tensor(f"wanted_s{n}", [P, GROUP * RING], I32))
                sage_pass(nc, k, table, n == 0)
            sage_end(nc, k, table, Wl, bl, Wr, to, n == 1)


_INS = ["x", "src", "dst", "L0_gnn_W_w", "L0_gnn_W_b", "L0_gnn_a", "L1_gnn_W_l1", "L1_gnn_b1", "L1_gnn_W_r1",
        "L1_gnn_W_l2", "L1_gnn_b2", "L1_gnn_W_r2"]


def kernel(**inputs):
    import concourse.bacc as bacc
    import numpy as np
    from concourse.bass_utils import run_bass_kernel_spmd as run

    nc = bacc.Bacc("TRN2", target_bir_lowering=False, num_devices=1)
    arrays, args = {}, []
    for name in _INS:
        array = np.ascontiguousarray(inputs[name])
        arrays[f"in_{name}"] = array
        args.append(nc.dram_tensor(f"in_{name}", array.shape, mybir.dt.from_np(array.dtype),
                                   kind="ExternalInput").ap())
    out = nc.dram_tensor("out", (N, D), F32, kind="ExternalOutput").ap()
    build(nc, *args, out)
    got = run(nc, [arrays], core_ids=[0])
    return got.results[0]["out"]
```

```python
from contextlib import ExitStack

import concourse.bass as bass
from concourse import mybir

F32 = mybir.dt.float32
BF16 = mybir.dt.bfloat16
I32 = mybir.dt.int32
ALU = mybir.AluOpType
ACT = mybir.ActivationFunctionType
X = mybir.AxisListType.X
ds = bass.ds

P = 128
N = 12500
D = 256
HEADS = 2
HD = D // HEADS
E = 200000
NB = -(-N // P)
LAST = N - (NB - 1) * P
EP = 125
EC = E // EP
LISTS = 2
GROUP = 4
RING = 8
BODY = GROUP * RING
CHUNKS = -(-((E + NB * (P - 1)) // P) // BODY) * BODY
GROUPS = CHUNKS // GROUP
TURNS = GROUPS // RING
SHIFT = 7
LOC = 256
PAD = N * LOC + 200
FAR = -1.0e30
ROWT = D + HEADS
ACC = HEADS * (HD + 1)
HALF = 8
AHEAD = HALF - 1
COLS = EC + HALF
EPS = 1e-5
SLOPE = 0.2


def wait(eng, sem, value):
    if isinstance(value, int) and value <= 0:
        return
    eng.wait_ge(sem, value)


def per_head(ap):
    return ap.rearrange("p (h d) -> p h d", h=HEADS)


class Kernel:
    pass


def constants(nc, k, ctx):
    sb = k.sb
    k.ramp = sb("ramp", [P, P], F32)
    k.place = sb("place", [P, 1], F32)
    k.ident = sb("ident", [P, P], F32)
    k.ones = sb("ones", [P, P], F32)
    with ExitStack() as c:
        ramp_i = c.enter_context(nc.sbuf_tensor("ramp_i", [P, P], I32))
        place_i = c.enter_context(nc.sbuf_tensor("place_i", [P, 1], I32))
        iotas = c.enter_context(nc.semaphore("iotas"))
        ramps = c.enter_context(nc.semaphore("ramps"))
        block = c.enter_context(nc.Block())

        @block.gpsimd
        def _(pool):
            pool.iota(ramp_i[:, :], pattern=[[1, P]], base=0, channel_multiplier=0).then_inc(iotas, 1)
            pool.iota(place_i[:, :], pattern=[[1, 1]], base=0, channel_multiplier=1).then_inc(iotas, 1)

        @block.vector
        def _(dve):
            dve.memset(k.ones[:, :], 1.0)
            dve.wait_ge(iotas, 2)
            dve.tensor_copy(k.ramp[:, :], ramp_i[:, :]).then_inc(ramps, 1)
            dve.tensor_copy(k.place[:, :], place_i[:, :]).then_inc(ramps, 1)
            dve.wait_ge(ramps, 2)
            dve.tensor_scalar(k.ident[:, :], k.ramp[:, :], k.place[:, 0:1], None, ALU.is_equal)


def sort_edges(nc, k, src, dst):
    PIECES = 4
    PIECE = CHUNKS // PIECES
    WINDOWS = CHUNKS // P
    assert WINDOWS * P == CHUNKS
    IN_ROWS = E // P + 2
    sb = k.sb
    k.block_row = [sb(f"block_row{q}", [1, CHUNKS], I32) for q in range(LISTS)]
    with ExitStack() as c:
        def tmp(name, shape, dt):
            return c.enter_context(nc.sbuf_tensor(name, shape, dt))

        def sem(name):
            return c.enter_context(nc.semaphore(name))

        key_block = tmp("key_block", [EP, LISTS, COLS], F32)
        entry = tmp("entry", [EP, LISTS, EC], I32)
        pads = tmp("pads", [P, CHUNKS], I32)
        before = tmp("before", [EP, EP], BF16)
        after = tmp("after", [EP, EP], BF16)
        before_f = tmp("before_f", [P, P], F32)
        chunks_f = tmp("chunks_f", [NB, LISTS], F32)
        start = tmp("start", [NB, LISTS], F32)
        base = tmp("base", [NB, LISTS, EP], F32)
        chunk_no = tmp("chunk_no", [NB, CHUNKS], I32)
        edges_f = tmp("edges_f", [NB, 1], F32)
        edges_before = tmp("edges_before", [NB, 1], F32)
        disorder = tmp("disorder", [EP, 2], F32)
        disorder_i = tmp("disorder_i", [1, 1], I32)
        in_order_in = sem("in_order_in")
        s = Kernel()
        s.key_block, s.entry, s.pads, s.before, s.after, s.base = key_block, entry, pads, before, after, base

        with ExitStack() as c:
            ends = tmp_in(nc, c, "ends", [EP, LISTS, EC], I32)
            next_end = tmp_in(nc, c, "next_end", [EP, 8], I32)
            next_block = tmp_in(nc, c, "next_block", [EP, 1], I32)
            next_f = tmp_in(nc, c, "next_f", [EP, 1], F32)
            key_bf = tmp_in(nc, c, "key_bf", [EP, LISTS, EC], BF16)
            work_i = tmp_in(nc, c, "work_i", [EP, LISTS, EC], I32)
            work_f = tmp_in(nc, c, "work_f", [EP, LISTS, EC], F32)
            hits = tmp_in(nc, c, "hits", [EP, 2, EC], BF16)
            count = tmp_in(nc, c, "count", [EP, LISTS, NB], F32)
            chunks_i = tmp_in(nc, c, "chunks_i", [NB, LISTS], I32)
            chunks_j = tmp_in(nc, c, "chunks_j", [NB, LISTS], I32)
            begun = tmp_in(nc, c, "begun", [NB, LISTS, CHUNKS], BF16)
            ones_b = tmp_in(nc, c, "ones_b", [NB, P], BF16)
            block_f = tmp_in(nc, c, "block_f", [P, LISTS, CHUNKS], F32)
            same = tmp_in(nc, c, "same", [P, CHUNKS], F32)
            loaded = c.enter_context(nc.semaphore("loaded"))
            loaded_next = c.enter_context(nc.semaphore("loaded_next"))
            pads_set = c.enter_context(nc.semaphore("pads_set"))
            last_set = c.enter_context(nc.semaphore("last_set"))
            entries = c.enter_context(nc.semaphore("entries"))
            numbers = c.enter_context(nc.semaphore("numbers"))
            step = c.enter_context(nc.semaphore("step"))
            counted = c.enter_context(nc.semaphore("counted"))
            counts_sum = c.enter_context(nc.semaphore("counts_sum"))
            chunks_known = c.enter_context(nc.semaphore("chunks_known"))
            starts_sum = c.enter_context(nc.semaphore("starts_sum"))
            base_set = c.enter_context(nc.semaphore("base_set"))
            blocks_sum = c.enter_context(nc.semaphore("blocks_sum"))
            sums = c.enter_context(nc.psum_tensor("sums", [NB, 2 * LISTS + 1], F32))
            strays = c.enter_context(nc.psum_tensor("strays", [1, 1], F32))
            block_sum = c.enter_context(nc.psum_tensor("block_sum", [P, PIECES, 512], F32))
            block = c.enter_context(nc.Block())

            @block.sync
            def _(sp):
                for q, e in enumerate((src, dst)):
                    sp.dma_start(ends[:, q, :], e.rearrange("(p c) -> p c", p=EP)).then_inc(loaded, 16)
                sp.wait_ge(last_set, 1)
                sp.dma_start(next_end[0:EP - 1, :], dst.rearrange("(p c) -> p c", p=EP)[1:EP, 0:8]).then_inc(
                    loaded_next, 16)
                sp.wait_ge(pads_set, 1)
                sp.dma_start(k.edges[0], pads[:, :]).then_inc(k.pads_in[0], 16)
                rest = IN_ROWS * P - E
                sp.dma_start(k.in_order[E:E + rest].rearrange("(o n) -> o n", o=1), pads[0:1, 0:rest]).then_inc(
                    in_order_in, 16)
                sp.wait_ge(entries, 1)
                sp.dma_start(k.in_order[0:E].rearrange("(p c) -> p c", p=EP), entry[:, 1, :]).then_inc(
                    in_order_in, 16)

            @block.gpsimd
            def _(pool):
                pool.iota(chunk_no[:, :], pattern=[[1, CHUNKS]], base=0, channel_multiplier=0).then_inc(numbers, 1)

            @block.tensor
            def _(pe):
                pe.wait_ge(counted, LISTS + 1)
                for q in range(LISTS):
                    pe.matmul(sums[:, q:q + 1], count[:, q, :], k.ones[0:EP, 0:1], start=True, stop=True)
                for j in range(2):
                    last = pe.matmul(strays[:, :], disorder[:, j:j + 1], k.ones[0:EP, 0:1], start=(j == 0),
                                     stop=(j == 1))
                last.then_inc(counts_sum, 1)
                pe.wait_ge(chunks_known, 1)
                pe.matmul(sums[:, LISTS:2 * LISTS], before_f[0:NB, 0:NB], chunks_f[:, :], start=True, stop=True)
                pe.matmul(sums[:, 2 * LISTS:], before_f[0:NB, 0:NB], edges_f[:, :],
                          start=True, stop=True).then_inc(starts_sum, 1)
                pe.wait_ge(base_set, 1)
                for q in range(LISTS):
                    for j in range(PIECES):
                        pe.matmul(block_sum[:, j, 0:PIECE], ones_b[:, :], begun[:, q, j * PIECE:(j + 1) * PIECE],
                                  start=True, stop=True).then_inc(blocks_sum, 1)
                    if q + 1 < LISTS:
                        pe.wait_ge(chunks_known, 2)

            @block.vector
            def _(dve):
                done = [0]

                def after_all(ins):
                    ins.then_inc(step, 1)
                    done[0] += 1
                    dve.wait_ge(step, done[0])

                dve.memset(next_end[:, :], N).then_inc(last_set, 1)
                dve.memset(pads[:, :], PAD).then_inc(pads_set, 1)
                dve.memset(ones_b[:, :], 1.0)
                dve.memset(key_block[:, :, EC:COLS], 0.0)
                dve.tensor_scalar(before[:, :], k.ramp[0:EP, 0:EP], k.place[0:EP, 0:1], None, ALU.is_gt)
                dve.tensor_scalar(after[:, :], k.ramp[0:EP, 0:EP], k.place[0:EP, 0:1], None, ALU.is_le)
                dve.tensor_scalar(before_f[:, :], k.ramp[:, :], k.place[:, 0:1], None, ALU.is_gt)
                dve.wait_ge(loaded, 16 * LISTS)
                after_all(dve.tensor_single_scalar(work_i[:, :, :], ends[:, :, :], SHIFT, ALU.logical_shift_right))
                dve.tensor_copy(key_block[:, :, 0:EC], work_i[:, :, :])
                after_all(dve.tensor_copy(key_bf[:, :, :], work_i[:, :, :]))
                after_all(dve.tensor_single_scalar(work_i[:, :, :], ends[:, :, :], P - 1, ALU.bitwise_and))
                after_all(dve.tensor_copy(work_f[:, :, :], work_i[:, :, :]))
                for q in range(LISTS):
                    last = dve.scalar_tensor_tensor(entry[:, q, :], ends[:, 1 - q, :], float(LOC), work_f[:, q, :],
                                                    ALU.mult, ALU.add)
                last.then_inc(entries, 1)
                dve.wait_ge(loaded_next, 16)
                after_all(dve.tensor_single_scalar(next_block[:, :], next_end[:, 0:1], SHIFT, ALU.logical_shift_right))
                after_all(dve.tensor_copy(next_f[:, :], next_block[:, :]))
                dve.tensor_tensor(disorder[:, 1:2], key_block[:, 1, EC - 1:EC], next_f[:, :], ALU.is_gt)
                after_all(dve.tensor_tensor(work_f[:, 0, 0:EC - 1], key_block[:, 1, 0:EC - 1], key_block[:, 1, 1:EC],
                                            ALU.is_gt))
                dve.tensor_reduce(disorder[:, 0:1], work_f[:, 0, 0:EC - 1], X, ALU.add).then_inc(counted, 1)
                for q in range(LISTS):
                    for b in range(NB):
                        ins = dve.tensor_scalar(hits[:, b % 2, :], key_bf[:, q, :], float(b), None,
                                                ALU.is_equal, ALU.add, accum_out=count[:, q, b:b + 1])
                        ins.then_inc(step, 1)
                        done[0] += 1
                        if b:
                            dve.wait_ge(step, done[0] - 1)
                    dve.nop()
                    dve.wait_ge(step, done[0])
                    dve.nop().then_inc(counted, 1)
                dve.wait_ge(counts_sum, 1)
                dve.tensor_copy(disorder_i[:, :], strays[:, :])
                dve.tensor_copy(edges_f[:, :], sums[:, 1:2])
                after_all(dve.tensor_scalar(chunks_i[:, :], sums[:, 0:LISTS], float(P - 1), None, ALU.add))
                after_all(dve.tensor_single_scalar(chunks_j[:, :], chunks_i[:, :], SHIFT, ALU.logical_shift_right))
                dve.tensor_copy(chunks_f[:, :], chunks_j[:, :]).then_inc(chunks_known, 1)
                dve.wait_ge(starts_sum, 1)
                dve.tensor_copy(edges_before[:, :], sums[:, 2 * LISTS:])
                after_all(dve.tensor_copy(start[:, :], sums[:, LISTS:2 * LISTS]))
                dve.wait_ge(numbers, 1)
                for q in range(LISTS):
                    dve.tensor_scalar(base[:, q, :], k.ones[0:NB, 0:EP], start[:, q:q + 1], float(P),
                                      ALU.mult, ALU.mult)
                    last = dve.tensor_scalar(begun[:, q, :], chunk_no[:, :], start[:, q:q + 1], None, ALU.is_ge)
                last.then_inc(base_set, 1)
                for q in range(LISTS):
                    dve.wait_ge(blocks_sum, PIECES * (q + 1))
                    after_all(dve.tensor_scalar(block_f[:, q, :].rearrange("p (a b) -> p a b", a=PIECES),
                                                block_sum[:, :, 0:PIECE], -1.0, None, ALU.add))
                    if q == 0:
                        dve.nop().then_inc(chunks_known, 1)
                    dve.tensor_copy(k.block_row[q][:, :], block_f[0:1, q, :])
                dve.memset(same[:, 0:1], 0.0)
                after_all(dve.tensor_tensor(same[:, 1:CHUNKS], block_f[:, 0, 1:CHUNKS], block_f[:, 0, 0:CHUNKS - 1],
                                            ALU.is_equal))
                after_all(dve.memset(k.carry[:, :, :, :], 0.0))
                for h in range(HEADS):
                    dve.tensor_copy(k.carry[:, :, h, 1:GROUP + 1], same[:, :].rearrange("p (g c) -> p g c", c=GROUP))
                dve.tensor_scalar(k.fresh[:, :], same[:, :], 1.0, -FAR, ALU.subtract, ALU.mult)

        with ExitStack() as c:
            reached = tmp_in(nc, c, "reached", [NB, CHUNKS], F32)
            next_start = tmp_in(nc, c, "next_start", [NB, 1], F32)
            within = tmp_in(nc, c, "within", [NB, CHUNKS], F32)
            limits = tmp_in(nc, c, "limits", [NB, 2], F32)
            own_no = tmp_in(nc, c, "own_no", [P, WINDOWS], I32)
            own_f = tmp_in(nc, c, "own_f", [P, WINDOWS], F32)
            first_f = tmp_in(nc, c, "first_f", [P, WINDOWS], F32)
            first_i = tmp_in(nc, c, "first_i", [P, WINDOWS], I32)
            length = tmp_in(nc, c, "length", [P, WINDOWS], F32)
            row_of = tmp_in(nc, c, "row_of", [P, 2, WINDOWS], I32)
            skip = tmp_in(nc, c, "skip", [P, WINDOWS], I32)
            bit = tmp_in(nc, c, "bit", [P, SHIFT, WINDOWS], I32)
            bit_f = tmp_in(nc, c, "bit_f", [P, SHIFT, WINDOWS], F32)
            raw_w = tmp_in(nc, c, "raw_w", [P, WINDOWS, 2, P], I32)
            window = tmp_in(nc, c, "window", [P, WINDOWS, 2 * P], F32)
            change = tmp_in(nc, c, "change", [P, WINDOWS, 2 * P], F32)
            listed = tmp_in(nc, c, "listed", [P, CHUNKS], I32)
            w_step = c.enter_context(nc.semaphore("w_step"))
            own_set = c.enter_context(nc.semaphore("own_set"))
            within_set = c.enter_context(nc.semaphore("within_set"))
            limits_out = c.enter_context(nc.semaphore("limits_out"))
            rows_known = c.enter_context(nc.semaphore("rows_known"))
            fetched = c.enter_context(nc.semaphore("fetched"))
            masked = c.enter_context(nc.semaphore("masked"))
            turned = c.enter_context(nc.semaphore("turned_w"))
            listed_set = c.enter_context(nc.semaphore("listed_set"))
            list_in = c.enter_context(nc.semaphore("list_in"))
            at_chunk = c.enter_context(nc.psum_tensor("at_chunk", [P, WINDOWS, 2], F32))
            turned_w = c.enter_context(nc.psum_tensor("turned_windows", [P, 4, 512], F32))
            block = c.enter_context(nc.Block())

            @block.gpsimd
            def _(pool):
                pool.iota(own_no[:, :], pattern=[[P * P, WINDOWS]], base=0, channel_multiplier=P).then_inc(own_set, 1)
                bound = pool.to_reg(IN_ROWS - 1)
                pool.wait_ge(in_order_in, 32)
                pool.wait_ge(rows_known, 1)
                for w in range(WINDOWS):
                    for r in range(2):
                        pool.indirect_dma_start(
                            out=raw_w[:, w, r, :], out_offset=None,
                            in_=k.in_order.rearrange("(r e) -> r e", e=P),
                            in_offset=bass.IndirectOffsetOnAxis(ap=row_of[:, r, w:w + 1], axis=0),
                            bounds_check=bound, oob_is_err=False).then_inc(fetched, 16)

            @block.tensor
            def _(pe):
                pe.wait_ge(within_set, 1)
                for w in range(WINDOWS):
                    last = pe.matmul(at_chunk[:, w, :], within[:, w * P:(w + 1) * P], limits[:, :],
                                     start=True, stop=True)
                last.then_inc(limits_out, 1)
                pe.wait_ge(masked, 1)
                for w in range(WINDOWS):
                    last = pe.transpose(turned_w[:, w // 4, (w % 4) * P:(w % 4 + 1) * P], window[:, w, 0:P],
                                        k.ident[:, :])
                last.then_inc(turned, 1)

            @block.vector
            def _(dve):
                done = [0]

                def after_all(ins):
                    ins.then_inc(w_step, 1)
                    done[0] += 1
                    dve.wait_ge(w_step, done[0])

                dve.tensor_tensor(next_start[:, :], start[:, 1:2], chunks_f[:, 1:2], ALU.add)
                dve.scalar_tensor_tensor(limits[:, 0:1], start[:, 1:2], -float(P), edges_before[:, :],
                                         ALU.mult, ALU.add)
                dve.tensor_tensor(limits[:, 1:2], edges_before[:, :], edges_f[:, :], ALU.add)
                after_all(dve.tensor_scalar(reached[:, :], chunk_no[:, :], start[:, 1:2], None, ALU.is_ge))
                dve.scalar_tensor_tensor(within[:, :], chunk_no[:, :], next_start[:, 0:1], reached[:, :],
                                         ALU.is_lt, ALU.mult).then_inc(within_set, 1)
                dve.wait_ge(own_set, 1)
                after_all(dve.tensor_copy(own_f[:, :], own_no[:, :]))
                dve.wait_ge(limits_out, 1)
                firsts, stops = (at_chunk[:, :, j:j + 1].rearrange("p w o -> p (w o)") for j in range(2))
                after_all(dve.tensor_tensor(first_f[:, :], firsts, own_f[:, :], ALU.add))
                after_all(dve.tensor_scalar(first_f[:, :], first_f[:, :], float(E), 0.0, ALU.min, ALU.max))
                dve.tensor_tensor(length[:, :], stops, first_f[:, :], ALU.subtract)
                after_all(dve.tensor_copy(first_i[:, :], first_f[:, :]))
                dve.tensor_single_scalar(skip[:, :], first_i[:, :], P - 1, ALU.bitwise_and)
                after_all(dve.tensor_single_scalar(row_of[:, 0, :], first_i[:, :], SHIFT, ALU.logical_shift_right))
                dve.tensor_scalar(row_of[:, 1, :], row_of[:, 0, :], 1.0, None, ALU.add).then_inc(rows_known, 1)
                for j in range(SHIFT):
                    last = dve.tensor_single_scalar(bit[:, j, :], skip[:, :], 1 << j, ALU.bitwise_and)
                after_all(last)
                dve.tensor_scalar(bit_f[:, :, :], bit[:, :, :], 0.0, None, ALU.is_gt)
                dve.wait_ge(fetched, 16 * 2 * WINDOWS)
                after_all(dve.tensor_copy(window[:, :, :], raw_w[:, :, :, :].rearrange("p w r e -> p w (r e)")))
                have = 2 * P
                for j in reversed(range(SHIFT)):
                    by = 1 << j
                    have -= by
                    after_all(dve.tensor_tensor(change[:, :, 0:have], window[:, :, by:by + have],
                                                window[:, :, 0:have], ALU.subtract))
                    after_all(dve.tensor_tensor(change[:, :, 0:have], change[:, :, 0:have],
                                                bit_f[:, j, :].unsqueeze(2).to_broadcast([P, WINDOWS, have]),
                                                ALU.mult))
                    after_all(dve.tensor_tensor(window[:, :, 0:have], window[:, :, 0:have], change[:, :, 0:have],
                                                ALU.add))
                after_all(dve.tensor_tensor(change[:, :, 0:P], k.ramp[:, :].unsqueeze(1).to_broadcast([P, WINDOWS, P]),
                                            length[:, :].unsqueeze(2).to_broadcast([P, WINDOWS, P]), ALU.is_ge))
                dve.scalar_tensor_tensor(window[:, :, 0:P], change[:, :, 0:P], float(PAD), window[:, :, 0:P],
                                         ALU.mult, ALU.max).then_inc(masked, 1)
                dve.wait_ge(turned, 1)
                dve.tensor_copy(listed[:, :], turned_w[:, :, :].rearrange("p a b -> p (a b)")[:, 0:CHUNKS]).then_inc(
                    listed_set, 1)

            @block.sync
            def _(sp):
                sp.wait_ge(listed_set, 1)
                sp.dma_start(k.edges[1], listed[:, :]).then_inc(list_in, 16)
                sp.wait_ge(list_in, 16)

        scatter(nc, k, s, 0, None)
        scatter(nc, k, s, 1, disorder_i)


def tmp_in(nc, c, name, shape, dt):
    return c.enter_context(nc.sbuf_tensor(name, shape, dt))


def scatter(nc, k, s, q, wanted):
    TURN = 2 * HALF
    assert EC % TURN == 0

    def if_wanted(eng, program):
        if wanted is None:
            program()
            return
        flag = eng.alloc_register(f"disorder_{eng.engine.name}")
        eng.load([flag], wanted[0:1, 0:1])
        with eng.If_ne(flag, 0):
            program()

    with ExitStack() as c:
        def tmp(name, shape, dt):
            return tmp_in(nc, c, f"{name}{q}", shape, dt)

        def sem(name):
            return c.enter_context(nc.semaphore(f"{name}{q}"))

        onehot = tmp("onehot", [EP, HALF, NB], BF16)
        ranked = tmp("ranked", [EP, 2, NB], F32)
        spot_f = tmp("spot_f", [EP, 2, HALF], F32)
        spot_i = tmp("spot_i", [EP, 2, HALF], I32)
        spot_p = tmp("spot_p", [EP, 2, HALF], I32)
        spot_c = tmp("spot_c", [EP, 2, HALF], I32)
        address = tmp("address", [EP, 2, HALF], I32)
        moved = tmp("moved", [EP, 2, HALF], I32)
        hot = sem("hot")
        place_known = sem("place_known")
        rank_sum = sem("rank_sum")
        spots = sem("spots")
        placed = sem("placed")
        scattered = [sem(f"scattered{h}_") for h in range(2)]
        running = c.enter_context(nc.psum_tensor(f"running{q}", [EP, NB], F32))
        block = c.enter_context(nc.Block())

        @block.sync
        def _(sp):
            if wanted is None:
                return

            def program():
                sp.dma_start(k.edges[q], s.pads[:, :]).then_inc(k.pads_in[q], 16)
                sp.wait_ge(k.pads_in[q], 16)

            if_wanted(sp, program)

        @block.gpsimd
        def _(pool):
            due = pool.alloc_register(f"due{q}")

            def program():
                bound = pool.to_reg(P * CHUNKS - 1)
                pool.reg_mov(due, 1)
                pool.wait_ge(k.pads_in[q], 16)
                flat = k.edges[q].rearrange("p (c o) -> (p c) o", o=1)
                with pool.Fori(0, EC // TURN):
                    for h in range(2):
                        pool.wait_ge(spots, due)
                        pool.reg_add(due, due, 1)
                        for j in range(HALF):
                            pool.indirect_dma_start(
                                out=flat, out_offset=bass.IndirectOffsetOnAxis(ap=address[:, h, j:j + 1], axis=0),
                                in_=moved[:, h, j:j + 1], in_offset=None,
                                bounds_check=bound, oob_is_err=False).then_inc(scattered[h], 16)
                for h in range(2):
                    pool.wait_ge(scattered[h], 16 * HALF * (EC // TURN))

            if_wanted(pool, program)

        @block.tensor
        def _(pe):
            def column(g, j):
                if j != 0 or not isinstance(g, int):
                    wait(pe, place_known, g + j)
                    pe.matmul(running[:, :], s.after[:, :], onehot[:, (j - 1) % HALF, :],
                              start=False, stop=True, skip_group_check=True)
                pe.wait_ge(hot, g + j + 1)
                pe.matmul(running[:, :], s.before[:, :], onehot[:, j % HALF, :],
                          start=False, stop=True, skip_group_check=True).then_inc(rank_sum, 1)

            def program():
                pe.matmul(running[:, :], s.base[:, q, :], k.ident[0:NB, 0:NB], start=True, stop=True)
                for j in range(TURN):
                    column(0, j)
                with pe.Fori(1, EC // TURN) as i:
                    for j in range(TURN):
                        column(i * TURN, j)

            if_wanted(pe, program)

        @block.vector
        def _(dve):
            def hot_rows(col, j):
                dve.tensor_scalar(onehot[:, j % HALF, :], k.ramp[0:EP, 0:NB], s.key_block[:, q, ds(col, 1)], None,
                                  ALU.is_equal).then_inc(hot, 1)

            def half(i, h):
                first = isinstance(i, int)
                for j in range(h * HALF, (h + 1) * HALF):
                    col = i * TURN + j
                    dve.wait_ge(rank_sum, col + 1)
                    wait(dve, place_known, col - 1)
                    dve.scalar_tensor_tensor(ranked[:, j % 2, :], k.ramp[0:EP, 0:NB],
                                             s.key_block[:, q, ds(col, 1)], running[:, :], ALU.is_equal, ALU.mult,
                                             accum_out=spot_f[:, h, j % HALF:j % HALF + 1]).then_inc(place_known, 1)
                    hot_rows(col + AHEAD, j + AHEAD)
                dve.wait_ge(place_known, i * TURN + (h + 1) * HALF)
                n = 2 * i + h
                dve.tensor_copy(spot_i[:, h, :], spot_f[:, h, :]).then_inc(placed, 1)
                dve.wait_ge(placed, 3 * n + 1)
                dve.tensor_single_scalar(spot_p[:, h, :], spot_i[:, h, :], P - 1, ALU.bitwise_and)
                dve.tensor_single_scalar(spot_c[:, h, :], spot_i[:, h, :], SHIFT,
                                         ALU.logical_shift_right).then_inc(placed, 1)
                if not first:
                    dve.wait_ge(scattered[h], i * (16 * HALF))
                dve.tensor_copy(moved[:, h, :], s.entry[:, q, ds(i * TURN + h * HALF, HALF)])
                dve.wait_ge(placed, 3 * n + 2)
                dve.scalar_tensor_tensor(address[:, h, :], spot_p[:, h, :], float(CHUNKS), spot_c[:, h, :],
                                         ALU.mult, ALU.add).then_inc(placed, 1)
                dve.wait_ge(placed, 3 * n + 3)
                dve.nop().then_inc(spots, 1)

            def program():
                for j in range(AHEAD):
                    hot_rows(j, j)
                half(0, 0)
                half(0, 1)
                with dve.Fori(1, EC // TURN) as i:
                    half(i, 0)
                    half(i, 1)

            if_wanted(dve, program)


def load_list(nc, k, q):
    with ExitStack() as c:
        raw = c.enter_context(nc.sbuf_tensor(f"raw{q}", [P, CHUNKS], I32))
        part = c.enter_context(nc.sbuf_tensor(f"low_bits{q}", [P, CHUNKS], I32))
        read = c.enter_context(nc.semaphore(f"read{q}"))
        cut = c.enter_context(nc.semaphore(f"cut{q}"))
        block = c.enter_context(nc.Block())

        @block.sync
        def _(sp):
            sp.dma_start(raw[:, :], k.edges[q]).then_inc(read, 16)

        @block.vector
        def _(dve):
            dve.wait_ge(read, 16)
            dve.tensor_single_scalar(k.row[:, :], raw[:, :], 8, ALU.logical_shift_right)
            dve.tensor_single_scalar(part[:, :], raw[:, :], LOC - 1, ALU.bitwise_and).then_inc(cut, 1)
            dve.wait_ge(cut, 1)
            dve.tensor_copy(k.spot[:, :], part[:, :])


def project(nc, k, x, Ww, Wb, a):
    W_EXT = D + 2 * HEADS
    RX = 4
    with ExitStack() as c:
        def tmp(name, shape, dt=F32):
            return c.enter_context(nc.sbuf_tensor(name, shape, dt))

        def sem(name):
            return c.enter_context(nc.semaphore(name))

        w = tmp("w", [P, 2, W_EXT])
        bias = tmp("bias", [P, W_EXT])
        a_all = tmp("a_all", [P, 2 * HD])
        junk = tmp("junk", [P, 12, HD])
        xin = tmp("xin", [P, RX, D])
        xT = tmp("xT", [P, 2, 2, P])
        wh = tmp("wh", [P, RX, W_EXT])
        t_all = tmp("t_all", [P, HEADS, NB])
        empty = tmp("empty", [P, ROWT])
        low = tmp("low", [P, HEADS])
        low_n = tmp("low_n", [P, HEADS])
        low_r = tmp("low_r", [P, HEADS])
        w_in = sem("w_in")
        cleared = sem("cleared")
        w_done = sem("w_done")
        x_in = [sem(f"x_in{r}") for r in range(RX)]
        turned = sem("turned")
        copied = sem("copied")
        product = sem("product")
        rows = sem("rows")
        stored = [sem(f"stored{r}") for r in range(RX)]
        empties = sem("empties")
        lows = sem("lows")
        all_low = sem("all_low")
        pT = c.enter_context(nc.psum_tensor("pT", [P, 2, 512], F32))
        pW = c.enter_context(nc.psum_tensor("pW", [P, 2, 512], F32))
        MAIN = NB - 1 - (NB - 1) % RX
        TAIL = range(MAIN, NB)

        def size(b):
            return LAST if isinstance(b, int) and b == NB - 1 else P

        def rows_of(t, b, n):
            return t[ds(b * P, n), :] if not isinstance(b, int) else t[b * P:b * P + n, :]

        def each(eng, f):
            for r in range(RX):
                f(r, r, 0)
            with eng.Fori(1, MAIN // RX) as i:
                for r in range(RX):
                    f(i * RX + r, r, i)
            for b in TAIL:
                f(b, b % RX, b // RX)

        block = c.enter_context(nc.Block())

        @block.sync
        def _(sp):
            sp.dma_start(w[:, :, 0:D], Ww.rearrange("(k p) n -> p k n", p=P)).then_inc(w_in, 16)
            sp.dma_start(bias[:, 0:D], Wb.rearrange("(o n) -> o n", o=1).to_broadcast([P, D])).then_inc(w_in, 16)
            sp.dma_start(a_all[:, :], a.rearrange("(o n) -> o n", o=1).to_broadcast([P, 2 * HD])).then_inc(w_in, 16)

            def load(b, r, i):
                wait(sp, copied, b - RX + 1)
                sp.dma_start(xin[0:size(b), r, :], rows_of(x, b, size(b))).then_inc(x_in[r], 16)

            each(sp, load)

        @block.scalar
        def _(act):
            def copy(b, r, i):
                act.wait_ge(turned, b + 1)
                wait(act, product, b - 1)
                n = size(b)
                act.activation(xT[:, r % 2, :, 0:n], pT[:, r % 2, 0:2 * P].rearrange("p (a n) -> p a n", a=2)[:, :, 0:n],
                               ACT.Copy).then_inc(copied, 1)

            each(act, copy)
            act.wait_ge(cleared, 1)
            act.dma_start(k.table[N:NB * P, :], empty[0:NB * P - N, :]).then_inc(empties, 16)
            act.wait_ge(empties, 16)

        @block.tensor
        def _(pe):
            def turn(b, r, i):
                pe.wait_ge(x_in[r], i * 16 + 16)
                wait(pe, copied, b - 1)
                n = size(b)
                for j in range(2):
                    last = pe.transpose(pT[:, r % 2, j * P:j * P + n], xin[0:n, r, j * P:(j + 1) * P],
                                        k.ident[0:n, 0:n])
                last.then_inc(turned, 1)

            def multiply(b, r, i):
                pe.wait_ge(copied, b + 1)
                wait(pe, rows, b - 1)
                n = size(b)
                for j in range(2):
                    last = pe.matmul(pW[0:n, r % 2, 0:W_EXT], xT[:, r % 2, j, 0:n], w[:, j, :],
                                     start=(j == 0), stop=(j == 1))
                last.then_inc(product, 1)

            def both(b, r, i):
                turn(b, r, i)
                if not (isinstance(b, int) and b == 0):
                    multiply(b - 1, (r - 1) % RX, i)

            pe.wait_ge(w_done, 1)
            each(pe, both)
            multiply(NB - 1, (NB - 1) % RX, 0)

        @block.gpsimd
        def _(pool):
            def store(b, r, i):
                pool.wait_ge(rows, b + 1)
                pool.dma_start(rows_of(k.table, b, size(b)), wh[0:size(b), r, 0:ROWT]).then_inc(stored[r], 16)

            def store_loop(i):
                for r in range(RX):
                    store(i * RX + r, r, i)

            due = pool.alloc_register("due_rows")
            for r in range(RX):
                store(r, r, 0)
            pool.reg_mov(due, RX + 1)
            with pool.Fori(1, MAIN // RX) as i:
                for r in range(RX):
                    pool.wait_ge(rows, due)
                    pool.reg_add(due, due, 1)
                    pool.dma_start(k.table[ds(i * (RX * P) + r * P, P), :], wh[:, r, 0:ROWT]).then_inc(stored[r], 16)
            for b in TAIL:
                store(b, b % RX, 0)
            pool.wait_ge(lows, 1)
            pool.partition_all_reduce(low_r[:, :], low_n[:, :], P, bass.bass_isa.ReduceOp.max).then_inc(all_low, 1)
            for r in range(RX):
                pool.wait_ge(stored[r], 16 * (len(range(r, NB, RX))))

        @block.vector
        def _(dve):
            dve.memset(empty[:, 0:D], 0.0)
            dve.memset(empty[:, D:ROWT], FAR).then_inc(cleared, 1)
            dve.memset(t_all[:, :, :], -FAR)
            dve.memset(k.s_all[:, :, :], 0.0)
            dve.wait_ge(w_in, 48)
            n = 0
            for part in range(2):
                for h in range(HEADS):
                    col = D + part * HEADS + h
                    av = a_all[:, (1 - part) * HD:(2 - part) * HD]
                    for j in range(3):
                        wv, to = (w[:, j, h * HD:(h + 1) * HD], w[:, j, col:col + 1]) if j < 2 else (
                            bias[:, h * HD:(h + 1) * HD], bias[:, col:col + 1])
                        last = dve.tensor_tensor_reduce(junk[:, n, :], wv, av, 1.0, 0.0, ALU.mult, ALU.add, to)
                        n += 1
            last.then_inc(w_done, 1)
            dve.wait_ge(w_done, 1)

            def finish(b, r, i):
                dve.wait_ge(product, b + 1)
                if not (isinstance(i, int) and i == 0):
                    dve.wait_ge(stored[r], i * 16)
                n = size(b)
                dve.tensor_tensor(wh[0:n, r, :], pW[0:n, r % 2, 0:W_EXT], bias[0:n, :], ALU.add).then_inc(rows, 1)
                dve.wait_ge(rows, b + 1)
                bs = slice(b, b + 1) if isinstance(b, int) else ds(b, 1)
                dve.tensor_copy(t_all[0:n, :, bs], wh[0:n, r, D:ROWT].unsqueeze(2))
                dve.tensor_copy(k.s_all[0:n, bs, :], wh[0:n, r, ROWT:W_EXT].unsqueeze(1))

            each(dve, finish)
            link = [0]

            def after_all(ins):
                link[0] += 1
                ins.then_inc(lows_step, 1)
                dve.wait_ge(lows_step, link[0])

            lows_step = k.link
            after_all(dve.nop())
            after_all(dve.drain())
            after_all(dve.tensor_reduce(low[:, :], t_all[:, :, :], X, ALU.min))
            dve.tensor_scalar(low_n[:, :], low[:, :], -1.0, None, ALU.mult).then_inc(lows, 1)
            dve.wait_ge(all_low, 1)
            after_all(dve.tensor_scalar(k.t_low[:, :], low_r[:, :], -1.0, None, ALU.mult))
            dve.tensor_tensor(k.s_all[:, :, :], k.s_all[:, :, :],
                              k.t_low[:, :].unsqueeze(1).to_broadcast([P, NB, HEADS]), ALU.add)


def slots(i, j):
    return i * RING + j, i + j // RING, j % RING


def gather_rows(pool, k, table, width, table_rows, ready, lead):
    bound = pool.to_reg(table_rows - 1)
    due = pool.alloc_register("due_group" + table.name)

    def gather(r):
        for c in range(GROUP):
            at = r * GROUP + c
            pool.indirect_dma_start(out=k.rows[:, at, 0:width], out_offset=None, in_=table[:, :],
                                    in_offset=bass.IndirectOffsetOnAxis(ap=k.wanted[:, at:at + 1], axis=0),
                                    bounds_check=bound, oob_is_err=False).then_inc(k.gathered[r], 16)

    for r in range(RING):
        pool.wait_ge(ready, max(1, r - lead + 2))
        gather(r)
    pool.reg_mov(due, RING - lead + 2)
    with pool.Fori(1, TURNS):
        for r in range(RING):
            pool.wait_ge(ready, due)
            pool.reg_add(due, due, 1)
            gather(r)


def block_values(eng, regs, k, q, g):
    eng.load(regs, k.block_row[q][0:1, ds(g * GROUP, GROUP)])
    return [eng.snap(r, min_val=0, max_val=NB - 1) for r in regs]


def turns(eng, step):
    for j in range(RING):
        step(0, j, True, False)
    with eng.Fori(1, TURNS - 1) as i:
        for j in range(RING):
            step(i, j, False, False)
    for j in range(RING):
        step(TURNS - 1, j, False, True)


def gat_pass(nc, k):
    LEAD = RING - 2
    with ExitStack() as c_:
        def tmp(name, shape, dt=F32):
            return c_.enter_context(nc.sbuf_tensor(name, shape, dt))

        def sem(name):
            return c_.enter_context(nc.semaphore(name))

        def ps(name, shape):
            return c_.enter_context(nc.psum_tensor(name, shape, F32))

        onehot = tmp("onehot_g", [P, 4, GROUP, P])
        scores = tmp("scores", [P, HEADS, GROUP, P])
        t_edge = tmp("t_edge", [P, 4, GROUP, HEADS])
        hot_node = tmp("hot_node", [P, 2, GROUP, P])
        weighted = tmp("weighted", [P, 2, GROUP, ACC])
        top = tmp("top", [P, 2, HEADS, GROUP + 1])
        running = tmp("running_max", [P, 2, HEADS, GROUP + 1])
        z_node = tmp("z_node", [P, 2, HEADS, GROUP])
        m_before = tmp("m_before", [P, HEADS, GROUP])
        fall = tmp("fall", [P, HEADS, GROUP])
        fall_m = tmp("fall_m", [P, 2, HEADS, GROUP])
        factor = tmp("factor", [P, 4, HEADS, GROUP])
        node = tmp("node", [P, 2, GROUP, 2 * HEADS])
        z_edge = tmp("z_edge", [P, GROUP, HEADS])
        e_edge = tmp("e_edge", [P, GROUP, HEADS])
        power = tmp("power", [P, 2, GROUP, HEADS])

        known = sem("known")
        t_ready = sem("t_ready")
        hot = sem("hot_g")
        scored = [sem(f"scored{h}") for h in range(HEADS)]
        turned = sem("turned_g")
        s_ready = sem("s_ready")
        maxed = sem("maxed")
        scanned = sem("scanned")
        z_ready = sem("z_ready")
        m_ready = sem("m_ready")
        fell = sem("fell")
        fall_ready = sem("fall_ready")
        factor_ready = sem("factor_ready")
        hot_copied = sem("hot_copied")
        q_ready = sem("q_ready")
        z_known = sem("z_known")
        e_known = sem("e_known")
        power_ready = sem("power_ready")
        weights = sem("weights")
        scaled = sem("scaled")
        summed = sem("summed")
        added = sem("added")

        scores_t = ps("scores_t", [P, HEADS * GROUP, P])
        hot_t = ps("hot_t", [P, GROUP, P])
        part = ps("part", [P, GROUP, 512])
        q_edge = ps("q_edge", [P, 2, GROUP, 2 * HEADS])

        def weights_at(s):
            return weighted[:, s, :, :].rearrange("p c (h d) -> p c h d", h=HEADS)[:, :, :, HD:HD + 1]

        block = c_.enter_context(nc.Block())

        @block.gpsimd
        def _(pool):
            gather_rows(pool, k, k.table, ROWT, NB * P, known, LEAD)

        @block.scalar
        def _(act):
            regs = [act.alloc_register(f"act_block{c}") for c in range(GROUP)]

            def node_s(i, j):
                g, _, _ = slots(i, j)
                for c, b in enumerate(block_values(act, regs, k, 0, g)):
                    last = act.activation(node[:, j % 2, c, 0:HEADS],
                                          k.s_all[:, ds(b, 1), :].rearrange("p o h -> p (o h)"), ACT.Copy)
                last.then_inc(s_ready, 1)

            def score(i, j):
                g, _, _ = slots(i, j)
                act.wait_ge(hot, g + 1)
                act.wait_ge(t_ready, g + 1)
                for c in range(GROUP):
                    last = act.activation(scores[:, 1, c, :], onehot[:, j % 4, c, :], ACT.Copy,
                                          scale=t_edge[:, j % 4, c, 1:2])
                last.then_inc(scored[1], 1)

            def weigh(i, j):
                g, _, r = slots(i, j)
                act.wait_ge(power_ready, g + 1)
                act.activation(weights_at(j % 2), power[:, j % 2, :, :].unsqueeze(3), ACT.Exp).then_inc(weights, 1)
                act.wait_ge(weights, g + 1)
                for c in range(GROUP):
                    for h in range(HEADS):
                        o = h * (HD + 1)
                        last = act.activation(weighted[:, j % 2, c, o:o + HD],
                                              k.rows[:, r * GROUP + c, h * HD:(h + 1) * HD], ACT.Copy,
                                              scale=weighted[:, j % 2, c, o + HD:o + HD + 1])
                    last.then_inc(scaled, 1)

            def step(i, j, first, last):
                g, _, _ = slots(i, j)
                act.wait_ge(turned, g + 1)
                act.activation(hot_node[:, j % 2, :, :], hot_t[:, :, :], ACT.Copy).then_inc(hot_copied, 1)
                if not (last and j == RING - 1):
                    score(i, j + 1)
                if not (first and j == 0):
                    weigh(i, j - 1)
                act.wait_ge(fall_ready, g + 1)
                act.activation(factor[:, j % 4, :, :], fall_m[:, j % 2, :, :], ACT.Exp).then_inc(factor_ready, 1)
                if not (last and j == RING - 1):
                    node_s(i, j + 1)

            node_s(0, 0)
            score(0, 0)
            turns(act, step)
            weigh(TURNS - 1, RING - 1)

        @block.tensor
        def _(pe):
            def turn_hot(i, j):
                g, _, _ = slots(i, j)
                pe.wait_ge(hot, g + 1)
                wait(pe, hot_copied, g)
                for c in range(GROUP):
                    pe.transpose(hot_t[:, c, :], onehot[:, j % 4, c, :], k.ident[:, :])

            def turn_scores(i, j, h):
                g, _, _ = slots(i, j)
                pe.wait_ge(scored[h], g + 1)
                if h == 0:
                    wait(pe, maxed, g)
                for c in range(GROUP):
                    last = pe.transpose(scores_t[:, h * GROUP + c, :], scores[:, h, c, :], k.ident[:, :])
                if h == HEADS - 1:
                    last.then_inc(turned, 1)

            def add_up(i, j, c):
                g, _, _ = slots(i, j)
                pe.wait_ge(scaled, g * GROUP + c + 1)
                if not (isinstance(i, int) and g <= 0):
                    pe.wait_ge(added, ((g - 1) * GROUP + c + 1) * HEADS)
                pe.matmul(part[:, c, 0:ACC], onehot[:, j % 4, c, :], weighted[:, j % 2, c, :],
                          start=True, stop=True).then_inc(summed, 1)

            def step(i, j, first, last):
                g, _, _ = slots(i, j)
                has_next = not (last and j == RING - 1)
                has_prev = not (first and j == 0)
                if has_next:
                    turn_hot(i, j + 1)
                    for h in range(HEADS):
                        turn_scores(i, j + 1, h)
                pe.wait_ge(hot_copied, g + 1)
                pe.wait_ge(m_ready, g + 1)
                wait(pe, power_ready, g)
                for c in range(GROUP):
                    mm = pe.matmul(q_edge[:, j % 2, c, :], hot_node[:, j % 2, c, :], node[:, j % 2, c, :],
                                   start=True, stop=True)
                mm.then_inc(q_ready, 1)
                for c in range(GROUP):
                    if has_prev:
                        add_up(i, j - 1, c)

            turn_hot(0, 0)
            for h in range(HEADS):
                turn_scores(0, 0, h)
            turns(pe, step)
            for c in range(GROUP):
                add_up(TURNS - 1, RING - 1, c)

        @block.vector
        def _(dve):
            regs = [dve.alloc_register(f"dve_block{c}") for c in range(GROUP)]

            def edge_t(i, j):
                g, turn, r = slots(i, j)
                dve.wait_ge(k.gathered[r], (k.turns_before + turn + 1) * (16 * GROUP))
                dve.tensor_tensor(t_edge[:, j % 4, :, :], k.rows[:, r * GROUP:(r + 1) * GROUP, D:ROWT],
                                  k.t_low[:, :].unsqueeze(1).to_broadcast([P, GROUP, HEADS]),
                                  ALU.subtract).then_inc(t_ready, 1)

            def edge_hot(i, j):
                g, _, _ = slots(i, j)
                dve.tensor_tensor(onehot[:, j % 4, :, :], k.ramp[:, :].unsqueeze(1).to_broadcast([P, GROUP, P]),
                                  k.spot[:, ds(g * GROUP, GROUP)].unsqueeze(2).to_broadcast([P, GROUP, P]),
                                  ALU.is_equal).then_inc(hot, 1)
                yield
                dve.wait_ge(hot, g + 1)
                dve.wait_ge(t_ready, g + 1)
                dve.tensor_tensor(scores[:, 0, :, :], onehot[:, j % 4, :, :],
                                  t_edge[:, j % 4, :, 0:1].to_broadcast([P, GROUP, P]), ALU.mult).then_inc(scored[0], 1)
                yield

            def node_max(i, j):
                g, _, _ = slots(i, j)
                s = j % 2
                dve.wait_ge(turned, g + 1)
                dve.tensor_reduce(top[:, s, :, 1:GROUP + 1],
                                  scores_t[:, :, :].rearrange("p (h c) e -> p h c e", h=HEADS), X, ALU.max)
                dve.tensor_copy(top[:, s, :, 0:1], running[:, 1 - s, :, GROUP:GROUP + 1]).then_inc(maxed, 1)
                yield
                dve.wait_ge(maxed, g + 1)
                dve.tensor_tensor_scan(running[:, s, :, :].rearrange("p h c -> p (h c)"),
                                       k.carry[:, ds(g, 1), :, :].rearrange("p o h c -> p (o h c)"),
                                       top[:, s, :, :].rearrange("p h c -> p (h c)"), 0.0,
                                       ALU.mult, ALU.max).then_inc(scanned, 1)
                yield
                dve.wait_ge(scanned, g + 1)
                dve.wait_ge(s_ready, g + 1)
                s_here = node[:, s, :, 0:HEADS].rearrange("p c h -> p h c")
                dve.tensor_tensor(z_node[:, 0, :, :], running[:, s, :, 1:GROUP + 1], s_here, ALU.add)
                dve.tensor_tensor(z_node[:, 1, :, :], running[:, s, :, 0:GROUP], s_here, ALU.add).then_inc(z_ready, 1)
                yield
                dve.wait_ge(z_ready, g + 1)
                m_here = node[:, s, :, HEADS:2 * HEADS].rearrange("p c h -> p h c")
                dve.scalar_tensor_tensor(m_here, z_node[:, 0, :, :], SLOPE, z_node[:, 0, :, :], ALU.mult, ALU.max)
                dve.scalar_tensor_tensor(m_before[:, :, :], z_node[:, 1, :, :], SLOPE, z_node[:, 1, :, :],
                                         ALU.mult, ALU.max).then_inc(m_ready, 1)
                yield
                dve.wait_ge(m_ready, g + 1)
                dve.tensor_tensor(fall[:, :, :], m_before[:, :, :], m_here, ALU.subtract).then_inc(fell, 1)
                yield
                dve.wait_ge(fell, g + 1)
                dve.scalar_tensor_tensor(fall_m[:, s, :, :], fall[:, :, :], 0.0,
                                         k.fresh[:, ds(g * GROUP, GROUP)].unsqueeze(1).to_broadcast([P, HEADS, GROUP]),
                                         ALU.min, ALU.add).then_inc(fall_ready, 1)
                yield

            def add_chunk(i, j, c, b):
                g, _, _ = slots(i, j)
                dve.wait_ge(summed, g * GROUP + c + 1)
                for h in range(HEADS):
                    wait(dve, added, (g * GROUP + c) * HEADS + h - 1)
                    mine = k.acc[:, ds(b * ACC + h * (HD + 1), HD + 1)]
                    last = dve.scalar_tensor_tensor(mine, mine, factor[:, j % 4, h, c:c + 1],
                                                    part[:, c, h * (HD + 1):(h + 1) * (HD + 1)], ALU.mult, ALU.add)
                    last.then_inc(added, 1)

            def edge_power(i, j):
                g, _, _ = slots(i, j)
                q_here = q_edge[:, j % 2, :, :]
                dve.wait_ge(q_ready, g + 1)
                dve.tensor_tensor(z_edge[:, :, :], q_here[:, :, 0:HEADS], t_edge[:, j % 4, :, :],
                                  ALU.add).then_inc(z_known, 1)
                yield
                dve.wait_ge(z_known, g + 1)
                dve.scalar_tensor_tensor(e_edge[:, :, :], z_edge[:, :, :], SLOPE, z_edge[:, :, :],
                                         ALU.mult, ALU.max).then_inc(e_known, 1)
                yield
                dve.wait_ge(e_known, g + 1)
                dve.tensor_tensor(power[:, j % 2, :, :], e_edge[:, :, :], q_here[:, :, HEADS:2 * HEADS],
                                  ALU.subtract).then_inc(power_ready, 1)
                yield

            def step(i, j, first, last):
                g, _, _ = slots(i, j)
                has_next = not (last and j == RING - 1)
                adds = not (first and j < 2)
                a_stage = edge_hot(i, j + 1) if has_next else iter(())
                b_stage = node_max(i, j)
                c_stage = edge_power(i, j - 1) if not (first and j == 0) else iter(())
                if has_next:
                    edge_t(i, j + 1)
                next(b_stage)
                if adds:
                    blocks = block_values(dve, regs, k, 0, g - 2)
                for _ in range(3):
                    next(a_stage, None)
                    next(b_stage)
                next(c_stage, None)
                if adds:
                    dve.wait_ge(factor_ready, g - 1)
                for c in range(GROUP):
                    if adds:
                        add_chunk(i, j - 2, c, blocks[c])
                    if c < 2:
                        next(c_stage, None)
                        next(b_stage)
                if not last or j + LEAD < RING:
                    r = (j + LEAD) % RING
                    dve.tensor_copy(k.wanted[:, r * GROUP:(r + 1) * GROUP],
                                    k.row[:, ds((g + LEAD) * GROUP, GROUP)]).then_inc(known, 1)

            dve.memset(k.acc[:, :], 0.0)
            dve.memset(running[:, :, :, :], 0.0)
            dve.tensor_copy(k.wanted[:, 0:LEAD * GROUP], k.row[:, 0:LEAD * GROUP]).then_inc(known, 1)
            edge_t(0, 0)
            for _ in edge_hot(0, 0):
                pass
            turns(dve, step)
            for _ in edge_power(TURNS - 1, RING - 1):
                pass
            for j in range(RING - 2, RING):
                end = block_values(dve, regs, k, 0, GROUPS - RING + j)
                dve.wait_ge(factor_ready, GROUPS - RING + j + 1)
                for c in range(GROUP):
                    add_chunk(TURNS - 1, j, c, end[c])


def sage_pass(nc, k, table, count):
    LEAD = RING
    WIDE = D + 1 if count else D
    tag = int(not count)
    with ExitStack() as c_:
        def sem(name):
            return c_.enter_context(nc.semaphore(name))

        onehot = c_.enter_context(nc.sbuf_tensor(f"onehot_s{tag}", [P, 4, GROUP, P], F32))
        known = sem(f"known_s{tag}")
        hot = sem(f"hot_s{tag}")
        summed = sem(f"summed_s{tag}")
        added = sem(f"added_s{tag}")
        part = c_.enter_context(nc.psum_tensor(f"part_s{tag}", [P, 2, GROUP, 512], F32))
        block = c_.enter_context(nc.Block())

        @block.gpsimd
        def _(pool):
            gather_rows(pool, k, table, D, NB * P, known, LEAD)

        @block.tensor
        def _(pe):
            def step(i, j, first, last):
                g, turn, r = slots(i, j)
                pe.wait_ge(k.gathered[r], (k.turns_before + turn + 1) * (16 * GROUP))
                pe.wait_ge(hot, g + 1)
                wait(pe, added, g * GROUP - GROUP)
                for c in range(GROUP):
                    pe.matmul(part[:, j % 2, c, 0:WIDE], onehot[:, j % 4, c, :],
                              k.rows[:, r * GROUP + c, 0:WIDE], start=True, stop=True).then_inc(summed, 1)

            turns(pe, step)

        @block.vector
        def _(dve):
            regs = [dve.alloc_register(f"dve_block_s{tag}{c}") for c in range(GROUP)]

            def hot_rows(i, j, c):
                g, _, _ = slots(i, j)
                ins = dve.tensor_scalar(onehot[:, j % 4, c, :], k.ramp[:, :], k.spot[:, ds(g * GROUP + c, 1)], None,
                                        ALU.is_equal)
                if c == GROUP - 1:
                    ins.then_inc(hot, 1)

            def step(i, j, first, last):
                g, _, _ = slots(i, j)
                blocks = block_values(dve, regs, k, 1, g)
                for c in range(GROUP):
                    dve.wait_ge(summed, g * GROUP + c + 1)
                    wait(dve, added, g * GROUP + c)
                    mine = k.acc[:, ds(blocks[c] * ACC, WIDE)]
                    dve.tensor_tensor(mine, mine, part[:, j % 2, c, 0:WIDE], ALU.add).then_inc(added, 1)
                    if not (last and j >= RING - 2):
                        hot_rows(i, j + 2, c)
                if not last:
                    r = j % RING
                    dve.tensor_copy(k.wanted[:, r * GROUP:(r + 1) * GROUP],
                                    k.row[:, ds((g + LEAD) * GROUP, GROUP)]).then_inc(known, 1)

            dve.memset(k.acc[:, :], 0.0)
            if count:
                dve.memset(k.rows[:, :, D:D + 1], 1.0)
            dve.nop()
            dve.tensor_copy(k.wanted[:, 0:LEAD * GROUP], k.row[:, 0:LEAD * GROUP]).then_inc(known, 1)
            for j in range(2):
                for c in range(GROUP):
                    hot_rows(0, j, c)
            turns(dve, step)


UNIT = 7
UNITS = NB // UNIT
assert UNITS * UNIT == NB and UNITS % 2 == 0


def unit_rows(table, u):
    rows = table[ds(u * (UNIT * P), UNIT * P), :] if not isinstance(u, int) else table[u * UNIT * P:(u + 1) * UNIT * P, :]
    return rows.rearrange("(b p) d -> p b d", p=P)


def move_unit(eng, on_chip, table, u, sem, load):
    whole = UNIT - 1
    first = u * (UNIT * P)
    last_rows = LAST if isinstance(u, int) and u == UNITS - 1 else P

    def rows(start, n):
        return table[start:start + n, :] if isinstance(start, int) else table[ds(start, n), :]

    for chip, dram in ((on_chip[:, 0:whole, :], rows(first, whole * P).rearrange("(b p) d -> p b d", p=P)),
                       (on_chip[0:last_rows, whole, :], rows(first + whole * P, last_rows))):
        eng.dma_start(*((chip, dram) if load else (dram, chip))).then_inc(sem, 16)


def unit_turns(eng, f):
    for h in range(2):
        f(h, h, 0)
    with eng.Fori(1, UNITS // 2 - 1) as i:
        for h in range(2):
            f(i * 2 + h, h, i)
    for h in range(2):
        f(UNITS - 2 + h, h, UNITS // 2 - 1)


def gat_end(nc, k, x):
    with ExitStack() as c:
        def tmp(name, shape, dt=F32):
            return c.enter_context(nc.sbuf_tensor(name, shape, dt))

        def sem(name):
            return c.enter_context(nc.semaphore(name))

        xin = tmp("xin_e", [P, 2, UNIT, D])
        own = tmp("own", [P, 2, UNIT, D])
        total = tmp("total", [P, 2, UNIT, D])
        weight = tmp("weight", [P, NB, HEADS])
        alone = tmp("alone", [P, NB, HEADS])
        stats = tmp("stats", [P, UNIT, 6])
        mean = tmp("mean", [P, UNIT, 2])
        spread = tmp("spread", [P, UNIT])
        eps = tmp("eps", [P, 1])
        x_in = [sem(f"x_in_e{h}") for h in range(2)]
        own_in = [sem(f"own_in{h}") for h in range(2)]
        tick = sem("tick")
        cleared = sem("cleared_e")
        var_ready = sem("var_ready")
        root_ready = sem("root_ready")
        normed = sem("normed")
        stored = [sem(f"stored_e{h}") for h in range(2)]
        block = c.enter_context(nc.Block())

        @block.sync
        def _(sp):
            def load(u, h, i):
                if h == 0 and isinstance(u, int) and u == 0:
                    sp.wait_ge(cleared, 1)
                wait(sp, normed, u - 1)
                move_unit(sp, xin[:, h, :, :], x, u, x_in[h], True)
                sp.dma_start(own[:, h, :, :], unit_rows(k.table, u)[:, :, 0:D]).then_inc(own_in[h], 16)

            unit_turns(sp, load)

        @block.scalar
        def _(act):
            def store(u, h, i):
                act.wait_ge(var_ready, u + 1)
                act.activation(spread[:, :], mean[:, :, 1:2].rearrange("p u o -> p (u o)"), ACT.Sqrt,
                               bias=eps[:, 0:1]).then_inc(root_ready, 1)
                act.wait_ge(normed, u + 1)
                act.dma_start(unit_rows(k.x1, u), total[:, h, :, :]).then_inc(stored[h], 16)

            unit_turns(act, store)
            for h in range(2):
                act.wait_ge(stored[h], 16 * (UNITS // 2))

        @block.vector
        def _(dve):
            dve.memset(eps[:, :], EPS)
            dve.memset(xin[:, :, UNIT - 1, :], 0.0).then_inc(cleared, 1)
            sums = k.acc[:, :].rearrange("p (b h d) -> p b h d", b=NB, h=HEADS)
            total_w = sums[:, :, :, HD:HD + 1].rearrange("p b h o -> p b (h o)")
            dve.tensor_scalar(alone[:, :, :], total_w, 0.0, None, ALU.is_equal)
            dve.tensor_scalar(weight[:, :, :], total_w, 1e-30, None, ALU.max).then_inc(tick, 1)
            dve.wait_ge(tick, 1)
            dve.reciprocal(weight[:, :, :], weight[:, :, :]).then_inc(tick, 1)
            dve.wait_ge(tick, 2)
            PER = 5

            def finish(u, h, i):
                n = u * PER + 2

                def stage(s):
                    dve.wait_ge(tick, n + s)

                dve.wait_ge(x_in[h], (i + 1) * 32)
                if not (isinstance(i, int) and i == 0):
                    dve.wait_ge(stored[h], i * 16)
                for b in range(UNIT):
                    for hd in range(HEADS):
                        at = u * UNIT + b
                        cut = slice(hd * HD, (hd + 1) * HD)
                        last = dve.scalar_tensor_tensor(
                            total[:, h, b, cut], k.acc[:, ds(at * ACC + hd * (HD + 1), HD)],
                            weight[:, ds(at, 1), hd:hd + 1].rearrange("p o h -> p (o h)"), xin[:, h, b, cut],
                            ALU.mult, ALU.add)
                last.then_inc(tick, 1)
                stage(1)
                dve.wait_ge(own_in[h], (i + 1) * 16)
                for b in range(UNIT):
                    for hd in range(HEADS):
                        cut = slice(hd * HD, (hd + 1) * HD)
                        last = dve.scalar_tensor_tensor(
                            total[:, h, b, cut], own[:, h, b, cut],
                            alone[:, ds(u * UNIT + b, 1), hd:hd + 1].rearrange("p o h -> p (o h)"),
                            total[:, h, b, cut], ALU.mult, ALU.add)
                last.then_inc(tick, 1)
                stage(2)
                for b in range(UNIT):
                    last = dve.bn_stats(stats[:, b, :], total[:, h, b, :])
                last.then_inc(tick, 1)
                stage(3)
                dve.nop().then_inc(k.link, 1)
                for b in range(UNIT):
                    last = dve.bn_aggr(mean[:, b, :], stats[:, b, :])
                last.then_inc(var_ready, 1)
                dve.wait_ge(root_ready, u + 1)
                dve.wait_ge(var_ready, u + 1)
                dve.reciprocal(spread[:, :], spread[:, :]).then_inc(tick, 1)
                stage(4)
                for b in range(UNIT):
                    last = dve.tensor_scalar(total[:, h, b, :], total[:, h, b, :], mean[:, b, 0:1],
                                             spread[:, b:b + 1], ALU.subtract, ALU.mult)
                last.then_inc(normed, 1)
                dve.wait_ge(normed, u + 1)
                dve.nop().then_inc(tick, 1)

            unit_turns(dve, finish)


def sage_end(nc, k, table, Wl, bl, Wr, out, final):
    with ExitStack() as c:
        def tmp(name, shape, dt=F32):
            return c.enter_context(nc.sbuf_tensor(name, shape, dt))

        def sem(name):
            return c.enter_context(nc.semaphore(name))

        tag = "f" if final else "h"
        wl = tmp("wl" + tag, [P, 2, D])
        wr = tmp("wr" + tag, [P, 2, D])
        bias = tmp("bias" + tag, [P, D])
        rows = tmp("rows_e" + tag, [P, 2, UNIT, D])
        first = tmp("first" + tag, [P, 2, UNIT, D]) if final else None
        result = tmp("result" + tag, [P, 2, UNIT, D])
        average = tmp("average" + tag, [P, 4, D])
        turned_sb = tmp("turned_sb" + tag, [P, 2, 4, P])
        biased = tmp("biased" + tag, [P, 2, D])
        stats = tmp("stats" + tag, [P, UNIT, 6])
        mean = tmp("mean" + tag, [P, UNIT, 2])
        spread = tmp("spread" + tag, [P, UNIT])
        eps = tmp("eps" + tag, [P, 1])
        w_in = sem("w_in" + tag)
        rows_in = [sem(f"rows_in{tag}{h}") for h in range(2)]
        first_in = [sem(f"first_in{tag}{h}") for h in range(2)]
        setup = sem("setup" + tag)
        averaged = sem("averaged" + tag)
        turned = sem("turned" + tag)
        copied = sem("copied" + tag)
        product = sem("product" + tag)
        biased_ready = sem("biased_ready" + tag)
        tick = sem("tick" + tag)
        var_ready = sem("var_ready" + tag)
        root_ready = sem("root_ready" + tag)
        unit_done = sem("unit_done" + tag)
        stored = [sem(f"stored{tag}{h}") for h in range(2)]
        pT = c.enter_context(nc.psum_tensor("pT" + tag, [P, 2, 4, P], F32))
        pO = c.enter_context(nc.psum_tensor("pO" + tag, [P, 2, 512], F32))
        block = c.enter_context(nc.Block())

        @block.sync
        def _(sp):
            for t, w in ((wl, Wl), (wr, Wr)):
                sp.dma_start(t[:, :, :], w.rearrange("(j p) n -> p j n", p=P)).then_inc(w_in, 16)
            sp.dma_start(bias[:, :], bl.rearrange("(o n) -> o n", o=1).to_broadcast([P, D])).then_inc(w_in, 16)

            def load(u, h, i):
                wait(sp, unit_done, u - 1)
                sp.dma_start(rows[:, h, :, :], unit_rows(table, u)).then_inc(rows_in[h], 16)
                if final:
                    sp.dma_start(first[:, h, :, :], unit_rows(k.x1, u)).then_inc(first_in[h], 16)

            unit_turns(sp, load)

        @block.tensor
        def _(pe):
            def turn(u, h, i, b):
                n = u * UNIT + b
                s = (h * UNIT + b)
                if b == 0:
                    pe.wait_ge(rows_in[h], (i + 1) * 16)
                pe.wait_ge(averaged, n + 1)
                wait(pe, copied, n - 1)
                for j in range(2):
                    pe.transpose(pT[:, s % 2, j, :], average[:, s % 2, j * P:(j + 1) * P],
                                 k.ident[:, :])
                for j in range(2):
                    last = pe.transpose(pT[:, s % 2, 2 + j, :], rows[:, h, b, j * P:(j + 1) * P], k.ident[:, :])
                last.then_inc(turned, 1)

            def multiply(u, h, b):
                n = u * UNIT + b
                s = (h * UNIT + b) % 2
                pe.wait_ge(copied, n + 1)
                wait(pe, biased_ready, n - 1)
                for j in range(4):
                    w = (wl, wr)[j // 2]
                    last = pe.matmul(pO[:, s, 0:D], turned_sb[:, s, j, :], w[:, j % 2, :], start=(j == 0),
                                     stop=(j == 3))
                last.then_inc(product, 1)

            def unit(u, h, i):
                for b in range(UNIT):
                    turn(u, h, i, b)
                    if not (isinstance(u, int) and u == 0 and b == 0):
                        if b:
                            multiply(u, h, b - 1)
                        else:
                            multiply(u - 1, 1 - h, UNIT - 1)

            pe.wait_ge(w_in, 48)
            unit_turns(pe, unit)
            multiply(UNITS - 1, 1, UNIT - 1)

        @block.scalar
        def _(act):
            act.wait_ge(setup, 1)

            def unit(u, h, i):
                for b in range(UNIT):
                    n = u * UNIT + b
                    s = (h * UNIT + b) % 2
                    act.wait_ge(turned, n + 1)
                    wait(act, product, n - 1)
                    act.activation(turned_sb[:, s, :, :], pT[:, s, :, :], ACT.Copy).then_inc(copied, 1)
                    if not final and not (isinstance(u, int) and u == 0 and b == 0):
                        rectify(u, h, i, b - 1)
                if final:
                    root(u)

            def rectify(u, h, i, b):
                if b < 0:
                    u, h, i, b = u - 1, 1 - h, (i if h == 1 else i - 1), UNIT - 1
                n = u * UNIT + b
                s = (h * UNIT + b) % 2
                if b == 0 and not (isinstance(i, int) and i == 0):
                    act.wait_ge(stored[h], i * 16)
                act.wait_ge(biased_ready, n + 1)
                ins = act.activation(result[:, h, b, :], biased[:, s, :], ACT.Relu)
                ins.then_inc(tick, 1)
                if b == UNIT - 1:
                    act.wait_ge(tick, n + 1)
                    act.nop().then_inc(unit_done, 1)

            def root(u):
                act.wait_ge(var_ready, u + 1)
                act.activation(spread[:, :], mean[:, :, 1:2].rearrange("p u o -> p (u o)"), ACT.Sqrt,
                               bias=eps[:, 0:1]).then_inc(root_ready, 1)

            unit_turns(act, unit)
            if not final:
                rectify(UNITS - 1, 1, UNITS // 2 - 1, UNIT - 1)

        @block.gpsimd
        def _(pool):
            due = pool.alloc_register("due_unit" + tag)
            pool.reg_mov(due, 3)

            def store(u, h, i):
                if isinstance(u, int):
                    pool.wait_ge(unit_done, u + 1)
                else:
                    pool.wait_ge(unit_done, due)
                    pool.reg_add(due, due, 1)
                if final:
                    move_unit(pool, result[:, h, :, :], out, u, stored[h], False)
                else:
                    pool.dma_start(unit_rows(out, u), result[:, h, :, :]).then_inc(stored[h], 16)

            unit_turns(pool, store)
            for h in range(2):
                pool.wait_ge(stored[h], (32 if final else 16) * (UNITS // 2))

        @block.vector
        def _(dve):
            dve.memset(eps[:, :], EPS).then_inc(setup, 1)
            if not final:
                counts = k.acc[:, :].rearrange("p (b d) -> p b d", b=NB)[:, :, D:D + 1].rearrange("p b o -> p (b o)")
                dve.tensor_scalar(k.share[:, :], counts, 1.0, None, ALU.max).then_inc(setup, 1)
                dve.wait_ge(setup, 2)
                dve.reciprocal(k.share[:, :], k.share[:, :]).then_inc(setup, 1)
                dve.wait_ge(setup, 3)

            def average_of(u, h, b):
                n = u * UNIT + b
                s = (h * UNIT + b) % 2
                wait(dve, turned, n - 1)
                dve.tensor_scalar(average[:, s, :], k.acc[:, ds(n * ACC, D)], k.share[:, ds(n, 1)], None,
                                  ALU.mult).then_inc(averaged, 1)

            dve.wait_ge(w_in, 48)

            def unit(u, h, i):
                if final:
                    dve.wait_ge(first_in[h], (i + 1) * 16)
                    if not (isinstance(i, int) and i == 0):
                        dve.wait_ge(stored[h], i * 32)
                for b in range(UNIT):
                    n = u * UNIT + b
                    s = (h * UNIT + b) % 2
                    if b < UNIT - 1:
                        average_of(u, h, b + 1)
                    elif not (isinstance(u, int) and u == UNITS - 1):
                        average_of(u + 1, 1 - h, 0)
                    dve.wait_ge(product, n + 1)
                    if final:
                        wait(dve, biased_ready, n)
                    dve.tensor_tensor(biased[:, s, :], pO[:, s, 0:D], bias[:, :], ALU.add).then_inc(biased_ready, 1)
                    if final:
                        dve.wait_ge(biased_ready, n + 1)
                        dve.tensor_tensor(result[:, h, b, :], biased[:, s, :], first[:, h, b, :],
                                          ALU.add).then_inc(tick, 1)
                if not final:
                    return
                t = u * (UNIT + 2)
                dve.wait_ge(tick, t + UNIT)
                for b in range(UNIT):
                    last = dve.bn_stats(stats[:, b, :], result[:, h, b, :])
                last.then_inc(tick, 1)
                dve.wait_ge(tick, t + UNIT + 1)
                dve.nop().then_inc(k.link, 1)
                for b in range(UNIT):
                    last = dve.bn_aggr(mean[:, b, :], stats[:, b, :])
                last.then_inc(var_ready, 1)
                dve.wait_ge(root_ready, u + 1)
                dve.reciprocal(spread[:, :], spread[:, :]).then_inc(tick, 1)
                dve.wait_ge(tick, t + UNIT + 2)
                for b in range(UNIT):
                    last = dve.tensor_scalar(result[:, h, b, :], result[:, h, b, :], mean[:, b, 0:1],
                                             spread[:, b:b + 1], ALU.subtract, ALU.mult)
                last.then_inc(unit_done, 1)

            average_of(0, 0, 0)
            unit_turns(dve, unit)


def build(nc, x, src, dst, Ww, Wb, a, Wl1, b1, Wr1, Wl2, b2, Wr2, out, debug=()):
    with ExitStack() as ctx:
        k = Kernel()

        def sb(name, shape, dt):
            return ctx.enter_context(nc.sbuf_tensor(name, shape, dt))

        def dram(name, shape, dt):
            kind = "ExternalOutput" if name in debug else "Internal"
            return nc.dram_tensor(name, shape, dt, kind=kind).ap()

        k.sb = sb
        k.pads_in = [ctx.enter_context(nc.semaphore(f"pads_in{q}")) for q in range(LISTS)]
        k.link = ctx.enter_context(nc.semaphore("link"))
        k.gathered = [ctx.enter_context(nc.semaphore(f"gathered{r}")) for r in range(RING)]
        k.turns_before = 0
        k.edges = [dram(f"edges{q}", (P, CHUNKS), I32) for q in range(LISTS)]
        k.in_order = dram("in_order", ((E // P + 2) * P,), I32)
        k.table = dram("table", (NB * P, ROWT), F32)
        k.x1 = dram("x1", (NB * P, D), F32)
        k.hidden = dram("hidden", (NB * P, D), F32)
        k.carry = sb("carry", [P, GROUPS, HEADS, GROUP + 1], BF16)
        k.fresh = sb("fresh", [P, CHUNKS], F32)
        k.s_all = sb("s_all", [P, NB, HEADS], F32)
        k.t_low = sb("t_low", [P, HEADS], F32)
        constants(nc, k, ctx)
        sort_edges(nc, k, src, dst)
        project(nc, k, x, Ww, Wb, a)
        k.acc = sb("acc", [P, NB * ACC], F32)
        k.share = sb("share", [P, NB], F32)
        k.row = sb("row", [P, CHUNKS], I32)
        k.spot = sb("spot", [P, CHUNKS], F32)
        load_list(nc, k, 0)
        with ExitStack() as c:
            k.rows = c.enter_context(nc.sbuf_tensor("rows", [P, GROUP * RING, ROWT], F32))
            k.wanted = c.enter_context(nc.sbuf_tensor("wanted", [P, GROUP * RING], I32))
            gat_pass(nc, k)
            k.turns_before += TURNS
        gat_end(nc, k, x)
        load_list(nc, k, 1)
        for n, (table, Wl, bl, Wr, to) in enumerate(((k.x1, Wl1, b1, Wr1, k.hidden), (k.hidden, Wl2, b2, Wr2, out))):
            with ExitStack() as c:
                k.rows = c.enter_context(nc.sbuf_tensor(f"rows_s{n}", [P, GROUP * RING, D + 1], F32))
                k.wanted = c.enter_context(nc.sbuf_tensor(f"wanted_s{n}", [P, GROUP * RING], I32))
                sage_pass(nc, k, table, n == 0)
                k.turns_before += TURNS
            sage_end(nc, k, table, Wl, bl, Wr, to, n == 1)


_INS = ["x", "src", "dst", "L0_gnn_W_w", "L0_gnn_W_b", "L0_gnn_a", "L1_gnn_W_l1", "L1_gnn_b1", "L1_gnn_W_r1",
        "L1_gnn_W_l2", "L1_gnn_b2", "L1_gnn_W_r2"]


def kernel(**inputs):
    import concourse.bacc as bacc
    import numpy as np
    from concourse.bass_utils import run_bass_kernel_spmd as run

    nc = bacc.Bacc("TRN2", target_bir_lowering=False, num_devices=1)
    arrays, args = {}, []
    for name in _INS:
        array = np.ascontiguousarray(inputs[name])
        arrays[f"in_{name}"] = array
        args.append(nc.dram_tensor(f"in_{name}", array.shape, mybir.dt.from_np(array.dtype),
                                   kind="ExternalInput").ap())
    out = nc.dram_tensor("out", (N, D), F32, kind="ExternalOutput").ap()
    build(nc, *args, out)
    got = run(nc, [arrays], core_ids=[0])
    return got.results[0]["out"]
```

```python
from contextlib import ExitStack

import concourse.bass as bass
from concourse import mybir

F32 = mybir.dt.float32
BF16 = mybir.dt.bfloat16
I32 = mybir.dt.int32
ALU = mybir.AluOpType
ACT = mybir.ActivationFunctionType
X = mybir.AxisListType.X
ds = bass.ds

P = 128
N = 12500
D = 256
HEADS = 2
HD = D // HEADS
E = 200000
NB = -(-N // P)
LAST = N - (NB - 1) * P
EP = 125
EC = E // EP
LISTS = 2
GROUP = 4
RING = 8
BODY = GROUP * RING
PAIR = 2
MULTIPLE = (PAIR, 1)
PAIRS = GROUP // PAIR
CHUNKS = [-(-((E + NB * (P * u - 1)) // P) // BODY) * BODY for u in MULTIPLE]
MOST = max(CHUNKS)
GROUPS = [c // GROUP for c in CHUNKS]
TURNS = [g // RING for g in GROUPS]
SHIFT = 7
LOC = 256
PAD = N * LOC + 200
FAR = -1.0e30
ROWT = D + HEADS
ACC = HEADS * (HD + 1)
LOW_BITS = 3
LOWS = 1 << LOW_BITS
HIGHS = -(-NB // LOWS)
BATCH = 8
assert HIGHS * BATCH <= P and EC % (BATCH * BATCH) == 0
HALF = 8
AHEAD = HALF - 1
COLS = EC + HALF
EPS = 1e-5
SLOPE = 0.2


def wait(eng, sem, value):
    if isinstance(value, int) and value <= 0:
        return
    eng.wait_ge(sem, value)


def per_head(ap):
    return ap.rearrange("p (h d) -> p h d", h=HEADS)


class Kernel:
    pass


def constants(nc, k, ctx):
    sb = k.sb
    k.ramp = sb("ramp", [P, P], F32)
    k.place = sb("place", [P, 1], F32)
    k.ident = sb("ident", [P, P], F32)
    k.ones = sb("ones", [P, P], F32)
    with ExitStack() as c:
        ramp_i = c.enter_context(nc.sbuf_tensor("ramp_i", [P, P], I32))
        place_i = c.enter_context(nc.sbuf_tensor("place_i", [P, 1], I32))
        iotas = c.enter_context(nc.semaphore("iotas"))
        ramps = c.enter_context(nc.semaphore("ramps"))
        block = c.enter_context(nc.Block())

        @block.gpsimd
        def _(pool):
            pool.iota(ramp_i[:, :], pattern=[[1, P]], base=0, channel_multiplier=0).then_inc(iotas, 1)
            pool.iota(place_i[:, :], pattern=[[1, 1]], base=0, channel_multiplier=1).then_inc(iotas, 1)

        @block.vector
        def _(dve):
            dve.memset(k.ones[:, :], 1.0)
            dve.wait_ge(iotas, 2)
            dve.tensor_copy(k.ramp[:, :], ramp_i[:, :]).then_inc(ramps, 1)
            dve.tensor_copy(k.place[:, :], place_i[:, :]).then_inc(ramps, 1)
            dve.wait_ge(ramps, 2)
            dve.tensor_scalar(k.ident[:, :], k.ramp[:, :], k.place[:, 0:1], None, ALU.is_equal)


def sort_edges(nc, k, src, dst):
    PIECES = 4
    WINDOWS = CHUNKS[1] // P
    assert WINDOWS * P == CHUNKS[1] and all(n % PIECES == 0 for n in CHUNKS)
    IN_ROWS = E // P + 2
    sb = k.sb
    k.block_row = [sb(f"block_row{q}", [1, CHUNKS[q] // MULTIPLE[q]], I32) for q in range(LISTS)]
    with ExitStack() as c:
        def tmp(name, shape, dt):
            return c.enter_context(nc.sbuf_tensor(name, shape, dt))

        def sem(name):
            return c.enter_context(nc.semaphore(name))

        key_block = tmp("key_block", [EP, LISTS, COLS], F32)
        entry = tmp("entry", [EP, LISTS, EC], I32)
        pads = tmp("pads", [P, MOST], I32)
        before = tmp("before", [EP, EP], BF16)
        after = tmp("after", [EP, EP], BF16)
        before_f = tmp("before_f", [P, P], F32)
        chunks_f = tmp("chunks_f", [NB, LISTS], F32)
        start = tmp("start", [NB, LISTS], F32)
        base = tmp("base", [NB, LISTS, EP], F32)
        chunk_no = tmp("chunk_no", [NB, MOST], I32)
        edges_f = tmp("edges_f", [NB, 1], F32)
        edges_before = tmp("edges_before", [NB, 1], F32)
        disorder = tmp("disorder", [EP, 2], F32)
        disorder_i = tmp("disorder_i", [1, 1], I32)
        in_order_in = sem("in_order_in")
        s = Kernel()
        s.key_block, s.entry, s.pads, s.before, s.after, s.base = key_block, entry, pads, before, after, base

        with ExitStack() as c:
            ends = tmp_in(nc, c, "ends", [EP, LISTS, EC], I32)
            next_end = tmp_in(nc, c, "next_end", [EP, 8], I32)
            next_block = tmp_in(nc, c, "next_block", [EP, 1], I32)
            next_f = tmp_in(nc, c, "next_f", [EP, 1], F32)
            work_i = tmp_in(nc, c, "work_i", [EP, LISTS, EC], I32)
            work_f = tmp_in(nc, c, "work_f", [EP, LISTS, EC], F32)
            high_i = tmp_in(nc, c, "high_i", [EP, EC], I32)
            high_b = tmp_in(nc, c, "high_b", [EP, EC], BF16)
            low_b = tmp_in(nc, c, "low_b", [EP, EC], BF16)
            high_hot = tmp_in(nc, c, "high_hot", [EP, EC // BATCH, HIGHS, BATCH], BF16)
            low_hot = tmp_in(nc, c, "low_hot", [EP, EC // BATCH, LOWS, BATCH], BF16)
            row_i = tmp_in(nc, c, "row_i", [HIGHS * BATCH, 3], I32)
            row_f = tmp_in(nc, c, "row_f", [HIGHS * BATCH, 3], F32)
            block_i = tmp_in(nc, c, "block_i", [P, 2, P], I32)
            block_high = tmp_in(nc, c, "block_high", [P, P], F32)
            to_block = tmp_in(nc, c, "to_block", [HIGHS * BATCH, NB], F32)
            low_i = tmp_in(nc, c, "low_i", [P, 1], I32)
            low_f = tmp_in(nc, c, "low_f", [P, 1], F32)
            same_column = tmp_in(nc, c, "same_column", [HIGHS * BATCH, BATCH], F32)
            own_pairs = tmp_in(nc, c, "own_pairs", [HIGHS * BATCH, LISTS, LOWS, BATCH], F32)
            pairs = tmp_in(nc, c, "pairs", [HIGHS * BATCH, LISTS, LOWS], F32)
            is_low = tmp_in(nc, c, "is_low", [NB, LOWS], F32)
            counts = tmp_in(nc, c, "counts", [NB, LISTS, LOWS], F32)
            number = tmp_in(nc, c, "number", [NB, LISTS], F32)
            chunks_i = tmp_in(nc, c, "chunks_i", [NB, LISTS], I32)
            chunks_j = tmp_in(nc, c, "chunks_j", [NB, LISTS], I32)
            begun = tmp_in(nc, c, "begun", [NB, LISTS, MOST], BF16)
            ones_b = tmp_in(nc, c, "ones_b", [NB, P], BF16)
            block_f = tmp_in(nc, c, "block_f", [P, LISTS, MOST], F32)
            same = tmp_in(nc, c, "same", [P, CHUNKS[0] // PAIR], F32)
            loaded = c.enter_context(nc.semaphore("loaded"))
            loaded_next = c.enter_context(nc.semaphore("loaded_next"))
            pads_set = c.enter_context(nc.semaphore("pads_set"))
            last_set = c.enter_context(nc.semaphore("last_set"))
            entries = c.enter_context(nc.semaphore("entries"))
            numbers = c.enter_context(nc.semaphore("numbers"))
            step = c.enter_context(nc.semaphore("step"))
            counted = c.enter_context(nc.semaphore("counted"))
            counts_sum = c.enter_context(nc.semaphore("counts_sum"))
            chunks_known = c.enter_context(nc.semaphore("chunks_known"))
            starts_sum = c.enter_context(nc.semaphore("starts_sum"))
            base_set = c.enter_context(nc.semaphore("base_set"))
            blocks_sum = c.enter_context(nc.semaphore("blocks_sum"))
            hots = c.enter_context(nc.semaphore("hots"))
            pairs_sum = c.enter_context(nc.semaphore("pairs_sum"))
            pairs_known = c.enter_context(nc.semaphore("pairs_known"))
            sums = c.enter_context(nc.psum_tensor("sums", [NB, LISTS + 1], F32))
            pair_sum = c.enter_context(nc.psum_tensor("pair_sum", [HIGHS * BATCH, LISTS, LOWS * BATCH], F32))
            by_block = c.enter_context(nc.psum_tensor("by_block", [NB, LISTS, LOWS], F32))
            strays = c.enter_context(nc.psum_tensor("strays", [1, 1], F32))
            block_sum = c.enter_context(nc.psum_tensor("block_sum", [P, PIECES, 512], F32))
            block = c.enter_context(nc.Block())

            @block.sync
            def _(sp):
                for q, e in enumerate((src, dst)):
                    sp.dma_start(ends[:, q, :], e.rearrange("(p c) -> p c", p=EP)).then_inc(loaded, 16)
                sp.wait_ge(last_set, 1)
                sp.dma_start(next_end[0:EP - 1, :], dst.rearrange("(p c) -> p c", p=EP)[1:EP, 0:8]).then_inc(
                    loaded_next, 16)
                sp.wait_ge(pads_set, 1)
                sp.dma_start(k.edges[0], pads[:, 0:CHUNKS[0]]).then_inc(k.pads_in[0], 16)
                rest = IN_ROWS * P - E
                sp.dma_start(k.in_order[E:E + rest].rearrange("(o n) -> o n", o=1), pads[0:1, 0:rest]).then_inc(
                    in_order_in, 16)
                sp.wait_ge(entries, 1)
                sp.dma_start(k.in_order[0:E].rearrange("(p c) -> p c", p=EP), entry[:, 1, :]).then_inc(
                    in_order_in, 16)

            @block.gpsimd
            def _(pool):
                pool.iota(chunk_no[:, :], pattern=[[1, MOST]], base=0, channel_multiplier=0).then_inc(numbers, 1)
                pool.iota(row_i[:, 0:1], pattern=[[1, 1]], base=0, channel_multiplier=1).then_inc(numbers, 1)
                pool.iota(block_i[:, 0, :], pattern=[[1, P]], base=0, channel_multiplier=0).then_inc(numbers, 1)
                pool.iota(low_i[:, :], pattern=[[1, 1]], base=0, channel_multiplier=1).then_inc(numbers, 1)

            @block.tensor
            def _(pe):
                def count(q, i, j, first=False, last=False):
                    ins = pe.matmul(pair_sum[:, q, :], high_hot[:, ds(i * BATCH + j, 1), :, :].rearrange(
                        "p o h c -> p (o h c)"), low_hot[:, ds(i * BATCH + j, 1), :, :].rearrange(
                        "p o l c -> p (o l c)"), start=first, stop=last)
                    if last:
                        ins.then_inc(pairs_sum, 1)

                turns_here = EC // (BATCH * BATCH)
                for q in range(LISTS):
                    pe.wait_ge(hots, q + 1)
                    for j in range(BATCH):
                        count(q, 0, j, first=(j == 0))
                    with pe.Fori(1, turns_here - 1) as i:
                        for j in range(BATCH):
                            count(q, i, j)
                    for j in range(BATCH):
                        count(q, turns_here - 1, j, last=(j == BATCH - 1))
                pe.wait_ge(pairs_known, 1)
                pe.matmul(by_block[:, :, :].rearrange("p q l -> p (q l)"), to_block[:, :],
                          pairs[:, :, :].rearrange("p q l -> p (q l)"), start=True, stop=True)
                pe.wait_ge(counted, 1)
                for j in range(2):
                    last = pe.matmul(strays[:, :], disorder[:, j:j + 1], k.ones[0:EP, 0:1], start=(j == 0),
                                     stop=(j == 1))
                last.then_inc(counts_sum, 1)
                pe.wait_ge(chunks_known, 1)
                pe.matmul(sums[:, 0:LISTS], before_f[0:NB, 0:NB], chunks_f[:, :], start=True, stop=True)
                pe.matmul(sums[:, LISTS:], before_f[0:NB, 0:NB], edges_f[:, :],
                          start=True, stop=True).then_inc(starts_sum, 1)
                pe.wait_ge(base_set, 1)
                for q in range(LISTS):
                    PIECE = CHUNKS[q] // PIECES
                    for j in range(PIECES):
                        pe.matmul(block_sum[:, j, 0:PIECE], ones_b[:, :], begun[:, q, j * PIECE:(j + 1) * PIECE],
                                  start=True, stop=True).then_inc(blocks_sum, 1)
                    if q + 1 < LISTS:
                        pe.wait_ge(chunks_known, 2)

            @block.vector
            def _(dve):
                done = [0]

                def after_all(ins):
                    ins.then_inc(step, 1)
                    done[0] += 1
                    dve.wait_ge(step, done[0])

                dve.memset(next_end[:, :], N).then_inc(last_set, 1)
                dve.memset(pads[:, :], PAD).then_inc(pads_set, 1)
                dve.memset(ones_b[:, :], 1.0)
                dve.memset(key_block[:, :, EC:COLS], 0.0)
                dve.tensor_scalar(before[:, :], k.ramp[0:EP, 0:EP], k.place[0:EP, 0:1], None, ALU.is_gt)
                dve.tensor_scalar(after[:, :], k.ramp[0:EP, 0:EP], k.place[0:EP, 0:1], None, ALU.is_le)
                dve.tensor_scalar(before_f[:, :], k.ramp[:, :], k.place[:, 0:1], None, ALU.is_gt)
                dve.wait_ge(loaded, 16 * LISTS)
                after_all(dve.tensor_single_scalar(work_i[:, :, :], ends[:, :, :], SHIFT, ALU.logical_shift_right))
                dve.tensor_copy(key_block[:, :, 0:EC], work_i[:, :, :])

                def hot_parts(q):
                    after_all(dve.tensor_single_scalar(high_i[:, :], work_i[:, q, :], LOW_BITS,
                                                       ALU.logical_shift_right))
                    after_all(dve.tensor_copy(high_b[:, :], high_i[:, :]))
                    after_all(dve.tensor_single_scalar(high_i[:, :], work_i[:, q, :], LOWS - 1, ALU.bitwise_and))
                    after_all(dve.tensor_copy(low_b[:, :], high_i[:, :]))
                    if q:
                        dve.wait_ge(pairs_sum, q)
                    for hot, part, n in ((high_hot, high_b, HIGHS), (low_hot, low_b, LOWS)):
                        for v in range(n):
                            last = dve.tensor_scalar(hot[:, :, v, :], part[:, :].rearrange("p (a c) -> p a c", c=BATCH),
                                                     float(v), None, ALU.is_equal)
                    last.then_inc(hots, 1)

                for q in range(LISTS):
                    hot_parts(q)
                after_all(dve.tensor_single_scalar(work_i[:, :, :], ends[:, :, :], P - 1, ALU.bitwise_and))
                after_all(dve.tensor_copy(work_f[:, :, :], work_i[:, :, :]))
                for q in range(LISTS):
                    last = dve.scalar_tensor_tensor(entry[:, q, :], ends[:, 1 - q, :], float(LOC), work_f[:, q, :],
                                                    ALU.mult, ALU.add)
                last.then_inc(entries, 1)
                dve.wait_ge(loaded_next, 16)
                after_all(dve.tensor_single_scalar(next_block[:, :], next_end[:, 0:1], SHIFT, ALU.logical_shift_right))
                after_all(dve.tensor_copy(next_f[:, :], next_block[:, :]))
                dve.tensor_tensor(disorder[:, 1:2], key_block[:, 1, EC - 1:EC], next_f[:, :], ALU.is_gt)
                after_all(dve.tensor_tensor(work_f[:, 0, 0:EC - 1], key_block[:, 1, 0:EC - 1], key_block[:, 1, 1:EC],
                                            ALU.is_gt))
                dve.tensor_reduce(disorder[:, 0:1], work_f[:, 0, 0:EC - 1], X, ALU.add).then_inc(counted, 1)
                dve.wait_ge(numbers, 4)
                dve.tensor_single_scalar(row_i[:, 1:2], row_i[:, 0:1], BATCH - 1, ALU.bitwise_and)
                dve.tensor_single_scalar(row_i[:, 2:3], row_i[:, 0:1], BATCH.bit_length() - 1,
                                         ALU.logical_shift_right)
                dve.tensor_single_scalar(block_i[:, 1, :], block_i[:, 0, :], LOW_BITS, ALU.logical_shift_right)
                after_all(dve.tensor_single_scalar(low_i[:, :], low_i[:, :], LOWS - 1, ALU.bitwise_and))
                dve.tensor_copy(row_f[:, 1:3], row_i[:, 1:3])
                dve.tensor_copy(low_f[:, :], low_i[:, :])
                after_all(dve.tensor_copy(block_high[:, :], block_i[:, 1, :]))
                dve.tensor_scalar(same_column[:, :], k.ramp[0:HIGHS * BATCH, 0:BATCH], row_f[:, 1:2], None,
                                  ALU.is_equal)
                dve.tensor_scalar(is_low[:, :], k.ramp[0:NB, 0:LOWS], low_f[0:NB, 0:1], None, ALU.is_equal)
                after_all(dve.tensor_scalar(to_block[:, :], block_high[0:HIGHS * BATCH, 0:NB], row_f[:, 2:3], None,
                                            ALU.is_equal))
                dve.wait_ge(pairs_sum, LISTS)
                for q in range(LISTS):
                    last = dve.tensor_tensor(own_pairs[:, q, :, :],
                                             pair_sum[:, q, :].rearrange("p (l c) -> p l c", c=BATCH),
                                             same_column[:, :].unsqueeze(1).to_broadcast([HIGHS * BATCH, LOWS, BATCH]),
                                             ALU.mult)
                after_all(last)
                dve.tensor_reduce(pairs[:, :, :], own_pairs[:, :, :, :], X, ALU.add).then_inc(pairs_known, 1)
                dve.wait_ge(counts_sum, 1)
                dve.tensor_copy(disorder_i[:, :], strays[:, :])
                after_all(dve.tensor_tensor(counts[:, :, :], by_block[:, :, :],
                                            is_low[:, :].unsqueeze(1).to_broadcast([NB, LISTS, LOWS]), ALU.mult))
                after_all(dve.tensor_reduce(number[:, :], counts[:, :, :], X, ALU.add))
                dve.tensor_copy(edges_f[:, :], number[:, 1:2])
                for q, u in enumerate(MULTIPLE):
                    last = dve.tensor_scalar(chunks_i[:, q:q + 1], number[:, q:q + 1], float(P * u - 1), None, ALU.add)
                after_all(last)
                for q, u in enumerate(MULTIPLE):
                    last = dve.tensor_single_scalar(chunks_j[:, q:q + 1], chunks_i[:, q:q + 1], SHIFT + u // 2,
                                                    ALU.logical_shift_right)
                after_all(last)
                for q, u in enumerate(MULTIPLE):
                    last = dve.tensor_scalar(chunks_f[:, q:q + 1], chunks_j[:, q:q + 1], float(u), None, ALU.mult)
                last.then_inc(chunks_known, 1)
                dve.wait_ge(starts_sum, 1)
                dve.tensor_copy(edges_before[:, :], sums[:, LISTS:])
                after_all(dve.tensor_copy(start[:, :], sums[:, 0:LISTS]))
                for q in range(LISTS):
                    dve.tensor_scalar(base[:, q, :], k.ones[0:NB, 0:EP], start[:, q:q + 1], float(P),
                                      ALU.mult, ALU.mult)
                    last = dve.tensor_scalar(begun[:, q, :], chunk_no[:, :], start[:, q:q + 1], None, ALU.is_ge)
                last.then_inc(base_set, 1)
                for q in range(LISTS):
                    dve.wait_ge(blocks_sum, PIECES * (q + 1))
                    after_all(dve.tensor_scalar(
                        block_f[:, q, 0:CHUNKS[q]].rearrange("p (a b) -> p a b", a=PIECES),
                        block_sum[:, :, 0:CHUNKS[q] // PIECES], -1.0, None, ALU.add))
                    if q == 0:
                        dve.nop().then_inc(chunks_known, 1)
                    first_of_unit = block_f[0:1, q, 0:CHUNKS[q]].rearrange("p (a u) -> p a u", u=MULTIPLE[q])[:, :, 0:1]
                    dve.tensor_copy(k.block_row[q][:, :].unsqueeze(2), first_of_unit)
                dve.memset(same[:, 0:1], 0.0)
                of_pair = block_f[:, 0, 0:CHUNKS[0]].rearrange("p (a u) -> p a u", u=PAIR)[:, :, 0:1]
                after_all(dve.tensor_tensor(same[:, 1:].unsqueeze(2), of_pair[:, 1:, :],
                                            of_pair[:, 0:CHUNKS[0] // PAIR - 1, :], ALU.is_equal))
                after_all(dve.memset(k.carry[:, :, :, :], 0.0))
                for h in range(HEADS):
                    dve.tensor_copy(k.carry[:, :, h, 1:PAIRS + 1], same[:, :].rearrange("p (g c) -> p g c", c=PAIRS))
                dve.tensor_scalar(k.fresh[:, :], same[:, :], 1.0, -FAR, ALU.subtract, ALU.mult)

        with ExitStack() as c:
            reached = tmp_in(nc, c, "reached", [NB, CHUNKS[1]], F32)
            next_start = tmp_in(nc, c, "next_start", [NB, 1], F32)
            within = tmp_in(nc, c, "within", [NB, CHUNKS[1]], F32)
            limits = tmp_in(nc, c, "limits", [NB, 2], F32)
            own_no = tmp_in(nc, c, "own_no", [P, WINDOWS], I32)
            own_f = tmp_in(nc, c, "own_f", [P, WINDOWS], F32)
            first_f = tmp_in(nc, c, "first_f", [P, WINDOWS], F32)
            first_i = tmp_in(nc, c, "first_i", [P, WINDOWS], I32)
            length = tmp_in(nc, c, "length", [P, WINDOWS], F32)
            row_of = tmp_in(nc, c, "row_of", [P, 2, WINDOWS], I32)
            skip = tmp_in(nc, c, "skip", [P, WINDOWS], I32)
            bit = tmp_in(nc, c, "bit", [P, SHIFT, WINDOWS], I32)
            bit_f = tmp_in(nc, c, "bit_f", [P, SHIFT, WINDOWS], F32)
            raw_w = tmp_in(nc, c, "raw_w", [P, WINDOWS, 2, P], I32)
            window = tmp_in(nc, c, "window", [P, WINDOWS, 2 * P], F32)
            change = tmp_in(nc, c, "change", [P, WINDOWS, 2 * P], F32)
            listed = tmp_in(nc, c, "listed", [P, CHUNKS[1]], I32)
            w_step = c.enter_context(nc.semaphore("w_step"))
            own_set = c.enter_context(nc.semaphore("own_set"))
            within_set = c.enter_context(nc.semaphore("within_set"))
            limits_out = c.enter_context(nc.semaphore("limits_out"))
            rows_known = c.enter_context(nc.semaphore("rows_known"))
            fetched = c.enter_context(nc.semaphore("fetched"))
            masked = c.enter_context(nc.semaphore("masked"))
            turned = c.enter_context(nc.semaphore("turned_w"))
            listed_set = c.enter_context(nc.semaphore("listed_set"))
            list_in = c.enter_context(nc.semaphore("list_in"))
            at_chunk = c.enter_context(nc.psum_tensor("at_chunk", [P, WINDOWS, 2], F32))
            turned_w = c.enter_context(nc.psum_tensor("turned_windows", [P, 4, 512], F32))
            block = c.enter_context(nc.Block())

            @block.gpsimd
            def _(pool):
                pool.iota(own_no[:, :], pattern=[[P * P, WINDOWS]], base=0, channel_multiplier=P).then_inc(own_set, 1)
                bound = pool.to_reg(IN_ROWS - 1)
                pool.wait_ge(in_order_in, 32)
                pool.wait_ge(rows_known, 1)
                for w in range(WINDOWS):
                    for r in range(2):
                        pool.indirect_dma_start(
                            out=raw_w[:, w, r, :], out_offset=None,
                            in_=k.in_order.rearrange("(r e) -> r e", e=P),
                            in_offset=bass.IndirectOffsetOnAxis(ap=row_of[:, r, w:w + 1], axis=0),
                            bounds_check=bound, oob_is_err=False).then_inc(fetched, 16)

            @block.tensor
            def _(pe):
                pe.wait_ge(within_set, 1)
                for w in range(WINDOWS):
                    last = pe.matmul(at_chunk[:, w, :], within[:, w * P:(w + 1) * P], limits[:, :],
                                     start=True, stop=True)
                last.then_inc(limits_out, 1)
                pe.wait_ge(masked, 1)
                for w in range(WINDOWS):
                    last = pe.transpose(turned_w[:, w // 4, (w % 4) * P:(w % 4 + 1) * P], window[:, w, 0:P],
                                        k.ident[:, :])
                last.then_inc(turned, 1)

            @block.vector
            def _(dve):
                done = [0]

                def after_all(ins):
                    ins.then_inc(w_step, 1)
                    done[0] += 1
                    dve.wait_ge(w_step, done[0])

                dve.tensor_tensor(next_start[:, :], start[:, 1:2], chunks_f[:, 1:2], ALU.add)
                dve.scalar_tensor_tensor(limits[:, 0:1], start[:, 1:2], -float(P), edges_before[:, :],
                                         ALU.mult, ALU.add)
                dve.tensor_tensor(limits[:, 1:2], edges_before[:, :], edges_f[:, :], ALU.add)
                after_all(dve.tensor_scalar(reached[:, :], chunk_no[:, 0:CHUNKS[1]], start[:, 1:2], None, ALU.is_ge))
                dve.scalar_tensor_tensor(within[:, :], chunk_no[:, 0:CHUNKS[1]], next_start[:, 0:1], reached[:, :],
                                         ALU.is_lt, ALU.mult).then_inc(within_set, 1)
                dve.wait_ge(own_set, 1)
                after_all(dve.tensor_copy(own_f[:, :], own_no[:, :]))
                dve.wait_ge(limits_out, 1)
                firsts, stops = (at_chunk[:, :, j:j + 1].rearrange("p w o -> p (w o)") for j in range(2))
                after_all(dve.tensor_tensor(first_f[:, :], firsts, own_f[:, :], ALU.add))
                after_all(dve.tensor_scalar(first_f[:, :], first_f[:, :], float(E), 0.0, ALU.min, ALU.max))
                dve.tensor_tensor(length[:, :], stops, first_f[:, :], ALU.subtract)
                after_all(dve.tensor_copy(first_i[:, :], first_f[:, :]))
                dve.tensor_single_scalar(skip[:, :], first_i[:, :], P - 1, ALU.bitwise_and)
                after_all(dve.tensor_single_scalar(row_of[:, 0, :], first_i[:, :], SHIFT, ALU.logical_shift_right))
                dve.tensor_scalar(row_of[:, 1, :], row_of[:, 0, :], 1.0, None, ALU.add).then_inc(rows_known, 1)
                for j in range(SHIFT):
                    last = dve.tensor_single_scalar(bit[:, j, :], skip[:, :], 1 << j, ALU.bitwise_and)
                after_all(last)
                dve.tensor_scalar(bit_f[:, :, :], bit[:, :, :], 0.0, None, ALU.is_gt)
                dve.wait_ge(fetched, 16 * 2 * WINDOWS)
                after_all(dve.tensor_copy(window[:, :, :], raw_w[:, :, :, :].rearrange("p w r e -> p w (r e)")))
                have = 2 * P
                for j in reversed(range(SHIFT)):
                    by = 1 << j
                    have -= by
                    after_all(dve.tensor_tensor(change[:, :, 0:have], window[:, :, by:by + have],
                                                window[:, :, 0:have], ALU.subtract))
                    after_all(dve.tensor_tensor(change[:, :, 0:have], change[:, :, 0:have],
                                                bit_f[:, j, :].unsqueeze(2).to_broadcast([P, WINDOWS, have]),
                                                ALU.mult))
                    after_all(dve.tensor_tensor(window[:, :, 0:have], window[:, :, 0:have], change[:, :, 0:have],
                                                ALU.add))
                after_all(dve.tensor_tensor(change[:, :, 0:P], k.ramp[:, :].unsqueeze(1).to_broadcast([P, WINDOWS, P]),
                                            length[:, :].unsqueeze(2).to_broadcast([P, WINDOWS, P]), ALU.is_ge))
                dve.scalar_tensor_tensor(window[:, :, 0:P], change[:, :, 0:P], float(PAD), window[:, :, 0:P],
                                         ALU.mult, ALU.max).then_inc(masked, 1)
                dve.wait_ge(turned, 1)
                dve.tensor_copy(listed[:, :], turned_w[:, :, :].rearrange("p a b -> p (a b)")[:, 0:CHUNKS[1]]).then_inc(
                    listed_set, 1)

            @block.sync
            def _(sp):
                sp.wait_ge(listed_set, 1)
                sp.dma_start(k.edges[1], listed[:, :]).then_inc(list_in, 16)
                sp.wait_ge(list_in, 16)

        scatter(nc, k, s, 0, None)
        scatter(nc, k, s, 1, disorder_i)


def tmp_in(nc, c, name, shape, dt):
    return c.enter_context(nc.sbuf_tensor(name, shape, dt))


def scatter(nc, k, s, q, wanted):
    TURN = 2 * HALF
    assert EC % TURN == 0

    def if_wanted(eng, program):
        if wanted is None:
            program()
            return
        flag = eng.alloc_register(f"disorder_{eng.engine.name}")
        eng.load([flag], wanted[0:1, 0:1])
        with eng.If_ne(flag, 0):
            program()

    with ExitStack() as c:
        def tmp(name, shape, dt):
            return tmp_in(nc, c, f"{name}{q}", shape, dt)

        def sem(name):
            return c.enter_context(nc.semaphore(f"{name}{q}"))

        onehot = tmp("onehot", [EP, HALF, NB], BF16)
        ranked = tmp("ranked", [EP, 2, NB], F32)
        spot_f = tmp("spot_f", [EP, 2, HALF], F32)
        spot_i = tmp("spot_i", [EP, 2, HALF], I32)
        spot_p = tmp("spot_p", [EP, 2, HALF], I32)
        spot_c = tmp("spot_c", [EP, 2, HALF], I32)
        address = tmp("address", [EP, 2, HALF], I32)
        moved = tmp("moved", [EP, 2, HALF], I32)
        hot = sem("hot")
        place_known = sem("place_known")
        rank_sum = sem("rank_sum")
        spots = sem("spots")
        placed = sem("placed")
        scattered = [sem(f"scattered{h}_") for h in range(2)]
        running = c.enter_context(nc.psum_tensor(f"running{q}", [EP, NB], F32))
        block = c.enter_context(nc.Block())

        @block.sync
        def _(sp):
            if wanted is None:
                return

            def program():
                sp.dma_start(k.edges[q], s.pads[:, 0:CHUNKS[q]]).then_inc(k.pads_in[q], 16)
                sp.wait_ge(k.pads_in[q], 16)

            if_wanted(sp, program)

        @block.gpsimd
        def _(pool):
            due = pool.alloc_register(f"due{q}")

            def program():
                bound = pool.to_reg(P * CHUNKS[q] - 1)
                pool.reg_mov(due, 1)
                pool.wait_ge(k.pads_in[q], 16)
                flat = k.edges[q].rearrange("p (c o) -> (p c) o", o=1)
                with pool.Fori(0, EC // TURN):
                    for h in range(2):
                        pool.wait_ge(spots, due)
                        pool.reg_add(due, due, 1)
                        for j in range(HALF):
                            pool.indirect_dma_start(
                                out=flat, out_offset=bass.IndirectOffsetOnAxis(ap=address[:, h, j:j + 1], axis=0),
                                in_=moved[:, h, j:j + 1], in_offset=None,
                                bounds_check=bound, oob_is_err=False).then_inc(scattered[h], 16)
                for h in range(2):
                    pool.wait_ge(scattered[h], 16 * HALF * (EC // TURN))

            if_wanted(pool, program)

        @block.tensor
        def _(pe):
            def column(g, j):
                if j != 0 or not isinstance(g, int):
                    wait(pe, place_known, g + j)
                    pe.matmul(running[:, :], s.after[:, :], onehot[:, (j - 1) % HALF, :],
                              start=False, stop=True, skip_group_check=True)
                pe.wait_ge(hot, g + j + 1)
                pe.matmul(running[:, :], s.before[:, :], onehot[:, j % HALF, :],
                          start=False, stop=True, skip_group_check=True).then_inc(rank_sum, 1)

            def program():
                pe.matmul(running[:, :], s.base[:, q, :], k.ident[0:NB, 0:NB], start=True, stop=True)
                for j in range(TURN):
                    column(0, j)
                with pe.Fori(1, EC // TURN) as i:
                    for j in range(TURN):
                        column(i * TURN, j)

            if_wanted(pe, program)

        @block.vector
        def _(dve):
            def hot_rows(col, j):
                dve.tensor_scalar(onehot[:, j % HALF, :], k.ramp[0:EP, 0:NB], s.key_block[:, q, ds(col, 1)], None,
                                  ALU.is_equal).then_inc(hot, 1)

            def half(i, h):
                first = isinstance(i, int)
                for j in range(h * HALF, (h + 1) * HALF):
                    col = i * TURN + j
                    dve.wait_ge(rank_sum, col + 1)
                    wait(dve, place_known, col - 1)
                    dve.scalar_tensor_tensor(ranked[:, j % 2, :], k.ramp[0:EP, 0:NB],
                                             s.key_block[:, q, ds(col, 1)], running[:, :], ALU.is_equal, ALU.mult,
                                             accum_out=spot_f[:, h, j % HALF:j % HALF + 1]).then_inc(place_known, 1)
                    hot_rows(col + AHEAD, j + AHEAD)
                dve.wait_ge(place_known, i * TURN + (h + 1) * HALF)
                n = 2 * i + h
                dve.tensor_copy(spot_i[:, h, :], spot_f[:, h, :]).then_inc(placed, 1)
                dve.wait_ge(placed, 3 * n + 1)
                dve.tensor_single_scalar(spot_p[:, h, :], spot_i[:, h, :], P - 1, ALU.bitwise_and)
                dve.tensor_single_scalar(spot_c[:, h, :], spot_i[:, h, :], SHIFT,
                                         ALU.logical_shift_right).then_inc(placed, 1)
                if not first:
                    dve.wait_ge(scattered[h], i * (16 * HALF))
                dve.tensor_copy(moved[:, h, :], s.entry[:, q, ds(i * TURN + h * HALF, HALF)])
                dve.wait_ge(placed, 3 * n + 2)
                dve.scalar_tensor_tensor(address[:, h, :], spot_p[:, h, :], float(CHUNKS[q]), spot_c[:, h, :],
                                         ALU.mult, ALU.add).then_inc(placed, 1)
                dve.wait_ge(placed, 3 * n + 3)
                dve.nop().then_inc(spots, 1)

            def program():
                for j in range(AHEAD):
                    hot_rows(j, j)
                half(0, 0)
                half(0, 1)
                with dve.Fori(1, EC // TURN) as i:
                    half(i, 0)
                    half(i, 1)

            if_wanted(dve, program)


def load_list(nc, k, q):
    with ExitStack() as c:
        raw = c.enter_context(nc.sbuf_tensor(f"raw{q}", [P, CHUNKS[q]], I32))
        part = c.enter_context(nc.sbuf_tensor(f"low_bits{q}", [P, CHUNKS[q]], I32))
        read = c.enter_context(nc.semaphore(f"read{q}"))
        cut = c.enter_context(nc.semaphore(f"cut{q}"))
        block = c.enter_context(nc.Block())

        @block.sync
        def _(sp):
            sp.dma_start(raw[:, :], k.edges[q]).then_inc(read, 16)

        @block.vector
        def _(dve):
            dve.wait_ge(read, 16)
            dve.tensor_single_scalar(k.row[:, 0:CHUNKS[q]], raw[:, :], 8, ALU.logical_shift_right)
            dve.tensor_single_scalar(part[:, :], raw[:, :], LOC - 1, ALU.bitwise_and).then_inc(cut, 1)
            dve.wait_ge(cut, 1)
            dve.tensor_copy(k.spot[:, 0:CHUNKS[q]], part[:, :])


def project(nc, k, x, Ww, Wb, a):
    W_EXT = D + 2 * HEADS
    RX = 4
    with ExitStack() as c:
        def tmp(name, shape, dt=F32):
            return c.enter_context(nc.sbuf_tensor(name, shape, dt))

        def sem(name):
            return c.enter_context(nc.semaphore(name))

        w = tmp("w", [P, 2, W_EXT])
        bias = tmp("bias", [P, W_EXT])
        a_all = tmp("a_all", [P, 2 * HD])
        junk = tmp("junk", [P, 12, HD])
        xin = tmp("xin", [P, RX, D])
        xT = tmp("xT", [P, 2, 2, P])
        wh = tmp("wh", [P, RX, W_EXT])
        t_all = tmp("t_all", [P, HEADS, NB])
        empty = tmp("empty", [P, ROWT])
        low = tmp("low", [P, HEADS])
        low_n = tmp("low_n", [P, HEADS])
        low_r = tmp("low_r", [P, HEADS])
        w_in = sem("w_in")
        cleared = sem("cleared")
        w_done = sem("w_done")
        x_in = [sem(f"x_in{r}") for r in range(RX)]
        turned = sem("turned")
        copied = sem("copied")
        product = sem("product")
        rows = sem("rows")
        stored = [sem(f"stored{r}") for r in range(RX)]
        empties = sem("empties")
        lows = sem("lows")
        all_low = sem("all_low")
        lows_step = sem("lows_step")
        pT = c.enter_context(nc.psum_tensor("pT", [P, 2, 512], F32))
        pW = c.enter_context(nc.psum_tensor("pW", [P, 2, 512], F32))
        MAIN = NB - 1 - (NB - 1) % RX
        TAIL = range(MAIN, NB)

        def size(b):
            return LAST if isinstance(b, int) and b == NB - 1 else P

        def rows_of(t, b, n):
            return t[ds(b * P, n), :] if not isinstance(b, int) else t[b * P:b * P + n, :]

        def each(eng, f):
            for r in range(RX):
                f(r, r, 0)
            with eng.Fori(1, MAIN // RX) as i:
                for r in range(RX):
                    f(i * RX + r, r, i)
            for b in TAIL:
                f(b, b % RX, b // RX)

        block = c.enter_context(nc.Block())

        @block.sync
        def _(sp):
            sp.dma_start(w[:, :, 0:D], Ww.rearrange("(k p) n -> p k n", p=P)).then_inc(w_in, 16)
            sp.dma_start(bias[:, 0:D], Wb.rearrange("(o n) -> o n", o=1).to_broadcast([P, D])).then_inc(w_in, 16)
            sp.dma_start(a_all[:, :], a.rearrange("(o n) -> o n", o=1).to_broadcast([P, 2 * HD])).then_inc(w_in, 16)

            def load(b, r, i):
                wait(sp, copied, b - RX + 1)
                sp.dma_start(xin[0:size(b), r, :], rows_of(x, b, size(b))).then_inc(x_in[r], 16)

            each(sp, load)

        @block.scalar
        def _(act):
            def copy(b, r, i):
                act.wait_ge(turned, b + 1)
                wait(act, product, b - 1)
                n = size(b)
                act.activation(xT[:, r % 2, :, 0:n], pT[:, r % 2, 0:2 * P].rearrange("p (a n) -> p a n", a=2)[:, :, 0:n],
                               ACT.Copy).then_inc(copied, 1)

            each(act, copy)
            act.wait_ge(cleared, 1)
            act.dma_start(k.table[N:NB * P, :], empty[0:NB * P - N, :]).then_inc(empties, 16)
            act.wait_ge(empties, 16)

        @block.tensor
        def _(pe):
            def turn(b, r, i):
                pe.wait_ge(x_in[r], i * 16 + 16)
                wait(pe, copied, b - 1)
                n = size(b)
                for j in range(2):
                    last = pe.transpose(pT[:, r % 2, j * P:j * P + n], xin[0:n, r, j * P:(j + 1) * P],
                                        k.ident[0:n, 0:n])
                last.then_inc(turned, 1)

            def multiply(b, r, i):
                pe.wait_ge(copied, b + 1)
                wait(pe, rows, b - 1)
                n = size(b)
                for j in range(2):
                    last = pe.matmul(pW[0:n, r % 2, 0:W_EXT], xT[:, r % 2, j, 0:n], w[:, j, :],
                                     start=(j == 0), stop=(j == 1))
                last.then_inc(product, 1)

            def both(b, r, i):
                turn(b, r, i)
                if not (isinstance(b, int) and b == 0):
                    multiply(b - 1, (r - 1) % RX, i)

            pe.wait_ge(w_done, 1)
            each(pe, both)
            multiply(NB - 1, (NB - 1) % RX, 0)

        @block.gpsimd
        def _(pool):
            def store(b, r, i):
                pool.wait_ge(rows, b + 1)
                pool.dma_start(rows_of(k.table, b, size(b)), wh[0:size(b), r, 0:ROWT]).then_inc(stored[r], 16)

            due = pool.alloc_register("due_rows")
            for r in range(RX):
                store(r, r, 0)
            pool.reg_mov(due, RX + 1)
            with pool.Fori(1, MAIN // RX) as i:
                for r in range(RX):
                    pool.wait_ge(rows, due)
                    pool.reg_add(due, due, 1)
                    pool.dma_start(k.table[ds(i * (RX * P) + r * P, P), :], wh[:, r, 0:ROWT]).then_inc(stored[r], 16)
            for b in TAIL:
                store(b, b % RX, 0)
            pool.wait_ge(lows, 1)
            pool.partition_all_reduce(low_r[:, :], low_n[:, :], P, bass.bass_isa.ReduceOp.max).then_inc(all_low, 1)
            for r in range(RX):
                pool.wait_ge(stored[r], 16 * (len(range(r, NB, RX))))

        @block.vector
        def _(dve):
            dve.memset(empty[:, 0:D], 0.0)
            dve.memset(empty[:, D:ROWT], FAR).then_inc(cleared, 1)
            dve.memset(t_all[:, :, :], -FAR)
            dve.memset(k.s_all[:, :, :], 0.0)
            dve.wait_ge(w_in, 48)
            n = 0
            for part in range(2):
                for h in range(HEADS):
                    col = D + part * HEADS + h
                    av = a_all[:, (1 - part) * HD:(2 - part) * HD]
                    for j in range(3):
                        wv, to = (w[:, j, h * HD:(h + 1) * HD], w[:, j, col:col + 1]) if j < 2 else (
                            bias[:, h * HD:(h + 1) * HD], bias[:, col:col + 1])
                        last = dve.tensor_tensor_reduce(junk[:, n, :], wv, av, 1.0, 0.0, ALU.mult, ALU.add, to)
                        n += 1
            last.then_inc(w_done, 1)
            dve.wait_ge(w_done, 1)

            def finish(b, r, i):
                dve.wait_ge(product, b + 1)
                if not (isinstance(i, int) and i == 0):
                    dve.wait_ge(stored[r], i * 16)
                n = size(b)
                dve.tensor_tensor(wh[0:n, r, :], pW[0:n, r % 2, 0:W_EXT], bias[0:n, :], ALU.add).then_inc(rows, 1)
                dve.wait_ge(rows, b + 1)
                bs = slice(b, b + 1) if isinstance(b, int) else ds(b, 1)
                dve.tensor_copy(t_all[0:n, :, bs], wh[0:n, r, D:ROWT].unsqueeze(2))
                dve.tensor_copy(k.s_all[0:n, bs, :], wh[0:n, r, ROWT:W_EXT].unsqueeze(1))

            each(dve, finish)
            done = [0]

            def after_all(ins):
                ins.then_inc(lows_step, 1)
                done[0] += 1
                dve.wait_ge(lows_step, done[0])

            after_all(dve.nop())
            after_all(dve.drain())
            after_all(dve.tensor_reduce(low[:, :], t_all[:, :, :], X, ALU.min))
            dve.tensor_scalar(low_n[:, :], low[:, :], -1.0, None, ALU.mult).then_inc(lows, 1)
            dve.wait_ge(all_low, 1)
            after_all(dve.tensor_scalar(k.t_low[:, :], low_r[:, :], -1.0, None, ALU.mult))
            dve.tensor_tensor(k.s_all[:, :, :], k.s_all[:, :, :],
                              k.t_low[:, :].unsqueeze(1).to_broadcast([P, NB, HEADS]), ALU.add)


def slots(i, j):
    return i * RING + j, i + j // RING, j % RING


def gather_rows(pool, k, q, table, width, table_rows, ready, lead):
    bound = pool.to_reg(table_rows - 1)
    due = pool.alloc_register("due_group" + table.name)

    def gather(r):
        for c in range(GROUP):
            at = r * GROUP + c
            pool.indirect_dma_start(out=k.rows[:, at, 0:width], out_offset=None, in_=table[:, :],
                                    in_offset=bass.IndirectOffsetOnAxis(ap=k.wanted[:, at:at + 1], axis=0),
                                    bounds_check=bound, oob_is_err=False).then_inc(k.gathered[r], 16)

    for r in range(RING):
        pool.wait_ge(ready, max(1, r - lead + 2))
        gather(r)
    pool.reg_mov(due, RING - lead + 2)
    with pool.Fori(1, TURNS[q]):
        for r in range(RING):
            pool.wait_ge(ready, due)
            pool.reg_add(due, due, 1)
            gather(r)


def block_values(eng, regs, k, q, g):
    eng.load(regs, k.block_row[q][0:1, ds(g * len(regs), len(regs))])
    return [eng.snap(r, min_val=0, max_val=NB - 1) for r in regs]


def turns(eng, q, step):
    for j in range(RING):
        step(0, j, True, False)
    with eng.Fori(1, TURNS[q] - 1) as i:
        for j in range(RING):
            step(i, j, False, False)
    for j in range(RING):
        step(TURNS[q] - 1, j, False, True)


def gat_pass(nc, k):
    LEAD = RING - 2
    with ExitStack() as c_:
        def tmp(name, shape, dt=F32):
            return c_.enter_context(nc.sbuf_tensor(name, shape, dt))

        def sem(name):
            return c_.enter_context(nc.semaphore(name))

        def ps(name, shape):
            return c_.enter_context(nc.psum_tensor(name, shape, F32))

        onehot = tmp("onehot_g", [P, 4, GROUP, P])
        scores = tmp("scores", [P, HEADS, GROUP, P])
        t_edge = tmp("t_edge", [P, 4, GROUP, HEADS])
        hot_node = tmp("hot_node", [P, 2, GROUP, P])
        weighted = tmp("weighted", [P, 2, GROUP, ACC])
        top = tmp("top", [P, 2, HEADS, PAIRS + 1])
        running = tmp("running_max", [P, 2, HEADS, PAIRS + 1])
        z_node = tmp("z_node", [P, 2, HEADS, PAIRS])
        m_before = tmp("m_before", [P, HEADS, PAIRS])
        fall = tmp("fall", [P, HEADS, PAIRS])
        fall_m = tmp("fall_m", [P, 2, HEADS, PAIRS])
        factor = tmp("factor", [P, 4, HEADS, PAIRS])
        node = tmp("node", [P, 2, PAIRS, 2 * HEADS])
        z_edge = tmp("z_edge", [P, GROUP, HEADS])
        e_edge = tmp("e_edge", [P, GROUP, HEADS])
        power = tmp("power", [P, 2, GROUP, HEADS])

        known = sem("known")
        t_ready = sem("t_ready")
        hot = sem("hot_g")
        scored = [sem(f"scored{h}") for h in range(HEADS)]
        turned = sem("turned_g")
        s_ready = sem("s_ready")
        maxed = sem("maxed")
        scanned = sem("scanned")
        z_ready = sem("z_ready")
        m_ready = sem("m_ready")
        fell = sem("fell")
        fall_ready = sem("fall_ready")
        factor_ready = sem("factor_ready")
        hot_copied = sem("hot_copied")
        q_ready = sem("q_ready")
        z_known = sem("z_known")
        e_known = sem("e_known")
        power_ready = sem("power_ready")
        weights = sem("weights")
        scaled = sem("scaled")
        summed = sem("summed")
        added = sem("added")

        scores_t = ps("scores_t", [P, HEADS * GROUP, P])
        hot_t = ps("hot_t", [P, GROUP, P])
        part = ps("part", [P, 2 * PAIRS, 512])
        q_edge = ps("q_edge", [P, 2, GROUP, 2 * HEADS])

        def weights_at(s):
            return weighted[:, s, :, :].rearrange("p c (h d) -> p c h d", h=HEADS)[:, :, :, HD:HD + 1]

        block = c_.enter_context(nc.Block())

        @block.gpsimd
        def _(pool):
            gather_rows(pool, k, 0, k.table, ROWT, NB * P, known, LEAD)

        @block.scalar
        def _(act):
            regs = [act.alloc_register(f"act_block{c}") for c in range(PAIRS)]

            def node_s(i, j):
                g, _, _ = slots(i, j)
                for c, b in enumerate(block_values(act, regs, k, 0, g)):
                    last = act.activation(node[:, j % 2, c, 0:HEADS],
                                          k.s_all[:, ds(b, 1), :].rearrange("p o h -> p (o h)"), ACT.Copy)
                last.then_inc(s_ready, 1)

            def score(i, j):
                g, _, _ = slots(i, j)
                act.wait_ge(hot, g + 1)
                act.wait_ge(t_ready, g + 1)
                for c in range(GROUP):
                    last = act.activation(scores[:, 1, c, :], onehot[:, j % 4, c, :], ACT.Copy,
                                          scale=t_edge[:, j % 4, c, 1:2])
                last.then_inc(scored[1], 1)

            def weigh(i, j):
                g, _, r = slots(i, j)
                act.wait_ge(power_ready, g + 1)
                act.activation(weights_at(j % 2), power[:, j % 2, :, :].unsqueeze(3), ACT.Exp).then_inc(weights, 1)
                act.wait_ge(weights, g + 1)
                for c in range(GROUP):
                    for h in range(HEADS):
                        o = h * (HD + 1)
                        last = act.activation(weighted[:, j % 2, c, o:o + HD],
                                              k.rows[:, r * GROUP + c, h * HD:(h + 1) * HD], ACT.Copy,
                                              scale=weighted[:, j % 2, c, o + HD:o + HD + 1])
                    last.then_inc(scaled, 1)

            def step(i, j, first, last):
                g, _, _ = slots(i, j)
                act.wait_ge(turned, g + 1)
                act.activation(hot_node[:, j % 2, :, :], hot_t[:, :, :], ACT.Copy).then_inc(hot_copied, 1)
                if not (last and j == RING - 1):
                    score(i, j + 1)
                if not (first and j == 0):
                    weigh(i, j - 1)
                act.wait_ge(fall_ready, g + 1)
                act.activation(factor[:, j % 4, :, :], fall_m[:, j % 2, :, :], ACT.Exp).then_inc(factor_ready, 1)
                if not (last and j == RING - 1):
                    node_s(i, j + 1)

            node_s(0, 0)
            score(0, 0)
            turns(act, 0, step)
            weigh(TURNS[0] - 1, RING - 1)

        @block.tensor
        def _(pe):
            def turn_hot(i, j):
                g, _, _ = slots(i, j)
                pe.wait_ge(hot, g + 1)
                wait(pe, hot_copied, g)
                for c in range(GROUP):
                    pe.transpose(hot_t[:, c, :], onehot[:, j % 4, c, :], k.ident[:, :])

            def turn_scores(i, j, h):
                g, _, _ = slots(i, j)
                pe.wait_ge(scored[h], g + 1)
                if h == 0:
                    wait(pe, maxed, g)
                for c in range(GROUP):
                    last = pe.transpose(scores_t[:, h * GROUP + c, :], scores[:, h, c, :], k.ident[:, :])
                if h == HEADS - 1:
                    last.then_inc(turned, 1)

            def add_up(i, j, c):
                g, _, _ = slots(i, j)
                pe.wait_ge(scaled, g * GROUP + c + 1)
                pair, of_pair = divmod(c, PAIR)
                if of_pair == 0:
                    wait(pe, added, ((g - 2) * PAIRS + pair + 1) * HEADS)
                mm = pe.matmul(part[:, (j % 2) * PAIRS + pair, 0:ACC], onehot[:, j % 4, c, :],
                               weighted[:, j % 2, c, :], start=(of_pair == 0), stop=(of_pair == PAIR - 1))
                if of_pair == PAIR - 1:
                    mm.then_inc(summed, 1)

            def step(i, j, first, last):
                g, _, _ = slots(i, j)
                has_next = not (last and j == RING - 1)
                has_prev = not (first and j == 0)
                if has_next:
                    turn_hot(i, j + 1)
                    for h in range(HEADS):
                        turn_scores(i, j + 1, h)
                pe.wait_ge(hot_copied, g + 1)
                pe.wait_ge(m_ready, g + 1)
                wait(pe, power_ready, g)
                for c in range(GROUP):
                    mm = pe.matmul(q_edge[:, j % 2, c, :], hot_node[:, j % 2, c, :], node[:, j % 2, c // PAIR, :],
                                   start=True, stop=True)
                mm.then_inc(q_ready, 1)
                for c in range(GROUP):
                    if has_prev:
                        add_up(i, j - 1, c)

            turn_hot(0, 0)
            for h in range(HEADS):
                turn_scores(0, 0, h)
            turns(pe, 0, step)
            for c in range(GROUP):
                add_up(TURNS[0] - 1, RING - 1, c)

        @block.vector
        def _(dve):
            regs = [dve.alloc_register(f"dve_block{c}") for c in range(PAIRS)]

            def edge_t(i, j):
                g, turn, r = slots(i, j)
                dve.wait_ge(k.gathered[r], (k.turns_before + turn + 1) * (16 * GROUP))
                dve.tensor_tensor(t_edge[:, j % 4, :, :], k.rows[:, r * GROUP:(r + 1) * GROUP, D:ROWT],
                                  k.t_low[:, :].unsqueeze(1).to_broadcast([P, GROUP, HEADS]),
                                  ALU.subtract).then_inc(t_ready, 1)

            def edge_hot(i, j):
                g, _, _ = slots(i, j)
                dve.tensor_tensor(onehot[:, j % 4, :, :], k.ramp[:, :].unsqueeze(1).to_broadcast([P, GROUP, P]),
                                  k.spot[:, ds(g * GROUP, GROUP)].unsqueeze(2).to_broadcast([P, GROUP, P]),
                                  ALU.is_equal).then_inc(hot, 1)
                yield
                dve.wait_ge(hot, g + 1)
                dve.wait_ge(t_ready, g + 1)
                dve.tensor_tensor(scores[:, 0, :, :], onehot[:, j % 4, :, :],
                                  t_edge[:, j % 4, :, 0:1].to_broadcast([P, GROUP, P]), ALU.mult).then_inc(scored[0], 1)
                yield

            def node_max(i, j):
                g, _, _ = slots(i, j)
                s = j % 2
                dve.wait_ge(turned, g + 1)
                dve.tensor_reduce(top[:, s, :, 1:PAIRS + 1],
                                  scores_t[:, :, :].rearrange("p (h c u) e -> p h c (u e)", h=HEADS, u=PAIR),
                                  X, ALU.max)
                dve.tensor_copy(top[:, s, :, 0:1], running[:, 1 - s, :, PAIRS:PAIRS + 1]).then_inc(maxed, 1)
                yield
                dve.wait_ge(maxed, g + 1)
                dve.tensor_tensor_scan(running[:, s, :, :].rearrange("p h c -> p (h c)"),
                                       k.carry[:, ds(g, 1), :, :].rearrange("p o h c -> p (o h c)"),
                                       top[:, s, :, :].rearrange("p h c -> p (h c)"), 0.0,
                                       ALU.mult, ALU.max).then_inc(scanned, 1)
                yield
                dve.wait_ge(scanned, g + 1)
                dve.wait_ge(s_ready, g + 1)
                s_here = node[:, s, :, 0:HEADS].rearrange("p c h -> p h c")
                dve.tensor_tensor(z_node[:, 0, :, :], running[:, s, :, 1:PAIRS + 1], s_here, ALU.add)
                dve.tensor_tensor(z_node[:, 1, :, :], running[:, s, :, 0:PAIRS], s_here, ALU.add).then_inc(z_ready, 1)
                yield
                dve.wait_ge(z_ready, g + 1)
                m_here = node[:, s, :, HEADS:2 * HEADS].rearrange("p c h -> p h c")
                dve.scalar_tensor_tensor(m_here, z_node[:, 0, :, :], SLOPE, z_node[:, 0, :, :], ALU.mult, ALU.max)
                dve.scalar_tensor_tensor(m_before[:, :, :], z_node[:, 1, :, :], SLOPE, z_node[:, 1, :, :],
                                         ALU.mult, ALU.max).then_inc(m_ready, 1)
                yield
                dve.wait_ge(m_ready, g + 1)
                dve.tensor_tensor(fall[:, :, :], m_before[:, :, :], m_here, ALU.subtract).then_inc(fell, 1)
                yield
                dve.wait_ge(fell, g + 1)
                dve.scalar_tensor_tensor(fall_m[:, s, :, :], fall[:, :, :], 0.0,
                                         k.fresh[:, ds(g * PAIRS, PAIRS)].unsqueeze(1).to_broadcast([P, HEADS, PAIRS]),
                                         ALU.min, ALU.add).then_inc(fall_ready, 1)
                yield

            def add_pair(i, j, c, b):
                g, _, _ = slots(i, j)
                dve.wait_ge(summed, g * PAIRS + c + 1)
                for h in range(HEADS):
                    wait(dve, added, (g * PAIRS + c) * HEADS + h - 1)
                    mine = k.acc[:, ds(b * ACC + h * (HD + 1), HD + 1)]
                    dve.scalar_tensor_tensor(mine, mine, factor[:, j % 4, h, c:c + 1],
                                             part[:, (j % 2) * PAIRS + c, h * (HD + 1):(h + 1) * (HD + 1)],
                                             ALU.mult, ALU.add).then_inc(added, 1)
                    yield

            def edge_power(i, j):
                g, _, _ = slots(i, j)
                q_here = q_edge[:, j % 2, :, :]
                dve.wait_ge(q_ready, g + 1)
                dve.tensor_tensor(z_edge[:, :, :], q_here[:, :, 0:HEADS], t_edge[:, j % 4, :, :],
                                  ALU.add).then_inc(z_known, 1)
                yield
                dve.wait_ge(z_known, g + 1)
                dve.scalar_tensor_tensor(e_edge[:, :, :], z_edge[:, :, :], SLOPE, z_edge[:, :, :],
                                         ALU.mult, ALU.max).then_inc(e_known, 1)
                yield
                dve.wait_ge(e_known, g + 1)
                dve.tensor_tensor(power[:, j % 2, :, :], e_edge[:, :, :], q_here[:, :, HEADS:2 * HEADS],
                                  ALU.subtract).then_inc(power_ready, 1)
                yield

            def step(i, j, first, last):
                g, _, _ = slots(i, j)
                has_next = not (last and j == RING - 1)
                adds = not (first and j < 2)
                a_stage = edge_hot(i, j + 1) if has_next else iter(())
                b_stage = node_max(i, j)
                c_stage = edge_power(i, j - 1) if not (first and j == 0) else iter(())
                if has_next:
                    edge_t(i, j + 1)
                next(b_stage)
                if adds:
                    blocks = block_values(dve, regs, k, 0, g - 2)
                for _ in range(2):
                    next(a_stage, None)
                    next(b_stage)
                next(c_stage, None)
                if adds:
                    dve.wait_ge(factor_ready, g - 1)
                for c in range(PAIRS):
                    d_stage = add_pair(i, j - 2, c, blocks[c]) if adds else iter(())
                    for _ in range(HEADS):
                        next(d_stage, None)
                        next(b_stage, None)
                        next(c_stage, None)
                if not last or j + LEAD < RING:
                    r = (j + LEAD) % RING
                    dve.tensor_copy(k.wanted[:, r * GROUP:(r + 1) * GROUP],
                                    k.row[:, ds((g + LEAD) * GROUP, GROUP)]).then_inc(known, 1)

            dve.tensor_copy(k.wanted[:, 0:LEAD * GROUP], k.row[:, 0:LEAD * GROUP]).then_inc(known, 1)
            dve.memset(k.acc[:, :], 0.0)
            dve.memset(running[:, :, :, :], 0.0)
            edge_t(0, 0)
            for _ in edge_hot(0, 0):
                pass
            turns(dve, 0, step)
            for _ in edge_power(TURNS[0] - 1, RING - 1):
                pass
            for j in range(RING - 2, RING):
                end = block_values(dve, regs, k, 0, GROUPS[0] - RING + j)
                dve.wait_ge(factor_ready, GROUPS[0] - RING + j + 1)
                for c in range(PAIRS):
                    for _ in add_pair(TURNS[0] - 1, j, c, end[c]):
                        pass


def sage_pass(nc, k, table, count):
    LEAD = RING
    WIDE = D + 1 if count else D
    tag = int(not count)
    with ExitStack() as c_:
        def sem(name):
            return c_.enter_context(nc.semaphore(name))

        onehot = c_.enter_context(nc.sbuf_tensor(f"onehot_s{tag}", [P, 4, GROUP, P], F32))
        known = sem(f"known_s{tag}")
        hot = sem(f"hot_s{tag}")
        summed = sem(f"summed_s{tag}")
        added = sem(f"added_s{tag}")
        part = c_.enter_context(nc.psum_tensor(f"part_s{tag}", [P, 2, GROUP, 512], F32))
        block = c_.enter_context(nc.Block())

        @block.gpsimd
        def _(pool):
            gather_rows(pool, k, 1, table, D, NB * P, known, LEAD)

        @block.tensor
        def _(pe):
            def step(i, j, first, last):
                g, turn, r = slots(i, j)
                pe.wait_ge(k.gathered[r], (k.turns_before + turn + 1) * (16 * GROUP))
                pe.wait_ge(hot, g + 1)
                wait(pe, added, g * GROUP - GROUP)
                for c in range(GROUP):
                    pe.matmul(part[:, j % 2, c, 0:WIDE], onehot[:, j % 4, c, :],
                              k.rows[:, r * GROUP + c, 0:WIDE], start=True, stop=True).then_inc(summed, 1)

            turns(pe, 1, step)

        @block.vector
        def _(dve):
            regs = [dve.alloc_register(f"dve_block_s{tag}{c}") for c in range(GROUP)]

            def hot_rows(i, j, c):
                g, _, _ = slots(i, j)
                ins = dve.tensor_scalar(onehot[:, j % 4, c, :], k.ramp[:, :], k.spot[:, ds(g * GROUP + c, 1)], None,
                                        ALU.is_equal)
                if c == GROUP - 1:
                    ins.then_inc(hot, 1)

            def step(i, j, first, last):
                g, _, _ = slots(i, j)
                blocks = block_values(dve, regs, k, 1, g)
                for c in range(GROUP):
                    dve.wait_ge(summed, g * GROUP + c + 1)
                    wait(dve, added, g * GROUP + c)
                    mine = k.acc[:, ds(blocks[c] * ACC, WIDE)]
                    dve.tensor_tensor(mine, mine, part[:, j % 2, c, 0:WIDE], ALU.add).then_inc(added, 1)
                    if not (last and j >= RING - 2):
                        hot_rows(i, j + 2, c)
                if not last:
                    r = j % RING
                    dve.tensor_copy(k.wanted[:, r * GROUP:(r + 1) * GROUP],
                                    k.row[:, ds((g + LEAD) * GROUP, GROUP)]).then_inc(known, 1)

            dve.tensor_copy(k.wanted[:, 0:LEAD * GROUP], k.row[:, 0:LEAD * GROUP]).then_inc(known, 1)
            if count:
                dve.memset(k.rows[:, :, D:D + 1], 1.0)
            dve.memset(k.acc[:, :], 0.0)
            for j in range(2):
                for c in range(GROUP):
                    hot_rows(0, j, c)
            turns(dve, 1, step)


UNIT = 7
UNITS = NB // UNIT
assert UNITS * UNIT == NB and UNITS % 2 == 0


def unit_rows(table, u):
    rows = table[ds(u * (UNIT * P), UNIT * P), :] if not isinstance(u, int) else table[u * UNIT * P:(u + 1) * UNIT * P, :]
    return rows.rearrange("(b p) d -> p b d", p=P)


def move_unit(eng, on_chip, table, u, sem, load):
    whole = UNIT - 1
    first = u * (UNIT * P)
    last_rows = LAST if isinstance(u, int) and u == UNITS - 1 else P

    def rows(start, n):
        return table[start:start + n, :] if isinstance(start, int) else table[ds(start, n), :]

    for chip, dram in ((on_chip[:, 0:whole, :], rows(first, whole * P).rearrange("(b p) d -> p b d", p=P)),
                       (on_chip[0:last_rows, whole, :], rows(first + whole * P, last_rows))):
        eng.dma_start(*((chip, dram) if load else (dram, chip))).then_inc(sem, 16)


def unit_turns(eng, f):
    for h in range(2):
        f(h, h, 0)
    with eng.Fori(1, UNITS // 2 - 1) as i:
        for h in range(2):
            f(i * 2 + h, h, i)
    for h in range(2):
        f(UNITS - 2 + h, h, UNITS // 2 - 1)


def gat_end(nc, k, x):
    with ExitStack() as c:
        def tmp(name, shape, dt=F32):
            return c.enter_context(nc.sbuf_tensor(name, shape, dt))

        def sem(name):
            return c.enter_context(nc.semaphore(name))

        xin = tmp("xin_e", [P, 2, UNIT, D])
        own = tmp("own", [P, 2, UNIT, D])
        total = tmp("total", [P, 2, UNIT, D])
        weight = tmp("weight", [P, NB, HEADS])
        alone = tmp("alone", [P, NB, HEADS])
        stats = tmp("stats", [P, UNIT, 6])
        mean = tmp("mean", [P, UNIT, 2])
        spread = tmp("spread", [P, UNIT])
        eps = tmp("eps", [P, 1])
        x_in = [sem(f"x_in_e{h}") for h in range(2)]
        own_in = [sem(f"own_in{h}") for h in range(2)]
        tick = sem("tick")
        cleared = sem("cleared_e")
        var_ready = sem("var_ready")
        root_ready = sem("root_ready")
        normed = sem("normed")
        stored = [sem(f"stored_e{h}") for h in range(2)]
        block = c.enter_context(nc.Block())

        @block.sync
        def _(sp):
            def load(u, h, i):
                if h == 0 and isinstance(u, int) and u == 0:
                    sp.wait_ge(cleared, 1)
                wait(sp, normed, u - 1)
                move_unit(sp, xin[:, h, :, :], x, u, x_in[h], True)
                sp.dma_start(own[:, h, :, :], unit_rows(k.table, u)[:, :, 0:D]).then_inc(own_in[h], 16)

            unit_turns(sp, load)

        @block.scalar
        def _(act):
            def store(u, h, i):
                act.wait_ge(var_ready, u + 1)
                act.activation(spread[:, :], mean[:, :, 1:2].rearrange("p u o -> p (u o)"), ACT.Sqrt,
                               bias=eps[:, 0:1]).then_inc(root_ready, 1)
                act.wait_ge(normed, u + 1)
                act.dma_start(unit_rows(k.x1, u), total[:, h, :, :]).then_inc(stored[h], 16)

            unit_turns(act, store)
            for h in range(2):
                act.wait_ge(stored[h], 16 * (UNITS // 2))

        @block.vector
        def _(dve):
            dve.memset(eps[:, :], EPS)
            dve.memset(xin[:, :, UNIT - 1, :], 0.0).then_inc(cleared, 1)
            sums = k.acc[:, :].rearrange("p (b h d) -> p b h d", b=NB, h=HEADS)
            total_w = sums[:, :, :, HD:HD + 1].rearrange("p b h o -> p b (h o)")
            dve.tensor_scalar(alone[:, :, :], total_w, 0.0, None, ALU.is_equal)
            dve.tensor_scalar(weight[:, :, :], total_w, 1e-30, None, ALU.max).then_inc(tick, 1)
            dve.wait_ge(tick, 1)
            dve.reciprocal(weight[:, :, :], weight[:, :, :]).then_inc(tick, 1)
            dve.wait_ge(tick, 2)
            PER = 5

            def finish(u, h, i):
                n = u * PER + 2

                def stage(s):
                    dve.wait_ge(tick, n + s)

                dve.wait_ge(x_in[h], (i + 1) * 32)
                if not (isinstance(i, int) and i == 0):
                    dve.wait_ge(stored[h], i * 16)
                for b in range(UNIT):
                    for hd in range(HEADS):
                        at = u * UNIT + b
                        cut = slice(hd * HD, (hd + 1) * HD)
                        last = dve.scalar_tensor_tensor(
                            total[:, h, b, cut], k.acc[:, ds(at * ACC + hd * (HD + 1), HD)],
                            weight[:, ds(at, 1), hd:hd + 1].rearrange("p o h -> p (o h)"), xin[:, h, b, cut],
                            ALU.mult, ALU.add)
                last.then_inc(tick, 1)
                stage(1)
                dve.wait_ge(own_in[h], (i + 1) * 16)
                for b in range(UNIT):
                    for hd in range(HEADS):
                        cut = slice(hd * HD, (hd + 1) * HD)
                        last = dve.scalar_tensor_tensor(
                            total[:, h, b, cut], own[:, h, b, cut],
                            alone[:, ds(u * UNIT + b, 1), hd:hd + 1].rearrange("p o h -> p (o h)"),
                            total[:, h, b, cut], ALU.mult, ALU.add)
                last.then_inc(tick, 1)
                stage(2)
                for b in range(UNIT):
                    last = dve.bn_stats(stats[:, b, :], total[:, h, b, :])
                last.then_inc(tick, 1)
                stage(3)
                dve.nop().then_inc(k.apart, 1)
                for b in range(UNIT):
                    last = dve.bn_aggr(mean[:, b, :], stats[:, b, :])
                last.then_inc(var_ready, 1)
                dve.wait_ge(root_ready, u + 1)
                dve.wait_ge(var_ready, u + 1)
                dve.reciprocal(spread[:, :], spread[:, :]).then_inc(tick, 1)
                stage(4)
                for b in range(UNIT):
                    last = dve.tensor_scalar(total[:, h, b, :], total[:, h, b, :], mean[:, b, 0:1],
                                             spread[:, b:b + 1], ALU.subtract, ALU.mult)
                last.then_inc(normed, 1)
                dve.wait_ge(normed, u + 1)
                dve.nop().then_inc(tick, 1)

            unit_turns(dve, finish)


def sage_end(nc, k, table, Wl, bl, Wr, out, final):
    with ExitStack() as c:
        def tmp(name, shape, dt=F32):
            return c.enter_context(nc.sbuf_tensor(name, shape, dt))

        def sem(name):
            return c.enter_context(nc.semaphore(name))

        tag = "f" if final else "h"
        wl = tmp("wl" + tag, [P, 2, D])
        wr = tmp("wr" + tag, [P, 2, D])
        bias = tmp("bias" + tag, [P, D])
        rows = tmp("rows_e" + tag, [P, 2, UNIT, D])
        first = tmp("first" + tag, [P, 2, UNIT, D]) if final else None
        result = tmp("result" + tag, [P, 2, UNIT, D])
        average = tmp("average" + tag, [P, UNIT, D])
        turned_sb = tmp("turned_sb" + tag, [P, 2, 4, P])
        biased = tmp("biased" + tag, [P, 2, D])
        stats = tmp("stats" + tag, [P, UNIT, 6])
        mean = tmp("mean" + tag, [P, UNIT, 2])
        spread = tmp("spread" + tag, [P, UNIT])
        eps = tmp("eps" + tag, [P, 1])
        w_in = sem("w_in" + tag)
        rows_in = [sem(f"rows_in{tag}{h}") for h in range(2)]
        first_in = [sem(f"first_in{tag}{h}") for h in range(2)]
        setup = sem("setup" + tag)
        averaged = sem("averaged" + tag)
        turned = sem("turned" + tag)
        copied = sem("copied" + tag)
        product = sem("product" + tag)
        biased_ready = sem("biased_ready" + tag)
        tick = sem("tick" + tag)
        stats_ready = sem("stats_ready" + tag)
        var_ready = sem("var_ready" + tag)
        inverted = sem("inverted" + tag)
        root_ready = sem("root_ready" + tag)
        unit_done = sem("unit_done" + tag)
        stored = [sem(f"stored{tag}{h}") for h in range(2)]
        pT = c.enter_context(nc.psum_tensor("pT" + tag, [P, 2, 4, P], F32))
        pO = c.enter_context(nc.psum_tensor("pO" + tag, [P, 2, 512], F32))
        block = c.enter_context(nc.Block())

        @block.sync
        def _(sp):
            for t, w in ((wl, Wl), (wr, Wr)):
                sp.dma_start(t[:, :, :], w.rearrange("(j p) n -> p j n", p=P)).then_inc(w_in, 16)
            sp.dma_start(bias[:, :], bl.rearrange("(o n) -> o n", o=1).to_broadcast([P, D])).then_inc(w_in, 16)

            def load(u, h, i):
                wait(sp, tick, (u - 1) * UNIT)
                sp.dma_start(rows[:, h, :, :], unit_rows(table, u)).then_inc(rows_in[h], 16)
                if final:
                    sp.dma_start(first[:, h, :, :], unit_rows(k.x1, u)).then_inc(first_in[h], 16)

            def store(u, h):
                sp.wait_ge(unit_done, u + 1)
                if final:
                    move_unit(sp, result[:, h, :, :], out, u, stored[h], False)
                else:
                    sp.dma_start(unit_rows(out, u), result[:, h, :, :]).then_inc(stored[h], 16)

            def both(u, h, i):
                load(u, h, i)
                if not (isinstance(u, int) and u < 2):
                    store(u - 2, h)

            unit_turns(sp, both)
            for h in range(2):
                store(UNITS - 2 + h, h)
            for h in range(2):
                sp.wait_ge(stored[h], (32 if final else 16) * (UNITS // 2))

        @block.tensor
        def _(pe):
            def turn(u, h, i, b):
                n = u * UNIT + b
                s = (h * UNIT + b)
                if b == 0:
                    pe.wait_ge(rows_in[h], (i + 1) * 16)
                pe.wait_ge(averaged, n + 1)
                wait(pe, copied, n - 1)
                for j in range(2):
                    pe.transpose(pT[:, s % 2, j, :], average[:, b, j * P:(j + 1) * P],
                                 k.ident[:, :])
                for j in range(2):
                    last = pe.transpose(pT[:, s % 2, 2 + j, :], rows[:, h, b, j * P:(j + 1) * P], k.ident[:, :])
                last.then_inc(turned, 1)

            def multiply(u, h, b):
                n = u * UNIT + b
                s = (h * UNIT + b) % 2
                pe.wait_ge(copied, n + 1)
                wait(pe, biased_ready, n - 1)
                for j in range(4):
                    w = (wl, wr)[j // 2]
                    last = pe.matmul(pO[:, s, 0:D], turned_sb[:, s, j, :], w[:, j % 2, :], start=(j == 0),
                                     stop=(j == 3))
                last.then_inc(product, 1)

            def unit(u, h, i):
                for b in range(UNIT):
                    turn(u, h, i, b)
                    if not (isinstance(u, int) and u == 0 and b == 0):
                        if b:
                            multiply(u, h, b - 1)
                        else:
                            multiply(u - 1, 1 - h, UNIT - 1)

            pe.wait_ge(w_in, 48)
            unit_turns(pe, unit)
            multiply(UNITS - 1, 1, UNIT - 1)

        @block.scalar
        def _(act):
            act.wait_ge(setup, 1)

            def unit(u, h, i):
                for b in range(UNIT):
                    n = u * UNIT + b
                    s = (h * UNIT + b) % 2
                    act.wait_ge(turned, n + 1)
                    wait(act, product, n - 1)
                    act.activation(turned_sb[:, s, :, :], pT[:, s, :, :], ACT.Copy).then_inc(copied, 1)
                    if not final and not (isinstance(u, int) and u == 0 and b == 0):
                        rectify(u, h, i, b - 1)
                    if final and b == 3 and not (isinstance(u, int) and u == 0):
                        root(u - 1)

            def rectify(u, h, i, b):
                if b < 0:
                    u, h, i, b = u - 1, 1 - h, (i if h == 1 else i - 1), UNIT - 1
                n = u * UNIT + b
                s = (h * UNIT + b) % 2
                if b == 0 and not (isinstance(i, int) and i == 0):
                    act.wait_ge(stored[h], i * 16)
                act.wait_ge(biased_ready, n + 1)
                ins = act.activation(result[:, h, b, :], biased[:, s, :], ACT.Relu)
                ins.then_inc(tick, 1)
                if b == UNIT - 1:
                    act.wait_ge(tick, n + 1)
                    act.nop().then_inc(unit_done, 1)

            def root(u):
                act.wait_ge(var_ready, u + 1)
                act.activation(spread[:, :], mean[:, :, 1:2].rearrange("p u o -> p (u o)"), ACT.Sqrt,
                               bias=eps[:, 0:1]).then_inc(root_ready, 1)

            unit_turns(act, unit)
            if final:
                root(UNITS - 1)
            else:
                rectify(UNITS - 1, 1, UNITS // 2 - 1, UNIT - 1)

        @block.vector
        def _(dve):
            dve.memset(eps[:, :], EPS).then_inc(setup, 1)
            if not final:
                counts = k.acc[:, :].rearrange("p (b d) -> p b d", b=NB)[:, :, D:D + 1].rearrange("p b o -> p (b o)")
                dve.tensor_scalar(k.share[:, :], counts, 1.0, None, ALU.max).then_inc(setup, 1)
                dve.wait_ge(setup, 2)
                dve.reciprocal(k.share[:, :], k.share[:, :]).then_inc(setup, 1)
                dve.wait_ge(setup, 3)

            def average_of(u, b):
                n = u * UNIT + b
                wait(dve, turned, n - UNIT + 1)
                dve.tensor_scalar(average[:, b, :], k.acc[:, ds(n * ACC, D)], k.share[:, ds(n, 1)], None,
                                  ALU.mult).then_inc(averaged, 1)

            dve.wait_ge(w_in, 48)

            def unit(u, h, i):
                if final:
                    dve.wait_ge(first_in[h], (i + 1) * 16)
                    if not (isinstance(i, int) and i == 0):
                        dve.wait_ge(stored[h], i * 32)
                for b in range(UNIT):
                    n = u * UNIT + b
                    s = (h * UNIT + b) % 2
                    if b < UNIT - 2:
                        average_of(u, b + 2)
                    elif not (isinstance(u, int) and u == UNITS - 1):
                        average_of(u + 1, b + 2 - UNIT)
                    dve.wait_ge(product, n + 1)
                    if final:
                        wait(dve, biased_ready, n)
                    dve.tensor_tensor(biased[:, s, :], pO[:, s, 0:D], bias[:, :], ALU.add).then_inc(biased_ready, 1)
                    if final:
                        dve.wait_ge(biased_ready, n + 1)
                        dve.tensor_tensor(result[:, h, b, :], biased[:, s, :], first[:, h, b, :],
                                          ALU.add).then_inc(tick, 1)
                    if final and not (isinstance(u, int) and u == 0):
                        normalise(u - 1, 1 - h, b)

            def normalise(u, h, part):
                if part == 0:
                    dve.wait_ge(tick, (u + 1) * UNIT)
                    for b in range(UNIT):
                        last = dve.bn_stats(stats[:, b, :], result[:, h, b, :])
                    last.then_inc(stats_ready, 1)
                elif part == 1:
                    dve.wait_ge(stats_ready, u + 1)
                    dve.nop().then_inc(k.apart, 1)
                    for b in range(UNIT):
                        last = dve.bn_aggr(mean[:, b, :], stats[:, b, :])
                    last.then_inc(var_ready, 1)
                elif part == 3:
                    dve.wait_ge(root_ready, u + 1)
                    dve.reciprocal(spread[:, :], spread[:, :]).then_inc(inverted, 1)
                elif part == 4:
                    dve.wait_ge(inverted, u + 1)
                    for b in range(UNIT):
                        last = dve.tensor_scalar(result[:, h, b, :], result[:, h, b, :], mean[:, b, 0:1],
                                                 spread[:, b:b + 1], ALU.subtract, ALU.mult)
                    last.then_inc(unit_done, 1)

            average_of(0, 0)
            average_of(0, 1)
            unit_turns(dve, unit)
            if final:
                for part in range(UNIT):
                    normalise(UNITS - 1, 1, part)


def build(nc, x, src, dst, Ww, Wb, a, Wl1, b1, Wr1, Wl2, b2, Wr2, out, debug=()):
    with ExitStack() as ctx:
        k = Kernel()

        def sb(name, shape, dt):
            return ctx.enter_context(nc.sbuf_tensor(name, shape, dt))

        def dram(name, shape, dt):
            kind = "ExternalOutput" if name in debug else "Internal"
            return nc.dram_tensor(name, shape, dt, kind=kind).ap()

        k.sb = sb
        k.pads_in = [ctx.enter_context(nc.semaphore(f"pads_in{q}")) for q in range(LISTS)]
        k.apart = ctx.enter_context(nc.semaphore("apart"))
        k.gathered = [ctx.enter_context(nc.semaphore(f"gathered{r}")) for r in range(RING)]
        k.turns_before = 0
        k.edges = [dram(f"edges{q}", (P, CHUNKS[q]), I32) for q in range(LISTS)]
        k.in_order = dram("in_order", ((E // P + 2) * P,), I32)
        k.table = dram("table", (NB * P, ROWT), F32)
        k.x1 = dram("x1", (NB * P, D), F32)
        k.hidden = dram("hidden", (NB * P, D), F32)
        k.carry = sb("carry", [P, GROUPS[0], HEADS, PAIRS + 1], BF16)
        k.fresh = sb("fresh", [P, CHUNKS[0] // PAIR], F32)
        k.s_all = sb("s_all", [P, NB, HEADS], F32)
        k.t_low = sb("t_low", [P, HEADS], F32)
        constants(nc, k, ctx)
        sort_edges(nc, k, src, dst)
        project(nc, k, x, Ww, Wb, a)
        k.acc = sb("acc", [P, NB * ACC], F32)
        k.share = sb("share", [P, NB], F32)
        k.row = sb("row", [P, MOST], I32)
        k.spot = sb("spot", [P, MOST], F32)
        load_list(nc, k, 0)
        with ExitStack() as c:
            k.rows = c.enter_context(nc.sbuf_tensor("rows", [P, GROUP * RING, ROWT], F32))
            k.wanted = c.enter_context(nc.sbuf_tensor("wanted", [P, GROUP * RING], I32))
            gat_pass(nc, k)
            k.turns_before += TURNS[0]
        gat_end(nc, k, x)
        load_list(nc, k, 1)
        for n, (table, Wl, bl, Wr, to) in enumerate(((k.x1, Wl1, b1, Wr1, k.hidden), (k.hidden, Wl2, b2, Wr2, out))):
            with ExitStack() as c:
                k.rows = c.enter_context(nc.sbuf_tensor(f"rows_s{n}", [P, GROUP * RING, D + 1], F32))
                k.wanted = c.enter_context(nc.sbuf_tensor(f"wanted_s{n}", [P, GROUP * RING], I32))
                sage_pass(nc, k, table, n == 0)
                k.turns_before += TURNS[1]
            sage_end(nc, k, table, Wl, bl, Wr, to, n == 1)


_INS = ["x", "src", "dst", "L0_gnn_W_w", "L0_gnn_W_b", "L0_gnn_a", "L1_gnn_W_l1", "L1_gnn_b1", "L1_gnn_W_r1",
        "L1_gnn_W_l2", "L1_gnn_b2", "L1_gnn_W_r2"]


def kernel(**inputs):
    import concourse.bacc as bacc
    import numpy as np
    from concourse.bass_utils import run_bass_kernel_spmd as run

    nc = bacc.Bacc("TRN2", target_bir_lowering=False, num_devices=1)
    arrays, args = {}, []
    for name in _INS:
        array = np.ascontiguousarray(inputs[name])
        arrays[f"in_{name}"] = array
        args.append(nc.dram_tensor(f"in_{name}", array.shape, mybir.dt.from_np(array.dtype),
                                   kind="ExternalInput").ap())
    out = nc.dram_tensor("out", (N, D), F32, kind="ExternalOutput").ap()
    build(nc, *args, out)
    got = run(nc, [arrays], core_ids=[0])
    return got.results[0]["out"]
```
